# Optimizing a Trainium2 kernel written in Bass

```python
import numpy as np
import jax
import jax.numpy as jnp

def _softmax(x, axis=-1):
    return jax.nn.softmax(x, axis=axis)

def _gelu(x):
    return jax.nn.gelu(x, approximate=True)

def _silu(x):
    return jax.nn.silu(x)

def _sigmoid(x):
    return jax.nn.sigmoid(x)

def _layernorm(x, axis=-1, eps=1e-05):
    m = jnp.mean(x, axis=axis, keepdims=True)
    v = jnp.var(x, axis=axis, keepdims=True)
    return (x - m) / jnp.sqrt(v + eps)

def _scatter_add(tgt, idx, src, axis=0):
    return tgt.at[idx].add(src)

def _segment_sum(src, seg, n):
    return jax.ops.segment_sum(src, seg, n)
kernel_name = 'mk_early_fusion_embed_d2_tok_img1024_r4_2883b9'

def setup_inputs(seed: int=0):
    np.random.seed(seed)
    _w = jnp.asarray

    def _rec_inputs():
        import jax
        import jax.numpy as jnp
        _rk = jax.random.key(seed)
        x = -0.00016672 + 0.999947 * jax.random.normal(jax.random.fold_in(_rk, 1), (32, 96, 96, 3), jnp.float32)
        x_txt = jax.random.randint(jax.random.fold_in(_rk, 51), (32, 32), 0, 250, jnp.int32)
        return (x, x_txt)
    x, x_txt = _rec_inputs()

    def _L0_tok_setup():
        import jax, jax.numpy as jnp
        import numpy as np
        P = 16
        E = 256

        def patchify(images, patch_size):
            B, H, W, C = images.shape
            hp, wp = (H // patch_size, W // patch_size)
            x = images.reshape(B, hp, patch_size, wp, patch_size, C)
            x = x.transpose(0, 1, 3, 2, 4, 5)
            return x.reshape(B, hp * wp, patch_size * patch_size * C)
        key = jax.random.key(seed)
        k_img, k_w, k_b, k_pos = jax.random.split(key, 4)
        B, H, W, C = (64, 96, 96, 3)
        patch_dim = P * P * C
        patch_count = H // P * (W // P)
        images = jax.random.normal(k_img, (B, H, W, C), dtype=jnp.float32)
        W_proj = jax.random.normal(k_w, (E, patch_dim), dtype=jnp.float32) * patch_dim ** (-0.5)
        b_proj = jax.random.normal(k_b, (E,), dtype=jnp.float32) * 0.02
        pos_emb = jax.random.normal(k_pos, (patch_count, E), dtype=jnp.float32) * 0.02
        return {'images': images, 'W_proj': W_proj, 'b_proj': b_proj, 'pos_emb': pos_emb}
    _L0_tok_all = _L0_tok_setup()
    _L0_tok_in = {k: v for k, v in _L0_tok_all.items() if k in ('W_proj', 'b_proj', 'pos_emb')}
    del _L0_tok_all

    def _L0_txt_setup():
        import math
        import jax, jax.numpy as jnp
        import numpy as np
        PAD_IDX = 1
        SEP_ID = 4
        STARTPOS = 1025
        BSZ, SEQ_LEN, EMBED_DIM = (32, 1024, 256)

        def _build_table(num_cons, dim, padding_idx, startpos):
            half = dim // 2
            freqs = jnp.exp(jnp.arange(half, dtype=jnp.float32) * -(math.log(10000.0) / (half - 1)))
            ang = jnp.arange(startpos, startpos + num_cons, dtype=jnp.float32)[:, None] * freqs[None, :]
            tab = jnp.concatenate([jnp.sin(ang), jnp.cos(ang)], axis=1)
            return tab.at[padding_idx].set(0.0)

        def _positions(tokens):
            L = tokens.shape[1]
            valid = jnp.cumprod((tokens != PAD_IDX).astype(jnp.int32), axis=1).astype(bool)
            j = jnp.arange(L, dtype=jnp.int32)
            sep_j = jnp.where(tokens == SEP_ID, j, 0)
            last_sep = jax.lax.associative_scan(jnp.maximum, sep_j, axis=1)
            pos = j - last_sep + 2
            return jnp.where(valid, pos, 1)
        key = jax.random.key(seed)
        tokens = jax.random.randint(key, (BSZ, SEQ_LEN), 0, 250, dtype=jnp.int64)
        num_cons = PAD_IDX + 1 + SEQ_LEN
        weights = _build_table(num_cons, EMBED_DIM, PAD_IDX, STARTPOS)
        return {'input': tokens, 'weights': weights}
    _L0_txt_all = _L0_txt_setup()
    _L0_txt_in = {k: v for k, v in _L0_txt_all.items() if k in ('weights',)}
    del _L0_txt_all

    def _L0_attn_setup():
        import jax, jax.numpy as jnp
        import numpy as np
        import math
        B, S, E, H = (2, 512, 256, 8)
        Dh = E // H

        def _pos_encoding(s, e):
            pos = jnp.arange(s, dtype=jnp.float32)[:, None]
            div = jnp.exp(jnp.arange(0, e, 2, dtype=jnp.float32) * (-math.log(10000.0) / e))
            pe = jnp.zeros((s, e), jnp.float32)
            pe = pe.at[:, 0::2].set(jnp.sin(pos * div))
            pe = pe.at[:, 1::2].set(jnp.cos(pos * div))
            return pe

        def _rel_shift(ps):
            b, h, s1, s2 = ps.shape
            padded = jnp.pad(ps, ((0, 0), (0, 0), (0, 0), (1, 0)))
            return padded.reshape(b, h, s2 + 1, s1)[:, :, 1:, :].reshape(b, h, s1, s2)

        def _forward(inputs, ln_gamma, ln_beta, Wq, bq, Wk, bk, Wv, bv, Wp, u_bias, v_bias, Wo, bo):
            b, s, e = inputs.shape
            mu = inputs.mean(-1, keepdims=True)
            var = inputs.var(-1, keepdims=True)
            xn = (inputs - mu) / jnp.sqrt(var + 1e-05) * ln_gamma + ln_beta
            xh = xn.reshape(b, s, H, Dh)
            q = xh @ Wq + bq
            k = xh @ Wk + bk
            v = xh @ Wv + bv
            pe = _pos_encoding(s, e).reshape(s, H, Dh)
            p = pe @ Wp
            content = jnp.einsum('bqhd,bkhd->bhqk', q + u_bias, k)
            pos_score = jnp.einsum('bqhd,khd->bhqk', q + v_bias, p)
            pos_score = _rel_shift(pos_score)
            score = (content + pos_score) / jnp.sqrt(jnp.float32(e))
            attn = jax.nn.softmax(score, axis=-1)
            ctx = jnp.einsum('bhqk,bkhd->bqhd', attn, v).reshape(b, s, e)
            return ctx @ Wo + bo
        key = jax.random.key(seed)
        ks = jax.random.split(key, 9)
        g = lambda k, shp: jax.random.normal(k, shp, jnp.float32) * 0.02
        return {'inputs': jax.random.normal(ks[0], (B, S, E), jnp.float32), 'ln_gamma': jnp.ones((E,), jnp.float32), 'ln_beta': jnp.zeros((E,), jnp.float32), 'Wq': g(ks[1], (Dh, Dh)), 'bq': jnp.zeros((Dh,), jnp.float32), 'Wk': g(ks[2], (Dh, Dh)), 'bk': jnp.zeros((Dh,), jnp.float32), 'Wv': g(ks[3], (Dh, Dh)), 'bv': jnp.zeros((Dh,), jnp.float32), 'Wp': g(ks[4], (Dh, Dh)), 'u_bias': g(ks[5], (H, Dh)), 'v_bias': g(ks[6], (H, Dh)), 'Wo': g(ks[7], (E, E)), 'bo': jnp.zeros((E,), jnp.float32)}
    _L0_attn_all = _L0_attn_setup()
    _L0_attn_in = {k: v for k, v in _L0_attn_all.items() if k in ('ln_gamma', 'ln_beta', 'Wq', 'bq', 'Wk', 'bk', 'Wv', 'bv', 'Wp', 'u_bias', 'v_bias', 'Wo', 'bo')}
    del _L0_attn_all

    def _L0_ffn_setup():
        import jax, jax.numpy as jnp
        import numpy as np
        B, S, D_MODEL, D_HIDDEN = (4, 512, 256, 1024)

        def act_quant(x):
            scale = 127.0 / jnp.clip(jnp.max(jnp.abs(x), axis=-1, keepdims=True), 1e-05)
            return jnp.clip(jnp.round(x * scale), -128, 127) / scale

        def weight_quant(w):
            scale = 1.0 / jnp.clip(jnp.mean(jnp.abs(w)), 1e-05)
            return jnp.clip(jnp.round(w * scale), -1, 1) / scale

        def bit_linear(x, w):
            xq = x + jax.lax.stop_gradient(act_quant(x) - x)
            wq = w + jax.lax.stop_gradient(weight_quant(w) - w)
            return jnp.einsum('bsd,hd->bsh', xq, wq)

        def depthwise_conv1d(x_bcl, w, b):
            y = jax.lax.conv_general_dilated(x_bcl, w, window_strides=(1,), padding=[(1, 1)], dimension_numbers=('NCH', 'OIH', 'NCH'), feature_group_count=x_bcl.shape[1])
            return y + b[None, :, None]
        key = jax.random.key(seed)
        ks = jax.random.split(key, 5)
        lim1 = 1.0 / np.sqrt(D_MODEL)
        lim2 = 1.0 / np.sqrt(D_HIDDEN)
        limc = 1.0 / np.sqrt(3.0)
        return {'x': jax.random.normal(ks[0], (B, S, D_MODEL), dtype=jnp.float32), 'w1': jax.random.uniform(ks[1], (D_HIDDEN, D_MODEL), jnp.float32, -lim1, lim1), 'conv_w': jax.random.uniform(ks[2], (D_HIDDEN, 1, 3), jnp.float32, -limc, limc), 'conv_b': jax.random.uniform(ks[3], (D_HIDDEN,), jnp.float32, -limc, limc), 'w2': jax.random.uniform(ks[4], (D_MODEL, D_HIDDEN), jnp.float32, -lim2, lim2)}
    _L0_ffn_all = _L0_ffn_setup()
    _L0_ffn_in = {k: v for k, v in _L0_ffn_all.items() if k in ('w1', 'conv_w', 'conv_b', 'w2')}
    del _L0_ffn_all

    def _L1_attn_setup():
        import jax, jax.numpy as jnp
        import numpy as np
        N_HEAD = 16
        key = jax.random.key(seed)
        k1, k2, k3, k4, k5 = jax.random.split(key, 5)
        B, T, C = (8, 512, 256)
        hs = C // N_HEAD
        return {'ids': jax.random.normal(k1, (B, T, C), dtype=jnp.float32), 'qkv_w': jax.random.normal(k2, (3 * hs, C), dtype=jnp.float32) * C ** (-0.5), 'qkv_b': jax.random.normal(k3, (3 * hs,), dtype=jnp.float32) * 0.02, 'proj_w': jax.random.normal(k4, (C, C), dtype=jnp.float32) * C ** (-0.5), 'proj_b': jax.random.normal(k5, (C,), dtype=jnp.float32) * 0.02}
    _L1_attn_all = _L1_attn_setup()
    _L1_attn_in = {k: v for k, v in _L1_attn_all.items() if k in ('qkv_w', 'qkv_b', 'proj_w', 'proj_b')}
    del _L1_attn_all

    def _L1_ffn_setup():
        import jax, jax.numpy as jnp
        import numpy as np
        D_MODEL, D_FF, N_EXP = (256, 1024, 8)
        key = jax.random.key(seed)
        ks = jax.random.split(key, 8)
        s = lambda fan_in: 1.0 / np.sqrt(fan_in)
        x = jax.random.normal(ks[0], (4, 512, D_MODEL), dtype=jnp.float32)
        Wr = jax.random.uniform(ks[1], (N_EXP, D_MODEL), jnp.float32, -s(D_MODEL), s(D_MODEL))
        br = jax.random.uniform(ks[2], (N_EXP,), jnp.float32, -s(D_MODEL), s(D_MODEL))
        W1 = jax.random.uniform(ks[3], (N_EXP, D_FF, D_MODEL), jnp.float32, -s(D_MODEL), s(D_MODEL))
        b1 = jax.random.uniform(ks[4], (N_EXP, D_FF), jnp.float32, -s(D_MODEL), s(D_MODEL))
        W2 = jax.random.uniform(ks[5], (N_EXP, D_MODEL, D_FF), jnp.float32, -s(D_FF), s(D_FF))
        b2 = jax.random.uniform(ks[6], (N_EXP, D_MODEL), jnp.float32, -s(D_FF), s(D_FF))
        return {'x': x, 'Wr': Wr, 'br': br, 'W1': W1, 'b1': b1, 'W2': W2, 'b2': b2}
    _L1_ffn_all = _L1_ffn_setup()
    _L1_ffn_in = {k: v for k, v in _L1_ffn_all.items() if k in ('Wr', 'br', 'W1', 'b1', 'W2', 'b2')}
    del _L1_ffn_all
    return {'x': x, 'x_txt': x_txt, 'L0_tok_W_proj': _L0_tok_in['W_proj'], 'L0_tok_b_proj': _L0_tok_in['b_proj'], 'L0_tok_pos_emb': _L0_tok_in['pos_emb'], 'L0_txt_weights': _L0_txt_in['weights'], 'L0_attn_ln_gamma': _L0_attn_in['ln_gamma'], 'L0_attn_ln_beta': _L0_attn_in['ln_beta'], 'L0_attn_Wq': _L0_attn_in['Wq'], 'L0_attn_bq': _L0_attn_in['bq'], 'L0_attn_Wk': _L0_attn_in['Wk'], 'L0_attn_bk': _L0_attn_in['bk'], 'L0_attn_Wv': _L0_attn_in['Wv'], 'L0_attn_bv': _L0_attn_in['bv'], 'L0_attn_Wp': _L0_attn_in['Wp'], 'L0_attn_u_bias': _L0_attn_in['u_bias'], 'L0_attn_v_bias': _L0_attn_in['v_bias'], 'L0_attn_Wo': _L0_attn_in['Wo'], 'L0_attn_bo': _L0_attn_in['bo'], 'L0_ffn_w1': _L0_ffn_in['w1'], 'L0_ffn_conv_w': _L0_ffn_in['conv_w'], 'L0_ffn_conv_b': _L0_ffn_in['conv_b'], 'L0_ffn_w2': _L0_ffn_in['w2'], 'L1_attn_qkv_w': _L1_attn_in['qkv_w'], 'L1_attn_qkv_b': _L1_attn_in['qkv_b'], 'L1_attn_proj_w': _L1_attn_in['proj_w'], 'L1_attn_proj_b': _L1_attn_in['proj_b'], 'L1_ffn_Wr': _L1_ffn_in['Wr'], 'L1_ffn_br': _L1_ffn_in['br'], 'L1_ffn_W1': _L1_ffn_in['W1'], 'L1_ffn_b1': _L1_ffn_in['b1'], 'L1_ffn_W2': _L1_ffn_in['W2'], 'L1_ffn_b2': _L1_ffn_in['b2']}

def reference(x, x_txt, L0_tok_W_proj, L0_tok_b_proj, L0_tok_pos_emb, L0_txt_weights, L0_attn_ln_gamma, L0_attn_ln_beta, L0_attn_Wq, L0_attn_bq, L0_attn_Wk, L0_attn_bk, L0_attn_Wv, L0_attn_bv, L0_attn_Wp, L0_attn_u_bias, L0_attn_v_bias, L0_attn_Wo, L0_attn_bo, L0_ffn_w1, L0_ffn_conv_w, L0_ffn_conv_b, L0_ffn_w2, L1_attn_qkv_w, L1_attn_qkv_b, L1_attn_proj_w, L1_attn_proj_b, L1_ffn_Wr, L1_ffn_br, L1_ffn_W1, L1_ffn_b1, L1_ffn_W2, L1_ffn_b2):
    import jax
    import jax.numpy as jnp

    def _L0_tok_ref(images, W_proj, b_proj, pos_emb):
        import jax, jax.numpy as jnp
        import numpy as np
        P = 16
        E = 256

        def patchify(images, patch_size):
            B, H, W, C = images.shape
            hp, wp = (H // patch_size, W // patch_size)
            x = images.reshape(B, hp, patch_size, wp, patch_size, C)
            x = x.transpose(0, 1, 3, 2, 4, 5)
            return x.reshape(B, hp * wp, patch_size * patch_size * C)
        patches = patchify(images, P)
        out = jnp.einsum('bnd,ed->bne', patches, W_proj) + b_proj + pos_emb[None, :, :]
        return out

    def _L0_txt_ref(input, weights):
        import math
        import jax, jax.numpy as jnp
        import numpy as np
        PAD_IDX = 1
        SEP_ID = 4
        STARTPOS = 1025
        BSZ, SEQ_LEN, EMBED_DIM = (32, 1024, 256)

        def _build_table(num_cons, dim, padding_idx, startpos):
            half = dim // 2
            freqs = jnp.exp(jnp.arange(half, dtype=jnp.float32) * -(math.log(10000.0) / (half - 1)))
            ang = jnp.arange(startpos, startpos + num_cons, dtype=jnp.float32)[:, None] * freqs[None, :]
            tab = jnp.concatenate([jnp.sin(ang), jnp.cos(ang)], axis=1)
            return tab.at[padding_idx].set(0.0)

        def _positions(tokens):
            L = tokens.shape[1]
            valid = jnp.cumprod((tokens != PAD_IDX).astype(jnp.int32), axis=1).astype(bool)
            j = jnp.arange(L, dtype=jnp.int32)
            sep_j = jnp.where(tokens == SEP_ID, j, 0)
            last_sep = jax.lax.associative_scan(jnp.maximum, sep_j, axis=1)
            pos = j - last_sep + 2
            return jnp.where(valid, pos, 1)
        pos = _positions(input)
        return jnp.take(weights, pos, axis=0)

    def _L0_attn_ref(inputs, ln_gamma, ln_beta, Wq, bq, Wk, bk, Wv, bv, Wp, u_bias, v_bias, Wo, bo):
        import jax, jax.numpy as jnp
        import numpy as np
        import math
        B, S, E, H = (2, 512, 256, 8)
        Dh = E // H

        def _pos_encoding(s, e):
            pos = jnp.arange(s, dtype=jnp.float32)[:, None]
            div = jnp.exp(jnp.arange(0, e, 2, dtype=jnp.float32) * (-math.log(10000.0) / e))
            pe = jnp.zeros((s, e), jnp.float32)
            pe = pe.at[:, 0::2].set(jnp.sin(pos * div))
            pe = pe.at[:, 1::2].set(jnp.cos(pos * div))
            return pe

        def _rel_shift(ps):
            b, h, s1, s2 = ps.shape
            padded = jnp.pad(ps, ((0, 0), (0, 0), (0, 0), (1, 0)))
            return padded.reshape(b, h, s2 + 1, s1)[:, :, 1:, :].reshape(b, h, s1, s2)

        def _forward(inputs, ln_gamma, ln_beta, Wq, bq, Wk, bk, Wv, bv, Wp, u_bias, v_bias, Wo, bo):
            b, s, e = inputs.shape
            mu = inputs.mean(-1, keepdims=True)
            var = inputs.var(-1, keepdims=True)
            xn = (inputs - mu) / jnp.sqrt(var + 1e-05) * ln_gamma + ln_beta
            xh = xn.reshape(b, s, H, Dh)
            q = xh @ Wq + bq
            k = xh @ Wk + bk
            v = xh @ Wv + bv
            pe = _pos_encoding(s, e).reshape(s, H, Dh)
            p = pe @ Wp
            content = jnp.einsum('bqhd,bkhd->bhqk', q + u_bias, k)
            pos_score = jnp.einsum('bqhd,khd->bhqk', q + v_bias, p)
            pos_score = _rel_shift(pos_score)
            score = (content + pos_score) / jnp.sqrt(jnp.float32(e))
            attn = jax.nn.softmax(score, axis=-1)
            ctx = jnp.einsum('bhqk,bkhd->bqhd', attn, v).reshape(b, s, e)
            return ctx @ Wo + bo
        return _forward(inputs, ln_gamma, ln_beta, Wq, bq, Wk, bk, Wv, bv, Wp, u_bias, v_bias, Wo, bo)

    def _L0_ffn_ref(x, w1, conv_w, conv_b, w2):
        import jax, jax.numpy as jnp
        import numpy as np
        B, S, D_MODEL, D_HIDDEN = (4, 512, 256, 1024)

        def act_quant(x):
            scale = 127.0 / jnp.clip(jnp.max(jnp.abs(x), axis=-1, keepdims=True), 1e-05)
            return jnp.clip(jnp.round(x * scale), -128, 127) / scale

        def weight_quant(w):
            scale = 1.0 / jnp.clip(jnp.mean(jnp.abs(w)), 1e-05)
            return jnp.clip(jnp.round(w * scale), -1, 1) / scale

        def bit_linear(x, w):
            xq = x + jax.lax.stop_gradient(act_quant(x) - x)
            wq = w + jax.lax.stop_gradient(weight_quant(w) - w)
            return jnp.einsum('bsd,hd->bsh', xq, wq)

        def depthwise_conv1d(x_bcl, w, b):
            y = jax.lax.conv_general_dilated(x_bcl, w, window_strides=(1,), padding=[(1, 1)], dimension_numbers=('NCH', 'OIH', 'NCH'), feature_group_count=x_bcl.shape[1])
            return y + b[None, :, None]
        h = bit_linear(x, w1)
        h = depthwise_conv1d(h.transpose(0, 2, 1), conv_w, conv_b)
        h = h.transpose(0, 2, 1)
        h = jax.nn.silu(h)
        return bit_linear(h, w2)

    def _L1_attn_ref(ids, qkv_w, qkv_b, proj_w, proj_b):
        import jax, jax.numpy as jnp
        import numpy as np
        N_HEAD = 16
        B, T, C = ids.shape
        hs = qkv_w.shape[0] // 3
        qkv = ids @ qkv_w.T + qkv_b
        q, k, v = jnp.split(qkv, 3, axis=-1)
        wei = jnp.einsum('btd,bsd->bts', q, k)
        tril = jnp.tril(jnp.ones((T, T), dtype=bool))
        wei = jnp.where(tril, wei, jnp.float32(0.0))
        out_h = jnp.einsum('bts,bsd->btd', wei, v)
        out = jnp.tile(out_h, (1, 1, N_HEAD))
        return out @ proj_w.T + proj_b

    def _L1_ffn_ref(x, Wr, br, W1, b1, W2, b2):
        import jax, jax.numpy as jnp
        import numpy as np
        D_MODEL, D_FF, N_EXP = (256, 1024, 8)
        B, S, D = x.shape
        xf = x.reshape(-1, D)
        logits = xf @ Wr.T + br
        expert_idx = jnp.argmax(logits, axis=-1)
        h = jax.nn.relu(jnp.einsum('td,efd->etf', xf, W1) + b1[:, None, :])
        y = jnp.einsum('etf,edf->etd', h, W2) + b2[:, None, :]
        out = y[expert_idx, jnp.arange(xf.shape[0])]
        return out.reshape(B, S, D)
    h = _L0_tok_ref(x, L0_tok_W_proj, L0_tok_b_proj, L0_tok_pos_emb)
    h = jnp.concatenate([h, _L0_txt_ref(x_txt, L0_txt_weights)], axis=1)
    h = h + _L0_attn_ref(_layernorm(h, axis=-1), L0_attn_ln_gamma, L0_attn_ln_beta, L0_attn_Wq, L0_attn_bq, L0_attn_Wk, L0_attn_bk, L0_attn_Wv, L0_attn_bv, L0_attn_Wp, L0_attn_u_bias, L0_attn_v_bias, L0_attn_Wo, L0_attn_bo)
    h = h + _L0_ffn_ref(_layernorm(h, axis=-1), L0_ffn_w1, L0_ffn_conv_w, L0_ffn_conv_b, L0_ffn_w2)
    h = h + _L1_attn_ref(_layernorm(h, axis=-1), L1_attn_qkv_w, L1_attn_qkv_b, L1_attn_proj_w, L1_attn_proj_b)
    h = h + _L1_ffn_ref(_layernorm(h, axis=-1), L1_ffn_Wr, L1_ffn_br, L1_ffn_W1, L1_ffn_b1, L1_ffn_W2, L1_ffn_b2)
    return h

_drawn_inputs = setup_inputs


def setup_inputs(seed=0):
    import zlib

    import numpy as np

    out = dict(_drawn_inputs(seed))
    spreads = {'L0_attn_ln_gamma': (1.0, 0.6),
     'L0_attn_ln_beta': (0.0, 0.411),
     'L0_attn_bq': (0.0, 0.8),
     'L0_attn_bk': (0.0, 2.0),
     'L0_attn_bv': (0.0, 0.1),
     'L0_attn_bo': (0.0, 0.1)}
    factors = {'L0_tok_pos_emb': 2.812,
     'L0_attn_Wq': 8.0,
     'L0_attn_Wk': 8.0,
     'L0_attn_Wp': 8.0,
     'L0_attn_u_bias': 8.0,
     'L0_attn_v_bias': 36.324,
     'L1_attn_proj_b': 8.0,
     'L1_ffn_Wr': 8.0,
     'L1_ffn_br': 8.0,
     'L1_ffn_W1': 8.0,
     'L1_ffn_b1': 8.0,
     'L1_ffn_W2': 7.416,
     'L1_ffn_b2': 64.0}
    for name, (base, spread) in spreads.items():
        noise = np.random.default_rng([zlib.crc32(name.encode()), seed]).standard_normal(out[name].shape)
        drawn = base * np.exp(spread * noise) if base else spread * noise
        out[name] = jnp.asarray(drawn.astype(out[name].dtype))
    for name, factor in factors.items():
        out[name] = (out[name] * factor).astype(out[name].dtype)
    return out
```

```python
import numpy as np
import concourse.bass as bass
from concourse import mybir
from contextlib import ExitStack

F32 = mybir.dt.float32
BF16 = mybir.dt.bfloat16
I32 = mybir.dt.int32
U32 = mybir.dt.uint32
ALU = mybir.AluOpType
ACT = mybir.ActivationFunctionType
AX = mybir.AxisListType
RED = bass.bass_isa.ReduceOp

P = 128
B, S_IMG, S_TXT = 32, 36, 32
S = S_IMG + S_TXT
NTOK = B * S
D = 256
C = D // P
TILES = NTOK // P
PAIRS = TILES // 2
LN_STEPS = PAIRS + 1
PATCH = 768
KP = PATCH // P
EG = 4
EGN = B // EG * S_IMG
NTXT = B * S_TXT
TAB = S_TXT + 2
H, DH = 8, 32
HC = H // C
SP1 = S + 1
FF = 1024
FJ = FF // P
GB = 4
GN = GB * S
GROUPS = B // GB
HS = 16
NREP = 16
E = 8
MAX_TILES = (NTOK + E * (P - 1)) // P
EPS = 1e-5
MAGIC = 1.5 * 2.0 ** 23
PSUM_W = 512
WE = C * FF + FJ * D
W_EARLY = 5


def wait(e, sem, v):
    if isinstance(v, int) and v <= 0:
        return
    e.wait_ge(sem, v)


def program(nc, a, out):
    ctx = ExitStack()
    with ctx:
        def sb(name, shape, dt=F32):
            return ctx.enter_context(nc.sbuf_tensor(name, shape, dt))

        def sem(name):
            return ctx.enter_context(nc.semaphore(name))

        moe_w = sb("moe_w", [P, E * WE])
        hT_t = sb("hT", [P, C * NTOK])
        yT_t = sb("yT", [P, C * NTOK])
        tm_t = sb("tm", [P, TILES * D])
        hT = hT_t[:, :].rearrange("p (c n) -> p c n", c=C)
        yT = yT_t[:, :].rearrange("p (c n) -> p c n", c=C)
        tm = tm_t[:, :].rearrange("p (t d) -> p t d", t=TILES)

        class Region:

            def __init__(self, tensor, at, end):
                self.tensor, self.at, self.end = tensor, at, end

            def take(self, shape, dt=F32, parts=P):
                n = int(np.prod(shape))
                words = n // 2 if dt == BF16 else n
                v = self.tensor[0:parts, self.at:self.at + words]
                self.at += words
                assert self.at <= self.end, (self.at, self.end)
                if dt != F32:
                    v = v.bitcast(dt)
                if len(shape) == 2:
                    v = v.rearrange("p (a b) -> p a b", a=shape[0])
                if len(shape) == 3:
                    v = v.rearrange("p (a b c) -> p a b c", a=shape[0], b=shape[1])
                return v

        def last_experts():
            return Region(moe_w, (E - 2) * WE, E * WE)

        ident = sb("ident", [P, P])
        identb = sb("identb", [P, P], BF16)
        onesf = sb("onesf", [P, P])
        neg_half = sb("neg_half", [P, TILES])
        pid = sb("pid", [P, 1])
        gamma = sb("gamma", [P, C])
        beta = sb("beta", [P, C])
        bqu = sb("bqu", [P, C])
        bqv = sb("bqv", [P, C])
        bk0 = sb("bk0", [P, 1])
        bv0 = sb("bv0", [P, 1])
        bo0 = sb("bo0", [P, C])
        hmask = sb("hmask", [P, HC])
        bproj = sb("bproj", [P, C])
        wq_bd = sb("wq_bd", [P, P])
        wk_bd = sb("wk_bd", [P, P])
        wv_bd = sb("wv_bd", [P, P])
        wo = sb("wo", [P, C * D])
        wi = sb("wi", [P, (C * FF + FJ * D) // 2])
        w1i = wi[:, 0:C * FF // 2].bitcast(BF16)
        w2i = wi[:, C * FF // 2:].bitcast(BF16)
        convw = sb("convw", [P, FJ * 3])
        convb = sb("convb", [P, FJ])
        w1m = sb("w1m", [P, 2])
        wsum = sb("wsum", [P, 4])

        r = last_experts()
        patches = r.take([EG, KP, EGN])
        r = Region(tm_t, 0, TILES * D)
        wproj = r.take([KP, D])
        tab = r.take([D], parts=TAB)
        posb = r.take([C, S_IMG])
        sepv = r.take([NTXT], parts=TAB)
        padv = r.take([NTXT], parts=TAB)
        r = Region(yT_t, 0, C * NTOK)
        tok_i = r.take([NTXT], I32, TAB)
        tokf = r.take([NTXT], parts=TAB)
        gidx = r.take([NTXT], parts=TAB)
        base = r.take([NTXT], parts=TAB)
        r = Region(moe_w, W_EARLY * WE, (W_EARLY + 1) * WE)
        w1raw = r.take([C * FF])
        w2raw = r.take([FJ * D])
        runs = moe_w[0:TAB, (E - 2) * WE + EG * KP * EGN:E * WE][:, 0:NTXT]
        runp = wi[0:TAB, 0:NTXT]

        stage = [sb(f"stage{i}", [P, 2 * D]) for i in range(2)]
        z = [sb(f"z{i}", [P, 2 * D]) for i in range(2)]
        zb = [z[i][:, 0:D].bitcast(BF16) for i in range(2)]
        bn = sb("bn", [P, TILES * 6])
        bnv = bn[:, :].rearrange("p (t k) -> p t k", k=6)
        bsum_t = sb("bsum", [P, 4 * TILES])
        bsum = bsum_t[:, :].rearrange("p (k t) -> p k t", k=4)
        mean = sb("mean", [P, TILES])
        var = sb("var", [P, TILES])
        ve = sb("ve", [P, TILES])
        rstd = sb("rstd", [P, TILES])
        amax = sb("amax", [P, TILES])
        qstep = sb("qstep", [P, TILES])
        qinv = sb("qinv", [P, TILES])

        r = last_experts()
        pbd = r.take([C, HC * SP1])
        kbd = [r.take([C, HC * S]) for _ in range(2)]
        qu = [r.take([C, S]) for _ in range(2)]
        qv = r.take([C, S])
        yst = [r.take([C, S]) for _ in range(2)]
        posp = [r.take([C, HC * SP1], parts=S) for _ in range(2)]
        poss = [r.take([C, HC * S], parts=S) for _ in range(2)]
        sx = [r.take([H, S], parts=S) for _ in range(2)]
        pr = [r.take([H, S], parts=S) for _ in range(2)]
        prT = r.take([H, S], parts=S)
        ctxn = r.take([H, DH], parts=S)
        ctxT = r.take([C, S])
        vaug = [r.take([H, DH + 1], parts=S) for _ in range(2)]
        rz = r.take([H], parts=S)
        mx = [r.take([H], parts=S) for _ in range(2)]
        pe_bd = Region(yT_t, 0, C * NTOK).take([C, HC * SP1])
        wp_bd = z[0][:, 0:P]

        r = last_experts()
        sv = [r.take([FJ, GN]) for _ in range(2)]
        si = r.take([FJ, GN], BF16)
        uu = [r.take([GB, S + 2]) for _ in range(2)]
        tt = [r.take([GB, S]) for _ in range(2)]
        am = [r.take([GN]) for _ in range(2)]
        fo = stage[0]
        r = Region(tm_t, 0, TILES * D)
        mr = [r.take([GN]) for _ in range(2)]
        mi = [r.take([GN]) for _ in range(2)]
        fo = [r.take([C, GN]) for _ in range(2)]
        ziT = yT_t[:, 0:NTOK].bitcast(BF16).rearrange("p (c n) -> p c n", c=C)
        rsb = yT_t[:, NTOK:2 * NTOK]

        wqkv = sb("wqkv", [P, C * 3 * HS])
        wqkv_v = wqkv[:, :].rearrange("p (c n) -> p c n", c=C)
        bq1 = sb("bq1", [HS, 1])
        bk1 = sb("bk1", [HS, 1])
        bv1 = sb("bv1", [S, HS])
        pj = sb("pj", [HS, D])
        pjb = sb("pjb", [P, C])
        cmask = sb("cmask", [S, S])
        pj_raw = carve_pj = Region(moe_w, W_EARLY * WE, (W_EARLY + 1) * WE).take([D, NREP], parts=HS)
        r = Region(tm_t, 0, TILES * D)
        y7 = [r.take([C, GN]) for _ in range(2)]
        q7 = [r.take([GN], parts=HS) for _ in range(2)]
        k7 = [r.take([GN], parts=HS) for _ in range(2)]
        v7 = [r.take([GB, HS], parts=S) for _ in range(2)]
        w7 = [r.take([GB, S], parts=S) for _ in range(2)]
        o7 = [r.take([GN], parts=HS) for _ in range(2)]

        wr = sb("wr", [P, C * E])
        br = sb("br", [P, E])
        lg = sb("lg", [P, TILES * E])
        lgv = lg[:, :].rearrange("p (t e) -> p t e", e=E)
        z3 = hT_t[:, :].rearrange("p (t d) -> p t d", t=TILES)
        r = Region(yT_t, 0, C * NTOK)
        zTs = [r.take([C, 2 * P]) for _ in range(2)]
        oh = r.take([TILES, E])
        ohb = r.take([TILES, E], BF16)
        rt = r.take([TILES, E])
        rcol = r.take([TILES])
        rev = r.take([E])
        thr = r.take([E, TILES])
        cmp_ = r.take([E, TILES])
        cntp = r.take([E])
        cntb = r.take([E], BF16)
        nt = r.take([E])
        tend = r.take([E])
        tst = r.take([E])
        it24 = r.take([MAX_TILES, E])
        te = r.take([MAX_TILES])
        triu = r.take([P], BF16)
        onesb = r.take([P], BF16)
        posu = sb("posu", [P, TILES], U32)
        tei = sb("tei", [1, MAX_TILES], I32)
        zeros = Region(yT_t, 0, C * NTOK)
        b2 = wi
        b1 = sb("b1", [P, E * FJ])
        r = Region(yT_t, 0, C * NTOK)
        xt = [r.take([D]) for _ in range(2)]
        xT = [r.take([D]) for _ in range(2)]
        h1 = r.take([FF])
        hTm = r.take([FJ, P])
        ysb = [r.take([D]) for _ in range(2)]
        b1s = [r.take([FJ]) for _ in range(2)]
        GATH = 2
        fg = [r.take([D]) for _ in range(GATH)]

        ps = ctx.enter_context(nc.psum_tensor("ps", [P, 8, PSUM_W], F32))

        scr = [nc.dram_tensor(f"shift{i}", [H, S * SP1], F32, kind="Internal").ap() for i in range(2)]
        xs = nc.dram_tensor("sorted_rows", [MAX_TILES * P, D], F32, kind="Internal").ap()
        ys = nc.dram_tensor("sorted_out", [MAX_TILES * P, D], F32, kind="Internal").ap()

        (pool_past, sync_past, ld_emb, ld_txt, ld_ln, ld_at, ld_w12, ld_ff, ld_a1, ld_pj, ld_rt, ld_b2, ld_pe, ld_moe, ld_moe5, ld_moe67,
         consts, iotas, txt_step, posb_ok, emb_mm, emb_out, txt_mm, txt_out,
         ln_staged, ln_tokps, ln_tok, ln_bn, ln_ba, ln_mv, ln_ve, ln_rstd, ln_z, ln_zT, ln_out,
         q_z, q_amax, q_step, q_inv, q_mul, q_diag, q_bps, q_rsb,
         wq_abs, wq_sum, wq_mean, wq_inv, wq_a, wq_b, wq_done, pj_done) = [sem(n) for n in (
             "pool_past sync_past ld_emb ld_txt ld_ln ld_at ld_w12 ld_ff ld_a1 ld_pj ld_rt ld_b2 ld_pe ld_moe ld_moe5 ld_moe67 "
             "consts iotas txt_step posb_ok emb_mm emb_out txt_mm txt_out "
             "ln_staged ln_tokps ln_tok ln_bn ln_ba ln_mv ln_ve ln_rstd ln_z ln_zT ln_out "
             "q_z q_amax q_step q_inv q_mul q_diag q_bps q_rsb "
             "wq_abs wq_sum wq_mean wq_inv wq_a wq_b wq_done pj_done").split()]
        (at_bias, at_pbps, at_pbd, at_y, at_qkps, at_qkv, at_vps, at_v, at_posps, at_posp, at_cps, at_s, at_mx,
         at_sub, at_p, at_pTps, at_pT, at_ctxps, at_rz, at_ctx, at_ctxTps, at_ctxT, at_wops, at_res, at_ones) = [
             sem(n) for n in (
                 "at_bias at_pbps at_pbd at_y at_qkps at_qkv at_vps at_v at_posps at_posp at_cps at_s at_mx "
                 "at_sub at_p at_pTps at_pT at_ctxps at_rz at_ctx at_ctxTps at_ctxT at_wops at_res at_ones").split()]
        (ff_pad, ff_mm, ff_u, ff_t1, ff_t2, ff_t3, ff_s, ff_am, ff_red, ff_mr, ff_mi, ff_mul, ff_si, ff_ops,
         ff_fo, ff_fo_free, ff_res) = [sem(n) for n in (
             "ff_pad ff_mm ff_u ff_t1 ff_t2 ff_t3 ff_s ff_am ff_red ff_mr ff_mi ff_mul ff_si ff_ops "
             "ff_fo ff_fo_free ff_res").split()]
        (a1_y, a1_qps, a1_kps, a1_q, a1_k, a1_vps, a1_v, a1_wps, a1_w, a1_ops, a1_o, a1_pps, a1_res) = [
            sem(n) for n in (
                "a1_y a1_qps a1_kps a1_q a1_k a1_vps a1_v a1_wps a1_w a1_ops a1_o a1_pps a1_res").split()]
        (z_kept, rt_c, rt_lgps, rt_lg, rt_step, rt_cntps, rt_pos, rt_te, rt_pps, rt_cb, sc_zero, sc_rows,
         mo_b1, mo_x, mo_xTps, mo_xT, mo_h1ps, mo_h1a, mo_h1b, mo_hTps, mo_hTa, mo_hTb, mo_yps, mo_y,
         fin_add, fin_out, st_zero) = [
            sem(n) for n in (
                "z_kept rt_c rt_lgps rt_lg rt_step rt_cntps rt_pos rt_te rt_pps rt_cb sc_zero sc_rows "
                "mo_b1 mo_x mo_xTps mo_xT mo_h1ps mo_h1a mo_h1b mo_hTps mo_hTa mo_hTb mo_yps mo_y "
                "fin_add fin_out st_zero").split()]
        ld_patch = [sem(f"ld_patch{i}") for i in range(EG)]
        at_out = [sem(f"at_out{i}") for i in range(2)]
        at_in = [sem(f"at_in{i}") for i in range(2)]
        mo_xin = [sem(f"mo_xin{i}") for i in range(2)]
        mo_yout = [sem(f"mo_yout{i}") for i in range(2)]
        fin_in = [sem(f"fin_in{i}") for i in range(GATH)]

        block = ctx.enter_context(nc.Block())

        def tokps(par):
            return ps[:, par, :]

        def zTps(par):
            return ps[:, 2 + par, :]

        def pairs_then_last(e, step, last):
            step(0, 0, 2)
            step(1, 1, 2)
            with e.Fori(1, PAIRS // 2) as i:
                step(2 * i, 0, 2)
                step(2 * i + 1, 1, 2)
            last(PAIRS, 0, 1)

        def pairs_then_last_staged(e, first, second):
            first(0, 0, 2)
            first(1, 1, 2)
            second(0, 0, 2)
            first(2, 0, 2)
            second(1, 1, 2)
            first(3, 1, 2)
            second(2, 0, 2)
            with e.Fori(2, PAIRS // 2) as i:
                first(2 * i, 0, 2)
                second(2 * i - 1, 1, 2)
                first(2 * i + 1, 1, 2)
                second(2 * i, 0, 2)
            first(PAIRS, 0, 1)
            second(PAIRS - 1, 1, 2)
            second(PAIRS, 0, 1)

        @block.sync
        def _(sp):
            sp.dma_start(wproj, a["w_proj"]).then_inc(ld_emb, 16)
            for g in range(EG):
                sp.dma_start(patches[:, g], a["patches"][:, g]).then_inc(ld_patch[g], 16)
                if g == 0:
                    sp.dma_start(posb, a["pos"]).then_inc(ld_emb, 16)
                    sp.dma_start(bproj[:, :], a["b_proj"]).then_inc(ld_emb, 16)
            sp.dma_start(w1raw, a["w1"]).then_inc(ld_w12, 16)
            sp.dma_start(w2raw, a["w2"]).then_inc(ld_w12, 16)
            for t, n in ((gamma, "gamma"), (beta, "beta")):
                sp.dma_start(t[:, :], a[n]).then_inc(ld_ln, 16)
            for t, n in ((bqu, "u_bias"), (bqv, "v_bias"), (wsum[:, 0:1], "bq"), (bk0, "bk"), (bv0, "bv"),
                         (bo0, "bo"), (wq_bd, "wq"), (wk_bd, "wk"), (wv_bd, "wv"), (wo, "wo")):
                sp.dma_start(t[:, :], a[n]).then_inc(ld_at, 16)
            for t, n in ((convw, "conv_w"), (convb, "conv_b")):
                sp.dma_start(t[:, :], a[n]).then_inc(ld_ff, 16)
            for t, n in ((wqkv, "wqkv"), (bq1, "bq1"), (bk1, "bk1"), (bv1, "bv1"), (pjb, "pjb")):
                sp.dma_start(t[:, :], a[n]).then_inc(ld_a1, 16)
            for t, n in ((wr, "wr"), (br, "br"), (b1, "b1")):
                sp.dma_start(t[:, :], a[n]).then_inc(ld_rt, 16)
            for e in range(W_EARLY):
                sp.dma_start(moe_w[:, e * WE:(e + 1) * WE], a["moe_w"][:, e]).then_inc(ld_moe, 16)
            sp.wait_ge(wq_done, 2)
            sp.dma_start(pj_raw, a["pj"]).then_inc(ld_pj, 16)

            def shift(i, par):
                b = 2 * i + par
                wait(sp, at_in[par], 16 * i)
                sp.sem_inc(sync_past, 1)
                sp.wait_ge(at_posp, b + 1)
                sp.dma_start(scr[par].rearrange("h (i c) -> i h c", c=SP1),
                             posp[par].rearrange("p a (h c) -> p (a h) c", c=SP1)).then_inc(at_out[par], 16)
                wait(sp, at_s, b - 1)
                sp.sem_inc(sync_past, 1)
                sp.wait_ge(at_out[par], 16 * i + 16)
                sp.dma_start(poss[par].rearrange("p a (h c) -> p (a h) c", c=S),
                             scr[par][:, S:S + S * S].rearrange("h (i c) -> i h c", c=S)).then_inc(at_in[par], 16)

            shift(0, 0)
            shift(0, 1)
            with sp.Fori(1, B // 2) as i:
                shift(i, 0)
                shift(i, 1)
            sp.wait_ge(pj_done, 1)
            sp.dma_start(moe_w[:, W_EARLY * WE:(W_EARLY + 1) * WE], a["moe_w"][:, W_EARLY]).then_inc(ld_moe5, 16)
            sp.wait_ge(ff_res, GROUPS)
            for e in range(W_EARLY + 1, E):
                sp.dma_start(moe_w[:, e * WE:(e + 1) * WE], a["moe_w"][:, e]).then_inc(ld_moe67, 16)

            sp.dma_start(b2[:, :], a["b2"]).then_inc(ld_b2, 16)
            sp.wait_ge(st_zero, 1)
            for n in range(3):
                k = MAX_TILES // 3 * P
                sp.dma_start(xs[n * k:(n + 1) * k, :].rearrange("(p t) d -> p (t d)", p=P),
                             tm_t[:, 0:k // P * D]).then_inc(sc_zero, 16)

            def rows_in(i, par):
                wait(sp, mo_xTps, i - 1)
                sp.dma_start(xt[par], xs[bass.ds(i * P, P), :]).then_inc(mo_xin[par], 16)

            def rows_out(i, par):
                sp.wait_ge(mo_y, i + 1)
                sp.dma_start(ys[bass.ds(i * P, P), :], ysb[par]).then_inc(mo_yout[par], 16)

            sp.wait_ge(sc_rows, 16 * TILES)
            rows_in(0, 0)
            rows_in(1, 1)
            with sp.Fori(0, MAX_TILES // 2 - 1) as i:
                for par in range(2):
                    rows_in(2 * i + 2 + par, par)
                    rows_out(2 * i + par, par)
            rows_out(MAX_TILES - 2, 0)
            rows_out(MAX_TILES - 1, 1)

            for t in range(TILES):
                sp.wait_ge(fin_add, t + 1)
                sp.dma_start(out[t * P:(t + 1) * P, :], tm[:, t]).then_inc(fin_out, 16)
            sp.wait_ge(fin_out, 16 * TILES)

        @block.gpsimd
        def _(gp):
            gp.iota(gidx, [[1, NTXT]], base=0, channel_multiplier=0,
                    allow_small_or_imprecise_dtypes=True).then_inc(iotas, 1)
            gp.iota(base.rearrange("p (b s) -> p b s", b=B), [[S_TXT, B], [0, S_TXT]], base=0,
                    channel_multiplier=0, allow_small_or_imprecise_dtypes=True).then_inc(iotas, 1)
            gp.iota(pid[:, :], [[0, 1]], base=0, channel_multiplier=1,
                    allow_small_or_imprecise_dtypes=True).then_inc(iotas, 1)
            gp.memset(ident[:, :], 0.0).then_inc(consts, 1)
            gp.memset(onesf[:, :], 1.0).then_inc(consts, 1)
            gp.memset(neg_half[:, :], -0.5).then_inc(consts, 1)
            gp.memset(hmask[:, :], 1.0).then_inc(consts, 1)
            gp.memset(cmask[:, :], 1.0).then_inc(consts, 1)
            gp.wait_ge(consts, 5)
            gp.affine_select(out=ident[:, :], in_=ident[:, :], compare_op=ALU.not_equal, fill=1.0,
                             base=0, pattern=[[-1, P]], channel_multiplier=1).then_inc(consts, 1)
            gp.affine_select(out=cmask[:, :], in_=cmask[:, :], compare_op=ALU.is_ge, fill=0.0,
                             base=0, pattern=[[1, S]], channel_multiplier=-1).then_inc(consts, 1)
            gp.affine_select(out=hmask[:, :], in_=hmask[:, :], compare_op=ALU.is_ge, fill=0.0,
                             base=0, pattern=[[-DH, HC]], channel_multiplier=1).then_inc(consts, 1)
            gp.wait_ge(consts, 8)
            gp.affine_select(out=hmask[:, :], in_=hmask[:, :], compare_op=ALU.is_ge, fill=0.0,
                             base=DH - 1, pattern=[[DH, HC]], channel_multiplier=-1).then_inc(consts, 1)
            gp.tensor_copy(identb[:, :], ident[:, :]).then_inc(consts, 1)

            for n in range(2):
                gp.wait_ge(wq_abs, n + 1)
                gp.partition_all_reduce(wsum[:, 2 + n:3 + n], w1m[:, n:n + 1], P, RED.add).then_inc(wq_sum, 1)

            def past(gp):
                gp.sem_inc(pool_past, 1)

            def ln_rstd_all(k):
                gp.wait_ge(ln_mv, k + 1)
                if k == 0:
                    gp.tensor_scalar(ve[:, :], var[:, :], 1.0 + EPS, EPS * EPS,
                                     ALU.mult, ALU.add).then_inc(ln_ve, 1)
                else:
                    gp.tensor_scalar(ve[:, :], var[:, :], EPS, None, ALU.add).then_inc(ln_ve, 1)
                gp.wait_ge(ln_ve, k + 1)
                gp.tensor_tensor(rstd[:, :], ve[:, :], neg_half[:, :], ALU.pow).then_inc(ln_rstd, 1)

            ln_rstd_all(0)

            for par in range(2):
                gp.memset(vaug[par][:, :, DH:DH + 1], 1.0).then_inc(at_ones, 1)

            def y_slice(s, par):
                wait(gp, at_vps, s - 1)
                gp.tensor_copy(yst[par], yT[:, :, bass.ds(s * S, S)]).then_inc(at_y, 1)

            def subtract_max(s, par):
                gp.wait_ge(at_mx, s + 1)
                gp.tensor_tensor(sx[par], sx[par], mx[par].unsqueeze(2).to_broadcast([S, H, S]),
                                 ALU.subtract).then_inc(at_sub, 1)

            gp.wait_ge(ln_out, LN_STEPS)
            y_slice(0, 0)
            y_slice(1, 1)
            subtract_max(0, 0)
            with gp.Fori(1, B // 2) as i:
                for par in range(2):
                    y_slice(2 * i + par, par)
                    subtract_max(2 * i + par - 1, 1 - par)
            subtract_max(B - 1, 1)

            ln_rstd_all(1)

            for par in range(2):
                gp.memset(uu[par][:, :, 0:1], 0.0)
                gp.memset(uu[par][:, :, S + 1:S + 2], 0.0).then_inc(ff_pad, 1)

            def quantise(g, par):
                gp.wait_ge(ff_am, g + 1)
                wait(gp, ff_fo, g - 1)
                past(gp)
                gp.partition_all_reduce(mr[par], am[par], P, RED.absmax).then_inc(ff_red, 1)
                gp.wait_ge(ff_red, g + 1)
                past(gp)
                gp.tensor_scalar(mr[par], mr[par], EPS, 1.0 / 127.0, ALU.max, ALU.mult).then_inc(ff_mr, 1)
                gp.wait_ge(ff_mi, g + 1)
                gp.tensor_tensor(sv[par], sv[par], mi[par].unsqueeze(1).to_broadcast([P, FJ, GN]),
                                 ALU.mult).then_inc(ff_mul, 1)

            def ff_add(g, par):
                gp.wait_ge(ff_fo, g + 1)
                gp.tensor_tensor(hT[:, :, bass.ds(g * GN, GN)], hT[:, :, bass.ds(g * GN, GN)], fo[par],
                                 ALU.add).then_inc(ff_res, 1)
                gp.wait_ge(ff_res, g + 1)
                gp.sem_inc(ff_fo_free, 1)

            gp.sem_inc(ff_fo_free, 1)
            quantise(0, 0)
            with gp.Fori(0, GROUPS // 2 - 1) as i:
                quantise(2 * i + 1, 1)
                ff_add(2 * i, 0)
                quantise(2 * i + 2, 0)
                ff_add(2 * i + 1, 1)
            quantise(GROUPS - 1, 1)
            ff_add(GROUPS - 2, 0)
            ff_add(GROUPS - 1, 1)

            ln_rstd_all(2)

            def y_group(g, par):
                wait(gp, a1_vps, g - 1)
                gp.tensor_copy(y7[par], yT[:, :, bass.ds(g * GN, GN)]).then_inc(a1_y, 1)

            gp.wait_ge(ln_out, 3 * LN_STEPS)
            y_group(0, 0)
            y_group(1, 1)
            with gp.Fori(1, GROUPS // 2) as i:
                y_group(2 * i, 0)
                y_group(2 * i + 1, 1)
            gp.wait_ge(a1_vps, GROUPS)
            gp.wait_ge(a1_res, GROUPS)
            gp.memset(tm_t[:, 0:MAX_TILES // 3 * D], 0.0).then_inc(st_zero, 1)

            ln_rstd_all(3)

            def keep_z(u, par, n):
                gp.wait_ge(ln_z, 3 * LN_STEPS + u + 1)
                past(gp)
                gp.tensor_copy(hT_t[:, bass.ds(u * 2 * D, n * D)], z[par][:, 0:n * D]).then_inc(z_kept, 1)

            pairs_then_last(gp, keep_z, keep_z)
            gp.wait_ge(rt_lg, LN_STEPS)
            gp.iota(rev, [[-1, E]], base=E, channel_multiplier=0,
                    allow_small_or_imprecise_dtypes=True).then_inc(rt_c, 1)
            gp.iota(thr, [[0, E], [P, TILES]], base=0, channel_multiplier=0,
                    allow_small_or_imprecise_dtypes=True).then_inc(rt_c, 1)
            gp.iota(it24, [[1, MAX_TILES], [0, E]], base=0, channel_multiplier=0,
                    allow_small_or_imprecise_dtypes=True).then_inc(rt_c, 1)
            gp.memset(onesb, 1.0).then_inc(rt_c, 1)
            gp.wait_ge(rt_c, 4)
            gp.affine_select(out=triu, in_=onesb, compare_op=ALU.is_gt, fill=0.0, base=0,
                             pattern=[[1, P]], channel_multiplier=-1).then_inc(rt_c, 1)

            gp.wait_ge(rt_pos, 1)
            gp.wait_ge(z_kept, LN_STEPS)
            gp.wait_ge(sc_zero, 48)
            for t in range(TILES):
                gp.indirect_dma_start(xs, bass.IndirectOffsetOnAxis(ap=posu[:, t:t + 1], axis=0),
                                      z3[:, t], None).then_inc(sc_rows, 16)

            def bias_slice(i, par):
                e = gp.value_load(tei[0:1, bass.ds(i, 1)], min_val=0, max_val=E - 1)
                wait(gp, mo_hTa, i - 1)
                wait(gp, mo_hTb, i - 1)
                past(gp)
                gp.tensor_copy(b1s[par], b1[:, bass.ds(e * FJ, FJ)]).then_inc(mo_b1, 1)

            gp.wait_ge(rt_te, 1)
            bias_slice(0, 0)
            bias_slice(1, 1)
            with gp.Fori(1, MAX_TILES // 2) as i:
                bias_slice(2 * i, 0)
                bias_slice(2 * i + 1, 1)

            gp.wait_ge(mo_yout[0], 16 * MAX_TILES // 2)
            gp.wait_ge(mo_yout[1], 16 * MAX_TILES // 2)
            for t in range(TILES):
                wait(gp, fin_add, t - GATH + 1)
                gp.indirect_dma_start(fg[t % GATH], None, ys,
                                      bass.IndirectOffsetOnAxis(ap=posu[:, t:t + 1], axis=0)
                                      ).then_inc(fin_in[t % GATH], 16)

        @block.scalar
        def _(act):
            act.dma_start(tok_i, a["x_txt"]).then_inc(ld_txt, 16)
            act.dma_start(tab, a["table"]).then_inc(ld_emb, 16)
            act.dma_start(wp_bd, a["wp"]).then_inc(ld_pe, 16)
            for m in range(4):
                c, half = m // 2, m % 2
                act.wait_ge(txt_mm, m + 1)
                dst = hT[:, c].rearrange("p (b s) -> p b s", s=S)[:, half * B // 2:(half + 1) * B // 2, S_IMG:S]
                act.activation(dst, ps[:, 4 + m, 0:PSUM_W].rearrange("p (b s) -> p b s", s=S_TXT),
                               ACT.Copy).then_inc(txt_out, 1)
            act.dma_start(pe_bd, a["pe_bd"]).then_inc(ld_pe, 16)
            for c in range(C):
                act.wait_ge(at_pbps, c + 1)
                act.activation(pbd[:, c], ps[:, 4 + c, 0:HC * SP1], ACT.Copy).then_inc(at_pbd, 1)

            def evac_tok(k):
                def step(u, par, n):
                    g = k * LN_STEPS + u
                    act.wait_ge(ln_tokps, g + 1)
                    act.activation(tm_t[:, bass.ds(u * 2 * D, n * D)], tokps(par)[:, 0:n * D],
                                   ACT.Copy).then_inc(ln_tok, 1)
                pairs_then_last(act, step, step)

            def evac_zT(k):
                def step(u, par, n):
                    g = k * LN_STEPS + u
                    act.wait_ge(ln_zT, g + 1)
                    w = n * P
                    if k == 0:
                        for c in range(C):
                            ins = act.activation(yT[:, c, bass.ds(u * 2 * P, w)], zTps(par)[:, c * w:(c + 1) * w],
                                                 ACT.Identity, bias=beta[:, c:c + 1], scale=gamma[:, c:c + 1])
                    elif k == 1:
                        src = zTps(par).bitcast(BF16)[:, 0:C * w].rearrange("p (c n) -> p c n", c=C)
                        act.activation(ziT[:, :, bass.ds(u * 2 * P, w)], src, ACT.Copy)
                        act.wait_ge(q_bps, u + 1)
                        ins = act.activation(rsb[:, bass.ds(u * 2 * P, w)], ps[:, 4 + par, 0:w], ACT.Copy,
                                             scale=w1m[:, 0:1])
                    elif k == 2:
                        src = zTps(par)[:, 0:C * w].rearrange("p (c n) -> p c n", c=C)
                        ins = act.activation(yT[:, :, bass.ds(u * 2 * P, w)], src, ACT.Copy)
                    else:
                        wait(act, rt_lgps, u - 1)
                        src = zTps(par)[:, 0:C * w].rearrange("p (c n) -> p c n", c=C)
                        ins = act.activation(zTs[par][:, :, 0:w], src, ACT.Copy)
                    ins.then_inc(ln_out, 1)
                pairs_then_last(act, step, step)

            act.wait_ge(ld_ln, 32)
            act.wait_ge(emb_out, EG * C)
            evac_tok(0)
            evac_zT(0)

            def evac_v(s, par):
                act.wait_ge(at_vps, s + 1)
                wait(act, at_ctxps, s - 1)
                act.activation(vaug[par][:, :, 0:DH], ps[0:S, 1, 0:D].rearrange("p (h d) -> p h d", h=H),
                               ACT.Copy).then_inc(at_v, 1)

            def evac_pT(s, par):
                act.wait_ge(at_pTps, s + 1)
                wait(act, at_ctxps, s)
                act.activation(prT.rearrange("p (a h) c -> p a (h c)", a=C), ps[0:S, 6:8, 0:HC * S],
                               ACT.Copy).then_inc(at_pT, 1)

            def evac_pos(i, s, par):
                act.wait_ge(at_posps, s + 1)
                wait(act, at_out[par], 16 * i)
                act.activation(posp[par], ps[0:S, 2:4, 0:HC * SP1], ACT.Copy).then_inc(at_posp, 1)

            def evac_ctxT(s, par):
                act.wait_ge(at_ctxTps, s + 1)
                wait(act, at_wops, s)
                act.activation(ctxT, ps[:, 0, 0:C * S].rearrange("p (c n) -> p c n", c=C), ACT.Identity,
                               bias=bv0[:, 0:1]).then_inc(at_ctxT, 1)

            def exps(s, par):
                act.wait_ge(at_sub, s + 1)
                wait(act, at_pTps, s - 1)
                act.activation(pr[par], sx[par], ACT.Exp, scale=1.0 / D ** 0.5).then_inc(at_p, 1)

            act.wait_ge(ld_at, 160)
            evac_pos(0, 0, 0)
            evac_v(0, 0)
            evac_pos(0, 1, 1)
            exps(0, 0)
            with act.Fori(1, B // 2) as i:
                for par in range(2):
                    s = 2 * i + par
                    evac_v(s - 1, 1 - par)
                    evac_pT(s - 2, par)
                    evac_pos(i, s, par)
                    evac_ctxT(s - 2, par)
                    exps(s - 1, 1 - par)
            evac_v(B - 1, 1)
            evac_pT(B - 2, 0)
            evac_ctxT(B - 2, 0)
            exps(B - 1, 1)
            evac_pT(B - 1, 1)
            evac_ctxT(B - 1, 1)

            evac_tok(1)
            evac_zT(1)

            def tap_mid(k, j, kp):
                act.wait_ge(ff_u, k + 1)
                wait(act, ff_s, k - 1)
                act.activation(tt[kp], uu[kp][:, :, 1:S + 1], ACT.Identity, bias=convb[:, j:j + 1],
                               scale=convw[:, 3 * j + 1:3 * j + 2]).then_inc(ff_t1, 1)

            def silu(k, j, kp, gpar, g=None):
                act.wait_ge(ff_t3, k + 1)
                if j == 0:
                    wait(act, ff_si, g - 1)
                act.activation(sv[gpar][:, j].rearrange("p (b s) -> p b s", b=GB), tt[kp],
                               ACT.Silu).then_inc(ff_s, 1)

            def ff_group(g, gpar, first=False):
                for j in range(FJ):
                    k = g * FJ + j
                    tap_mid(k, j, j % 2)
                    if j > 0:
                        silu(k - 1, j - 1, (j - 1) % 2, gpar, g)
                    elif not first:
                        silu(k - 1, FJ - 1, 1, 1 - gpar)

            act.wait_ge(ld_ff, 32)
            ff_group(0, 0, True)
            ff_group(1, 1)
            with act.Fori(1, GROUPS // 2) as i:
                ff_group(2 * i, 0)
                ff_group(2 * i + 1, 1)
            silu(GROUPS * FJ - 1, FJ - 1, 1, 1)

            evac_tok(2)
            evac_zT(2)

            def evac_qk7(g, par):
                act.wait_ge(a1_qps, g + 1)
                wait(act, a1_wps, g - 1)
                act.activation(q7[par], ps[0:HS, 0, 0:GN], ACT.Identity, bias=bq1[:, 0:1]).then_inc(a1_q, 1)
                act.wait_ge(a1_kps, g + 1)
                act.activation(k7[par], ps[0:HS, 1, 0:GN], ACT.Identity, bias=bk1[:, 0:1]).then_inc(a1_k, 1)

            def evac_o7(g, par):
                act.wait_ge(a1_ops, g + 1)
                wait(act, a1_pps, g - 1)
                act.activation(o7[par], ps[0:HS, 4, 0:GN], ACT.Copy).then_inc(a1_o, 1)

            act.wait_ge(ld_a1, 80)
            evac_qk7(0, 0)
            evac_qk7(1, 1)
            evac_o7(0, 0)
            with act.Fori(1, GROUPS // 2) as i:
                for par in range(2):
                    evac_qk7(2 * i + par, par)
                    evac_o7(2 * i + par - 1, 1 - par)
            evac_o7(GROUPS - 1, 1)

            act.wait_ge(sc_zero, 48)
            evac_tok(3)
            evac_zT(3)

            def evac_x(i, par):
                act.wait_ge(mo_xTps, i + 1)
                wait(act, mo_h1ps, i - 1)
                act.activation(xT[par], ps[:, 6 + par, 0:D], ACT.Copy).then_inc(mo_xT, 1)

            def evac_h(i, par):
                act.wait_ge(mo_h1ps, i + 1)
                wait(act, mo_hTps, i)
                act.activation(h1[:, 0:PSUM_W], ps[:, 0, :], ACT.Copy).then_inc(mo_h1a, 1)

            def relu_a(i, par):
                act.wait_ge(mo_hTps, i + 1)
                act.wait_ge(mo_b1, i + 1)
                for j in range(FJ // 2):
                    ins = act.activation(hTm[:, j], ps[:, 2, j * P:(j + 1) * P], ACT.Relu,
                                         bias=b1s[par][:, j:j + 1])
                ins.then_inc(mo_hTa, 1)

            def expert_step(i, par, more=True):
                if more:
                    evac_x(i + 1, 1 - par)
                evac_h(i, par)
                relu_a(i, par)

            evac_x(0, 0)
            expert_step(0, 0)
            expert_step(1, 1)
            with act.Fori(1, MAX_TILES // 2 - 1) as i:
                expert_step(2 * i, 0)
                expert_step(2 * i + 1, 1)
            expert_step(MAX_TILES - 2, 0)
            expert_step(MAX_TILES - 1, 1, more=False)

        @block.vector
        def _(dve):
            n = [0]

            def step(ins):
                n[0] += 1
                ins.then_inc(txt_step, 1)

            def after_step():
                dve.wait_ge(txt_step, n[0])

            dve.wait_ge(ld_txt, 16)
            dve.wait_ge(iotas, 3)
            step(dve.tensor_copy(tokf, tok_i))
            after_step()
            step(dve.scalar_tensor_tensor(sepv, tokf, 4.0, gidx, ALU.is_equal, ALU.mult))
            step(dve.tensor_scalar(padv, gidx, 1.0, None, ALU.add))
            after_step()
            step(dve.tensor_tensor(sepv, sepv, base, ALU.max))
            step(dve.scalar_tensor_tensor(padv, tokf, 1.0, padv, ALU.is_equal, ALU.mult))
            after_step()
            step(dve.tensor_tensor_scan(runs, sepv, sepv, 0.0, ALU.max, ALU.max))
            step(dve.tensor_tensor_scan(runp, padv, padv, 0.0, ALU.max, ALU.max))
            after_step()
            step(dve.tensor_tensor(runs, gidx, runs, ALU.subtract))
            step(dve.tensor_tensor(runp, runp, base, ALU.is_le))
            after_step()
            step(dve.scalar_tensor_tensor(runs, runs, 1.0, runp, ALU.add, ALU.mult))
            after_step()
            step(dve.tensor_scalar(sepv, runs, 1.0, pid[0:TAB, 0:1], ALU.add, ALU.is_equal))

            dve.wait_ge(ld_emb, 64)
            for c in range(C):
                ins = dve.tensor_scalar(posb[:, c], posb[:, c], bproj[:, c:c + 1], None, ALU.add)
            ins.then_inc(posb_ok, 1)
            dve.wait_ge(posb_ok, 1)
            for g in range(EG):
                for c in range(C):
                    m = g * C + c
                    dve.wait_ge(emb_mm, m + 1)
                    nb = B // EG
                    dst = hT[:, c].rearrange("p (b s) -> p b s", s=S)[:, g * nb:(g + 1) * nb, 0:S_IMG]
                    dve.tensor_tensor(dst, ps[:, m % 4, 0:EGN].rearrange("p (b s) -> p b s", s=S_IMG),
                                      posb[:, c:c + 1, :].to_broadcast([P, nb, S_IMG]),
                                      ALU.add).then_inc(emb_out, 1)

            dve.wait_ge(ld_w12, 32)
            for n_, raw in enumerate((w1raw, w2raw)):
                dve.tensor_reduce(w1m[:, n_:n_ + 1], raw, AX.X, ALU.add,
                                  apply_absolute_value=True).then_inc(wq_abs, 1)
            dve.wait_ge(ld_at, 160)
            dve.tensor_scalar(bqu[:, :], bqu[:, :], wsum[:, 0:1], None, ALU.add)
            dve.tensor_scalar(bqv[:, :], bqv[:, :], wsum[:, 0:1], None, ALU.add).then_inc(at_bias, 1)
            dve.wait_ge(wq_sum, 2)
            dve.tensor_scalar(w1m[:, :], wsum[:, 2:4], 1.0 / (D * FF), EPS, ALU.mult, ALU.max).then_inc(wq_mean, 1)
            dve.wait_ge(wq_mean, 1)
            dve.wait_ge(at_bias, 1)
            dve.reciprocal(wsum[:, 0:2], w1m[:, :]).then_inc(wq_inv, 1)
            dve.wait_ge(wq_inv, 1)
            for n_, raw in enumerate((w1raw, w2raw)):
                dve.tensor_scalar(raw, raw, wsum[:, n_:n_ + 1], MAGIC, ALU.mult, ALU.add).then_inc(wq_a, 1)
            for n_, raw in enumerate((w1raw, w2raw)):
                dve.wait_ge(wq_a, n_ + 1)
                dve.tensor_scalar(raw, raw, -MAGIC, -1.0, ALU.add, ALU.max).then_inc(wq_b, 1)
            for n_, (raw, wi_n) in enumerate(((w1raw, w1i), (w2raw, w2i))):
                dve.wait_ge(wq_b, n_ + 1)
                dve.tensor_scalar(wi_n, raw, 1.0, None, ALU.min).then_inc(wq_done, 1)

            def gather_stats(k):
                def stage_in(u, par, n):
                    g = k * LN_STEPS + u
                    wait(dve, ln_tokps, g - 1)
                    dve.tensor_copy(stage[par][:, 0:n * D].rearrange("p (c n) -> p c n", c=C),
                                    hT[:, :, bass.ds(u * 2 * P, n * P)]).then_inc(ln_staged, 1)

                def stats(u, par, n):
                    g = k * LN_STEPS + u
                    dve.wait_ge(ln_tok, g + 1)
                    for m in range(n):
                        ins = dve.bn_stats(bn[:, bass.ds((2 * u + m) * 6, 6)],
                                           tm_t[:, bass.ds((2 * u + m) * D, D)])
                    ins.then_inc(ln_bn, 1)

                pairs_then_last_staged(dve, stage_in, stats)
                dve.wait_ge(ln_bn, (k + 1) * LN_STEPS)
                dve.tensor_tensor(bsum[:, 0], bnv[:, :, 2], bnv[:, :, 5], ALU.add)
                dve.tensor_tensor(bsum[:, 1], bnv[:, :, 1], bnv[:, :, 4], ALU.subtract)
                dve.tensor_tensor(bsum[:, 2], bnv[:, :, 1], bnv[:, :, 4], ALU.add).then_inc(ln_ba, 1)
                dve.wait_ge(ln_ba, 2 * k + 1)
                dve.scalar_tensor_tensor(bsum[:, 3], bsum[:, 1], 0.25, bsum[:, 1], ALU.mult, ALU.mult)
                dve.tensor_scalar(mean[:, :], bsum[:, 2], 0.5, None, ALU.mult).then_inc(ln_ba, 1)
                dve.wait_ge(ln_ba, 2 * k + 2)
                dve.scalar_tensor_tensor(var[:, :], bsum[:, 0], 1.0 / D, bsum[:, 3], ALU.mult,
                                         ALU.add).then_inc(ln_mv, 1)

            def normalise(k):
                def step(u, par, n):
                    g = k * LN_STEPS + u
                    wait(dve, ln_zT, g - 1)
                    if k == 3:
                        wait(dve, z_kept, u - 1)
                    for m in range(n):
                        t = 2 * u + m
                        dst = z[par][:, m * D:(m + 1) * D]
                        ins = dve.tensor_scalar(dst, tm_t[:, bass.ds(t * D, D)], mean[:, bass.ds(t, 1)],
                                                rstd[:, bass.ds(t, 1)], ALU.subtract, ALU.mult)
                    ins.then_inc(ln_z, 1)
                dve.wait_ge(ln_rstd, k + 1)
                pairs_then_last(dve, step, step)

            dve.wait_ge(txt_out, 4)
            dve.wait_ge(emb_out, EG * C)
            gather_stats(0)
            normalise(0)

            def evac_qk(s, par):
                dve.wait_ge(at_qkps, s + 1)
                wait(dve, at_cps, s - 1)
                wait(dve, at_posps, s)
                q_ps = ps[:, 0, 0:C * S].rearrange("p (c n) -> p c n", c=C)
                dve.tensor_tensor(qv, q_ps, bqv[:, :].unsqueeze(2).to_broadcast([P, C, S]), ALU.add)
                dve.tensor_tensor(qu[par], q_ps, bqu[:, :].unsqueeze(2).to_broadcast([P, C, S]), ALU.add)
                for c in range(C):
                    k_ps = ps[:, 0, (C + c) * S:(C + c + 1) * S]
                    ins = dve.scalar_tensor_tensor(
                        kbd[par][:, c].rearrange("p (h n) -> p h n", h=HC),
                        k_ps.unsqueeze(1).to_broadcast([P, HC, S]), bk0[:, 0:1],
                        hmask[:, :].unsqueeze(2).to_broadcast([P, HC, S]), ALU.add, ALU.mult)
                ins.then_inc(at_qkv, 1)

            def add_scores(i, s, par):
                dve.wait_ge(at_cps, s + 1)
                dve.wait_ge(at_in[par], 16 * i + 16)
                wait(dve, at_p, s - 1)
                dve.tensor_tensor(sx[par].rearrange("p (a h) c -> p a (h c)", a=C), ps[0:S, 4:6, 0:HC * S],
                                  poss[par], ALU.add).then_inc(at_s, 1)
                dve.wait_ge(at_s, s + 1)
                dve.tensor_reduce(mx[par], sx[par], AX.X, ALU.max).then_inc(at_mx, 1)

            def norm_ctx(s, par):
                dve.wait_ge(at_ctxps, s + 1)
                wait(dve, at_ctxTps, s)
                c_ps = ps[0:S, 1, 0:H * (DH + 1)].rearrange("p (h d) -> p h d", h=H)
                dve.reciprocal(rz, c_ps[:, :, DH]).then_inc(at_rz, 1)
                dve.wait_ge(at_rz, s + 1)
                dve.tensor_tensor(ctxn, c_ps[:, :, 0:DH], rz.unsqueeze(2).to_broadcast([S, H, DH]),
                                  ALU.mult).then_inc(at_ctx, 1)

            def add_res(s, par):
                dve.wait_ge(at_wops, s + 1)
                for c in range(C):
                    dst = hT[:, c, bass.ds(s * S, S)]
                    ins = dve.scalar_tensor_tensor(dst, ps[:, 0, (C + c) * S:(C + c + 1) * S], bo0[:, c:c + 1],
                                                   dst, ALU.add, ALU.add)
                ins.then_inc(at_res, 1)

            dve.wait_ge(consts, 10)
            evac_qk(0, 0)
            evac_qk(1, 1)
            add_scores(0, 0, 0)
            with dve.Fori(1, B // 2) as i:
                for par in range(2):
                    s = 2 * i + par
                    evac_qk(s, par)
                    norm_ctx(s - 2, par)
                    add_scores(i + par - 1, s - 1, 1 - par)
                    add_res(s - 2, par)
            norm_ctx(B - 2, 0)
            add_scores(B // 2 - 1, B - 1, 1)
            add_res(B - 2, 0)
            norm_ctx(B - 1, 1)
            add_res(B - 1, 1)

            dve.wait_ge(at_res, B)
            gather_stats(1)
            dve.wait_ge(ln_rstd, 2)
            with dve.Fori(0, TILES) as t:
                x = tm_t[:, bass.ds(t * D, D)]
                dve.tensor_scalar(x, x, mean[:, bass.ds(t, 1)], rstd[:, bass.ds(t, 1)],
                                  ALU.subtract, ALU.mult).then_inc(q_z, 1)
            dve.wait_ge(q_z, TILES)
            dve.tensor_reduce(amax[:, :], tm, AX.X, ALU.max, apply_absolute_value=True).then_inc(q_amax, 1)
            dve.wait_ge(q_amax, 1)
            dve.tensor_scalar(qstep[:, :], amax[:, :], EPS, 1.0 / 127.0, ALU.max, ALU.mult).then_inc(q_step, 1)
            dve.wait_ge(q_step, 1)
            dve.reciprocal(qinv[:, :], qstep[:, :]).then_inc(q_inv, 1)
            dve.wait_ge(q_inv, 1)

            def quant_step(u, par, n):
                g = LN_STEPS + u
                for m in range(n):
                    t = 2 * u + m
                    x = tm_t[:, bass.ds(t * D, D)]
                    ins = dve.tensor_scalar(x, x, qinv[:, bass.ds(t, 1)], MAGIC, ALU.mult, ALU.add)
                ins.then_inc(q_mul, 1)
                wait(dve, ln_zT, g - 1)
                wait(dve, q_bps, u - 1)
                for m in range(n):
                    ins = dve.tensor_scalar(stage[par][:, m * P:(m + 1) * P], ident[:, :],
                                            qstep[:, bass.ds(2 * u + m, 1)], None, ALU.mult)
                ins.then_inc(q_diag, 1)
                dve.wait_ge(q_mul, u + 1)
                dve.tensor_scalar(zb[par][:, 0:n * D], tm_t[:, bass.ds(u * 2 * D, n * D)], -MAGIC, None,
                                  ALU.add).then_inc(ln_z, 1)

            dve.wait_ge(ln_tokps, 2 * LN_STEPS)
            pairs_then_last(dve, quant_step, quant_step)

            def dequant(k, kp, g):
                dve.wait_ge(ff_mm, k + 1)
                wait(dve, ff_t3, k - 1)
                dve.tensor_tensor(uu[kp][:, :, 1:S + 1], ps[:, kp, 0:GN].rearrange("p (b s) -> p b s", b=GB),
                                  rsb[:, bass.ds(g * GN, GN)].rearrange("p (b s) -> p b s", b=GB),
                                  ALU.mult).then_inc(ff_u, 1)

            def taps(k, j, kp):
                dve.wait_ge(ff_t1, k + 1)
                dve.scalar_tensor_tensor(tt[kp], uu[kp][:, :, 0:S], convw[:, 3 * j:3 * j + 1], tt[kp],
                                         ALU.mult, ALU.add).then_inc(ff_t2, 1)
                dve.wait_ge(ff_t2, k + 1)
                dve.scalar_tensor_tensor(tt[kp], uu[kp][:, :, 2:S + 2], convw[:, 3 * j + 2:3 * j + 3], tt[kp],
                                         ALU.mult, ALU.add).then_inc(ff_t3, 1)

            def largest(g, gpar):
                dve.wait_ge(ff_s, (g + 1) * FJ)
                wait(dve, ff_red, g - 1)
                dve.tensor_reduce(am[gpar], sv[gpar].rearrange("p j n -> p n j"), AX.X, ALU.max,
                                  apply_absolute_value=True).then_inc(ff_am, 1)

            def invert(g, gpar):
                dve.wait_ge(ff_mr, g + 1)
                dve.reciprocal(mi[gpar], mr[gpar]).then_inc(ff_mi, 1)

            def round_si(g, gpar):
                dve.wait_ge(ff_mul, g + 1)
                wait(dve, ff_ops, g)
                dve.tensor_scalar(si, sv[gpar], MAGIC, -MAGIC, ALU.add, ALU.add).then_inc(ff_si, 1)

            def ff_out(g, gpar):
                dve.wait_ge(ff_ops, g + 1)
                wait(dve, ff_fo_free, g)
                for c in range(C):
                    ins = dve.scalar_tensor_tensor(fo[gpar][:, c], ps[:, 4 + c, 0:GN], w1m[:, 1:2], mr[gpar],
                                                   ALU.mult, ALU.mult)
                ins.then_inc(ff_fo, 1)

            def ff_group(g, gpar, first=False, second=False):
                for j in range(FJ):
                    k = g * FJ + j
                    dequant(k, j % 2, g)
                    if j > 0 or not first:
                        taps(k - 1, (j - 1) % FJ, (j - 1) % 2)
                    if not first:
                        if j == 1:
                            largest(g - 1, 1 - gpar)
                            if not second:
                                ff_out(g - 2, gpar)
                        if j == 4:
                            invert(g - 1, 1 - gpar)
                        if j == 7:
                            round_si(g - 1, 1 - gpar)

            dve.wait_ge(ln_out, 2 * LN_STEPS)
            dve.wait_ge(ff_pad, 2)
            ff_group(0, 0, first=True)
            ff_group(1, 1, second=True)
            with dve.Fori(1, GROUPS // 2) as i:
                ff_group(2 * i, 0)
                ff_group(2 * i + 1, 1)
            taps(GROUPS * FJ - 1, FJ - 1, 1)
            ff_out(GROUPS - 2, 0)
            largest(GROUPS - 1, 1)
            invert(GROUPS - 1, 1)
            round_si(GROUPS - 1, 1)
            ff_out(GROUPS - 1, 1)

            dve.wait_ge(ld_pj, 16)
            dve.tensor_reduce(pj[:, :], pj_raw, AX.X, ALU.add).then_inc(pj_done, 1)

            dve.wait_ge(ff_res, GROUPS)
            gather_stats(2)
            normalise(2)

            def evac_v7(g, par):
                dve.wait_ge(a1_vps, g + 1)
                wait(dve, a1_ops, g - 1)
                dve.tensor_tensor(v7[par], ps[0:S, 2, 0:GB * HS].rearrange("p (b d) -> p b d", b=GB),
                                  bv1[:, :].unsqueeze(1).to_broadcast([S, GB, HS]), ALU.add).then_inc(a1_v, 1)

            def mask7(g, par):
                dve.wait_ge(a1_wps, g + 1)
                wait(dve, a1_ops, g - 1)
                dve.tensor_tensor(w7[par], ps[0:S, 3, 0:GN].rearrange("p (b n) -> p b n", b=GB),
                                  cmask[:, :].unsqueeze(1).to_broadcast([S, GB, S]), ALU.mult).then_inc(a1_w, 1)

            def add7(g, par):
                dve.wait_ge(a1_pps, g + 1)
                for c in range(C):
                    dst = hT[:, c, bass.ds(g * GN, GN)]
                    ins = dve.scalar_tensor_tensor(dst, ps[:, 5 + c, 0:GN], pjb[:, c:c + 1], dst,
                                                   ALU.add, ALU.add)
                ins.then_inc(a1_res, 1)

            dve.wait_ge(ld_a1, 80)
            evac_v7(0, 0)
            evac_v7(1, 1)
            mask7(0, 0)
            add7(0, 0)
            with dve.Fori(1, GROUPS // 2) as i:
                for par in range(2):
                    s = 2 * i + par
                    evac_v7(s, par)
                    mask7(s - 1, 1 - par)
                    add7(s - 1, 1 - par)
            mask7(GROUPS - 1, 1)
            add7(GROUPS - 1, 1)

            dve.wait_ge(a1_res, GROUPS)
            gather_stats(3)
            dve.wait_ge(ln_staged, 4 * LN_STEPS)

            normalise(3)

            dve.wait_ge(ld_rt, 48)
            dve.wait_ge(rt_lgps, LN_STEPS)
            dve.tensor_tensor(lgv, ps[:, 4, 0:TILES * E].rearrange("p (t e) -> p t e", e=E),
                              br[:, :].unsqueeze(1).to_broadcast([P, TILES, E]), ALU.add).then_inc(rt_lg, LN_STEPS)

            n[0] = 0

            def rstep(ins):
                n[0] += 1
                ins.then_inc(rt_step, 1)
                dve.wait_ge(rt_step, n[0])

            dve.wait_ge(rt_c, 5)
            dve.wait_ge(rt_lg, LN_STEPS)
            rstep(dve.tensor_reduce(rcol, lgv, AX.X, ALU.max))
            rstep(dve.tensor_tensor(rt, lgv, rcol.unsqueeze(2).to_broadcast([P, TILES, E]), ALU.is_equal))
            rstep(dve.tensor_tensor(rt, rt, rev.unsqueeze(1).to_broadcast([P, TILES, E]), ALU.mult))
            rstep(dve.tensor_reduce(rcol, rt, AX.X, ALU.max))
            rstep(dve.tensor_tensor(oh, rev.unsqueeze(1).to_broadcast([P, TILES, E]),
                                    rcol.unsqueeze(2).to_broadcast([P, TILES, E]), ALU.is_equal))
            dve.tensor_copy(ohb, oh)
            rstep(dve.tensor_reduce(cntp, oh.rearrange("p t e -> p e t"), AX.X, ALU.add))
            dve.tensor_copy(cntb, cntp).then_inc(rt_cb, 1)
            dve.wait_ge(rt_cntps, 1)
            rstep(dve.tensor_copy(nt, ps[:, 5, 0:E]))
            rstep(dve.tensor_tensor(cmp_, nt.unsqueeze(2).to_broadcast([P, E, TILES]), thr, ALU.is_gt))
            rstep(dve.tensor_reduce(nt, cmp_, AX.X, ALU.add))
            rstep(dve.tensor_tensor_scan(tend, onesf[:, 0:E], nt, 0.0, ALU.mult, ALU.add))
            rstep(dve.tensor_tensor(tst, tend, nt, ALU.subtract))
            rstep(dve.tensor_scalar(tst, tst, float(P), None, ALU.mult))
            dve.wait_ge(rt_pps, 1)
            rstep(dve.tensor_tensor(rt, ps[:, 6, 0:TILES * E].rearrange("p (t e) -> p t e", e=E),
                                    tst.unsqueeze(1).to_broadcast([P, TILES, E]), ALU.add))
            rstep(dve.tensor_tensor(rt, rt, oh, ALU.mult))
            rstep(dve.tensor_reduce(rcol, rt, AX.X, ALU.add))
            dve.tensor_copy(posu[:, :], rcol).then_inc(rt_pos, 1)
            rstep(dve.tensor_tensor(it24, it24, tend.unsqueeze(1).to_broadcast([P, MAX_TILES, E]), ALU.is_ge))
            rstep(dve.tensor_reduce(te, it24, AX.X, ALU.add))
            dve.tensor_scalar(tei[:, :], te[0:1, :], float(E - 1), None, ALU.min).then_inc(rt_te, 1)

            def evac_h(i, par):
                dve.wait_ge(mo_h1ps, i + 1)
                wait(dve, mo_hTps, i)
                dve.tensor_copy(h1[:, PSUM_W:FF], ps[:, 1, :]).then_inc(mo_h1b, 1)

            def relu_b(i, par):
                dve.wait_ge(mo_hTps, i + 1)
                dve.wait_ge(mo_b1, i + 1)
                for j in range(FJ // 2, FJ):
                    ins = dve.tensor_scalar(hTm[:, j], ps[:, 3, (j - FJ // 2) * P:(j - FJ // 2 + 1) * P],
                                            b1s[par][:, j:j + 1], 0.0, ALU.add, ALU.max)
                ins.then_inc(mo_hTb, 1)

            def out_y(i, ii, par):
                e = dve.value_load(tei[0:1, bass.ds(i, 1)], min_val=0, max_val=E - 1)
                dve.wait_ge(mo_yps, i + 1)
                wait(dve, mo_yout[par], 16 * ii)
                dve.tensor_tensor(ysb[par], ps[:, 4 + par, 0:D], b2[:, bass.ds(e * D, D)],
                                  ALU.add).then_inc(mo_y, 1)

            dve.wait_ge(rt_te, 1)
            dve.wait_ge(ld_b2, 16)
            evac_h(0, 0)
            relu_b(0, 0)
            evac_h(1, 1)
            out_y(0, 0, 0)
            relu_b(1, 1)
            with dve.Fori(1, MAX_TILES // 2) as i:
                for par in range(2):
                    s = 2 * i + par
                    evac_h(s, par)
                    out_y(s - 1, i + par - 1, 1 - par)
                    relu_b(s, par)
            out_y(MAX_TILES - 1, MAX_TILES // 2 - 1, 1)

            for t in range(TILES):
                dve.wait_ge(fin_in[t % GATH], 16 * (t // GATH + 1))
                dve.tensor_tensor(tm[:, t], tm[:, t], fg[t % GATH], ALU.add).then_inc(fin_add, 1)

        @block.tensor
        def _(pe):
            pe.wait_ge(ld_emb, 64)
            for g in range(EG):
                pe.wait_ge(ld_patch[g], 16)
                for c in range(C):
                    m = g * C + c
                    wait(pe, emb_out, m - 3)
                    for k in range(KP):
                        ins = pe.matmul(ps[:, m % 4, 0:EGN], wproj[:, k, c * P:(c + 1) * P],
                                        patches[:, g, k], start=(k == 0), stop=(k == KP - 1))
                    ins.then_inc(emb_mm, 1)
            pe.wait_ge(txt_step, 11)
            for m in range(4):
                c, half = m // 2, m % 2
                pe.matmul(ps[:, 4 + m, 0:PSUM_W], tab[:, c * P:(c + 1) * P],
                          sepv[:, half * PSUM_W:(half + 1) * PSUM_W], start=True, stop=True).then_inc(txt_mm, 1)
            pe.wait_ge(ld_pe, 32)
            pe.wait_ge(txt_out, 4)
            for c in range(C):
                pe.matmul(ps[:, 4 + c, 0:HC * SP1], wp_bd, pe_bd[:, c], start=True, stop=True).then_inc(at_pbps, 1)

            def to_tokens(k):
                def step(u, par, n):
                    g = k * LN_STEPS + u
                    pe.wait_ge(ln_staged, g + 1)
                    wait(pe, ln_tok, g - 1)
                    for m in range(n):
                        for c in range(C):
                            ins = pe.transpose(tokps(par)[:, m * D + c * P:m * D + (c + 1) * P],
                                               stage[par][:, c * n * P + m * P:c * n * P + (m + 1) * P],
                                               ident[:, :])
                    ins.then_inc(ln_tokps, 1)
                pairs_then_last(pe, step, step)

            def to_features(k):
                def step(u, par, n):
                    g = k * LN_STEPS + u
                    pe.wait_ge(ln_z, g + 1)
                    wait(pe, ln_out, g - 1)
                    for c in range(C):
                        for m in range(n):
                            lo = c * n * P + m * P
                            if k == 1:
                                ins = pe.transpose(zTps(par).bitcast(BF16)[:, lo:lo + P],
                                                   zb[par][:, m * D + c * P:m * D + (c + 1) * P], identb[:, :])
                            else:
                                ins = pe.transpose(zTps(par)[:, lo:lo + P],
                                                   z[par][:, m * D + c * P:m * D + (c + 1) * P], ident[:, :])
                    ins.then_inc(ln_zT, 1)
                    if k == 1:
                        pe.wait_ge(q_diag, u + 1)
                        pe.matmul(ps[:, 4 + par, 0:n * P], onesf[:, :], stage[par][:, 0:n * P],
                                  start=True, stop=True).then_inc(q_bps, 1)
                pairs_then_last(pe, step, step)

            pe.wait_ge(consts, 10)
            pe.wait_ge(emb_out, EG * C)
            to_tokens(0)
            to_features(0)

            def project_qk(s, par):
                pe.wait_ge(at_y, s + 1)
                wait(pe, at_res, s - 2)
                for c in range(C):
                    pe.matmul(ps[:, 0, c * S:(c + 1) * S], wq_bd[:, :], yst[par][:, c], start=True, stop=True)
                for c in range(C):
                    ins = pe.matmul(ps[:, 0, (C + c) * S:(C + c + 1) * S], wk_bd[:, :], yst[par][:, c],
                                    start=True, stop=True)
                ins.then_inc(at_qkps, 1)

            def project_v(s, par):
                wait(pe, at_ctx, s - 1)
                wait(pe, at_v, s)
                for c in range(C):
                    ins = pe.matmul(ps[0:S, 1, c * P:(c + 1) * P], yst[par][:, c], wv_bd[:, :],
                                    start=True, stop=True)
                ins.then_inc(at_vps, 1)

            def content(s, par):
                pe.wait_ge(at_qkv, s + 1)
                wait(pe, at_s, s)
                for c in range(C):
                    ins = pe.matmul(ps[0:S, 4 + c, 0:HC * S], qu[par][:, c], kbd[par][:, c], start=True, stop=True)
                ins.then_inc(at_cps, 1)

            def position(s, par):
                pe.wait_ge(at_qkv, s + 1)
                wait(pe, at_posp, s)
                for c in range(C):
                    ins = pe.matmul(ps[0:S, 2 + c, 0:HC * SP1], qv[:, c], pbd[:, c], start=True, stop=True)
                ins.then_inc(at_posps, 1)

            def transpose_p(s, par):
                pe.wait_ge(at_p, s + 1)
                wait(pe, at_pT, s)
                for h in range(H):
                    ins = pe.transpose(ps[0:S, 6 + h // HC, h % HC * S:(h % HC + 1) * S], pr[par][:, h],
                                       ident[0:S, 0:S])
                ins.then_inc(at_pTps, 1)

            def context(s, par, v_after):
                pe.wait_ge(at_pT, s + 1)
                pe.wait_ge(at_v, v_after)
                for h in range(H):
                    ins = pe.matmul(ps[0:S, 1, h * (DH + 1):(h + 1) * (DH + 1)], prT[:, h], vaug[par][:, h],
                                    start=True, stop=True)
                ins.then_inc(at_ctxps, 1)

            def out_proj(s, par, qk_after):
                pe.wait_ge(at_ctx, s + 1)
                pe.wait_ge(at_qkv, qk_after)
                flat = ctxn.rearrange("p h d -> p (h d)")
                for c in range(C):
                    ins = pe.transpose(ps[:, 0, c * S:(c + 1) * S], flat[:, c * P:(c + 1) * P], ident[0:S, 0:S])
                ins.then_inc(at_ctxTps, 1)
                pe.wait_ge(at_ctxT, s + 1)
                for c in range(C):
                    for k in range(C):
                        ins = pe.matmul(ps[:, 0, (C + c) * S:(C + c + 1) * S],
                                        wo[:, k * D + c * P:k * D + (c + 1) * P], ctxT[:, k],
                                        start=(k == 0), stop=(k == C - 1))
                ins.then_inc(at_wops, 1)

            pe.wait_ge(ld_at, 160)
            pe.wait_ge(at_pbd, 2)
            pe.wait_ge(at_ones, 2)
            project_qk(0, 0)
            position(0, 0)
            project_qk(1, 1)
            content(0, 0)
            project_v(0, 0)
            position(1, 1)
            with pe.Fori(1, B // 2) as i:
                for par in range(2):
                    s = 2 * i + par
                    project_qk(s, par)
                    content(s - 1, 1 - par)
                    project_v(s - 1, 1 - par)
                    transpose_p(s - 2, par)
                    position(s, par)
                    context(s - 2, par, s)
                    out_proj(s - 2, par, s + 1)
            content(B - 1, 1)
            project_v(B - 1, 1)
            transpose_p(B - 2, 0)
            context(B - 2, 0, B)
            pe.wait_ge(at_res, B - 2)
            out_proj(B - 2, 0, B)
            transpose_p(B - 1, 1)
            pe.wait_ge(at_ctx, B - 1)
            context(B - 1, 1, B)
            pe.wait_ge(at_res, B - 1)
            out_proj(B - 1, 1, B)

            to_tokens(1)
            to_features(1)

            w1v = w1i.rearrange("p (c f) -> p c f", c=C)
            w2v = w2i.rearrange("p (j d) -> p j d", j=FJ)

            def up(k, j, g):
                wait(pe, ff_u, k - 1)
                for c in range(C):
                    ins = pe.matmul(ps[:, j % 2, 0:GN], w1v[:, c, j * P:(j + 1) * P],
                                    ziT[:, c, bass.ds(g * GN, GN)], start=(c == 0), stop=(c == C - 1))
                ins.then_inc(ff_mm, 1)

            def down(g):
                pe.wait_ge(ff_si, g + 1)
                wait(pe, ff_fo, g)
                for c in range(C):
                    for j in range(FJ):
                        ins = pe.matmul(ps[:, 4 + c, 0:GN], w2v[:, j, c * P:(c + 1) * P], si[:, j],
                                        start=(j == 0), stop=(j == FJ - 1))
                ins.then_inc(ff_ops, 1)

            def ff_group(g, first=False):
                for j in range(FJ):
                    up(g * FJ + j, j, g)
                if not first:
                    down(g - 1)

            pe.wait_ge(ln_out, 2 * LN_STEPS)
            pe.wait_ge(wq_done, 2)
            ff_group(0, True)
            with pe.Fori(1, GROUPS) as g:
                ff_group(g)
            down(GROUPS - 1)

            to_tokens(2)
            to_features(2)

            def project7(g, par):
                pe.wait_ge(a1_y, g + 1)
                wait(pe, a1_q, g)
                for c in range(C):
                    ins = pe.matmul(ps[0:HS, 0, 0:GN], wqkv_v[:, c, 0:HS], y7[par][:, c],
                                    start=(c == 0), stop=(c == C - 1))
                ins.then_inc(a1_qps, 1)
                wait(pe, a1_k, g)
                for c in range(C):
                    ins = pe.matmul(ps[0:HS, 1, 0:GN], wqkv_v[:, c, HS:2 * HS], y7[par][:, c],
                                    start=(c == 0), stop=(c == C - 1))
                ins.then_inc(a1_kps, 1)
                wait(pe, a1_v, g)
                for b in range(GB):
                    for c in range(C):
                        ins = pe.matmul(ps[0:S, 2, b * HS:(b + 1) * HS], y7[par][:, c, b * S:(b + 1) * S],
                                        wqkv_v[:, c, 2 * HS:3 * HS], start=(c == 0), stop=(c == C - 1))
                ins.then_inc(a1_vps, 1)

            def attend7(g, par):
                pe.wait_ge(a1_q, g + 1)
                pe.wait_ge(a1_k, g + 1)
                for b in range(GB):
                    ins = pe.matmul(ps[0:S, 3, b * S:(b + 1) * S], k7[par][:, b * S:(b + 1) * S],
                                    q7[par][:, b * S:(b + 1) * S], start=True, stop=True)
                ins.then_inc(a1_wps, 1)
                pe.wait_ge(a1_w, g + 1)
                pe.wait_ge(a1_v, g + 1)
                for b in range(GB):
                    ins = pe.matmul(ps[0:HS, 4, b * S:(b + 1) * S], v7[par][:, b], w7[par][:, b],
                                    start=True, stop=True)
                ins.then_inc(a1_ops, 1)
                pe.wait_ge(a1_o, g + 1)
                wait(pe, a1_res, g)
                for c in range(C):
                    ins = pe.matmul(ps[:, 5 + c, 0:GN], pj[:, c * P:(c + 1) * P], o7[par], start=True, stop=True)
                ins.then_inc(a1_pps, 1)

            pe.wait_ge(ld_a1, 80)
            pe.wait_ge(pj_done, 1)
            project7(0, 0)
            project7(1, 1)
            attend7(0, 0)
            with pe.Fori(1, GROUPS // 2) as i:
                for par in range(2):
                    project7(2 * i + par, par)
                    attend7(2 * i + par - 1, 1 - par)
            attend7(GROUPS - 1, 1)

            to_tokens(3)

            def z_transposed(u, par, n):
                g = 3 * LN_STEPS + u
                pe.wait_ge(ln_z, g + 1)
                wait(pe, ln_out, g - 1)
                for c in range(C):
                    for m in range(n):
                        lo = c * n * P + m * P
                        ins = pe.transpose(zTps(par)[:, lo:lo + P], z[par][:, m * D + c * P:m * D + (c + 1) * P],
                                           ident[:, :])
                ins.then_inc(ln_zT, 1)

            def router(u, par, n):
                pe.wait_ge(ln_out, 3 * LN_STEPS + u + 1)
                for m in range(n):
                    for c in range(C):
                        ins = pe.matmul(ps[:, 4, bass.ds((2 * u + m) * E, E)], zTs[par][:, c, m * P:(m + 1) * P],
                                        wr[:, c * E:(c + 1) * E], start=(c == 0), stop=(c == C - 1))
                ins.then_inc(rt_lgps, 1)

            pe.wait_ge(ld_rt, 48)
            z_transposed(0, 0, 2)
            z_transposed(1, 1, 2)
            router(0, 0, 2)
            with pe.Fori(1, PAIRS // 2) as i:
                for par in range(2):
                    z_transposed(2 * i + par, par, 2)
                    router(2 * i + par - 1, 1 - par, 2)
            z_transposed(PAIRS, 0, 1)
            router(PAIRS - 1, 1, 2)
            router(PAIRS, 0, 1)

            pe.wait_ge(rt_cb, 1)
            pe.matmul(ps[:, 5, 0:E], onesb, cntb, start=True, stop=True).then_inc(rt_cntps, 1)
            flat = ohb.rearrange("p t e -> p (t e)")
            pe.matmul(ps[:, 6, 0:TILES * E], triu, flat, start=True, stop=False)
            for t in range(TILES - 1):
                m = TILES - 1 - t
                ins = pe.matmul(ps[:, 6, (t + 1) * E:TILES * E].rearrange("p (t e) -> p t e", e=E), onesb,
                                ohb[:, t:t + 1, :].to_broadcast([P, m, E]), start=False, stop=(m == 1))
            ins.then_inc(rt_pps, 1)

            def rows_T(i, ii, par):
                pe.wait_ge(mo_xin[par], 16 * ii + 16)
                wait(pe, mo_xT, i - 1)
                for c in range(C):
                    ins = pe.transpose(ps[:, 6 + par, c * P:(c + 1) * P], xt[par][:, c * P:(c + 1) * P],
                                       ident[:, :])
                ins.then_inc(mo_xTps, 1)

            def up_e(i, par):
                e = pe.value_load(tei[0:1, bass.ds(i, 1)], min_val=0, max_val=E - 1)
                pe.wait_ge(mo_xT, i + 1)
                wait(pe, mo_h1a, i)
                wait(pe, mo_h1b, i)
                for half in range(2):
                    for c in range(C):
                        ins = pe.matmul(ps[:, half, :], xT[par][:, c * P:(c + 1) * P],
                                        moe_w[:, bass.ds(e * WE + c * FF + half * PSUM_W, PSUM_W)],
                                        start=(c == 0), stop=(c == C - 1))
                ins.then_inc(mo_h1ps, 1)

            def hidden_T(i, par):
                pe.wait_ge(mo_h1a, i + 1)
                pe.wait_ge(mo_h1b, i + 1)
                wait(pe, mo_hTa, i)
                wait(pe, mo_hTb, i)
                for j in range(FJ):
                    ins = pe.transpose(ps[:, 2 + j // 4, j % 4 * P:(j % 4 + 1) * P], h1[:, j * P:(j + 1) * P],
                                       ident[:, :])
                ins.then_inc(mo_hTps, 1)

            def down_e(i, par):
                e = pe.value_load(tei[0:1, bass.ds(i, 1)], min_val=0, max_val=E - 1)
                pe.wait_ge(mo_hTa, i + 1)
                pe.wait_ge(mo_hTb, i + 1)
                wait(pe, mo_y, i - 1)
                for j in range(FJ):
                    ins = pe.matmul(ps[:, 4 + par, 0:D], hTm[:, j],
                                    moe_w[:, bass.ds(e * WE + C * FF + j * D, D)],
                                    start=(j == 0), stop=(j == FJ - 1))
                ins.then_inc(mo_yps, 1)

            pe.wait_ge(rt_te, 1)
            pe.wait_ge(ld_moe, 16 * W_EARLY)
            pe.wait_ge(ld_moe5, 16)
            pe.wait_ge(ld_moe67, 32)
            rows_T(0, 0, 0)
            up_e(0, 0)
            rows_T(1, 0, 1)
            hidden_T(0, 0)
            up_e(1, 1)
            down_e(0, 0)
            rows_T(2, 1, 0)
            hidden_T(1, 1)
            with pe.Fori(1, MAX_TILES // 2 - 1) as i:
                for par in range(2):
                    s = 2 * i + par
                    up_e(s, par)
                    down_e(s - 1, 1 - par)
                    rows_T(s + 1, i + par, 1 - par)
                    hidden_T(s, par)
            s = MAX_TILES - 2
            up_e(s, 0)
            down_e(s - 1, 1)
            rows_T(s + 1, MAX_TILES // 2 - 1, 1)
            hidden_T(s, 0)
            up_e(s + 1, 1)
            down_e(s, 0)
            hidden_T(s + 1, 1)
            down_e(s + 1, 1)


def lay_out(i):
    def cols(v):
        return v.reshape(-1, P).T

    def feat(w):
        return w.T.reshape(-1, P, w.shape[0]).transpose(1, 0, 2)

    def heads(w):
        m = np.zeros((P, P), w.dtype)
        for h in range(HC):
            m[h * DH:(h + 1) * DH, h * DH:(h + 1) * DH] = w
        return m

    def every(v):
        return np.broadcast_to(v.reshape(1, -1), (P, v.size))

    pos = np.arange(S, dtype=np.float32)[:, None]
    div = np.exp(np.arange(0, D, 2, dtype=np.float32) * np.float32(-np.log(10000.0) / D))
    pe = np.zeros((S, D), np.float32)
    pe[:, 0::2] = np.sin(pos * div)
    pe[:, 1::2] = np.cos(pos * div)
    pe_bd = np.zeros((P, C, HC, SP1), np.float32)
    for c in range(C):
        for h in range(HC):
            lo = (c * HC + h) * DH
            pe_bd[h * DH:(h + 1) * DH, c, h, 1:] = pe[:, lo:lo + DH].T

    hp = 6
    patches = (i["x"].reshape(B, hp, 16, hp, 16, 3).transpose(0, 1, 3, 2, 4, 5)
               .reshape(EG, EGN, KP, P).transpose(3, 0, 2, 1))
    w1e = i["L1_ffn_W1"].transpose(2, 0, 1).reshape(C, P, E, FF).transpose(1, 2, 0, 3).reshape(P, E, C * FF)
    w2e = i["L1_ffn_W2"].transpose(2, 0, 1).reshape(FJ, P, E, D).transpose(1, 2, 0, 3).reshape(P, E, FJ * D)
    qkv_b = i["L1_attn_qkv_b"]
    return {
        "patches": patches,
        "w_proj": feat(i["L0_tok_W_proj"]),
        "pos": feat(i["L0_tok_pos_emb"]),
        "b_proj": cols(i["L0_tok_b_proj"]),
        "x_txt": np.broadcast_to(i["x_txt"].reshape(1, -1), (TAB, NTXT)),
        "table": i["L0_txt_weights"][:TAB],
        "gamma": cols(i["L0_attn_ln_gamma"]),
        "beta": cols(i["L0_attn_ln_beta"]),
        "wq": heads(i["L0_attn_Wq"]), "wk": heads(i["L0_attn_Wk"]),
        "wv": heads(i["L0_attn_Wv"]), "wp": heads(i["L0_attn_Wp"]),
        "bq": np.tile(i["L0_attn_bq"], HC).reshape(P, 1),
        "bk": np.tile(i["L0_attn_bk"], HC).reshape(P, 1),
        "bv": np.tile(i["L0_attn_bv"], HC).reshape(P, 1),
        "u_bias": cols(i["L0_attn_u_bias"]), "v_bias": cols(i["L0_attn_v_bias"]),
        "wo": i["L0_attn_Wo"].reshape(C, P, D).transpose(1, 0, 2).reshape(P, C * D),
        "bo": cols(i["L0_attn_bo"]),
        "pe_bd": pe_bd.reshape(P, C, HC * SP1),
        "w1": feat(i["L0_ffn_w1"]).reshape(P, C * FF),
        "w2": feat(i["L0_ffn_w2"]).reshape(P, FJ * D),
        "conv_w": i["L0_ffn_conv_w"].reshape(FJ, P, 3).transpose(1, 0, 2).reshape(P, FJ * 3),
        "conv_b": cols(i["L0_ffn_conv_b"]),
        "wqkv": feat(i["L1_attn_qkv_w"]).reshape(P, C * 3 * HS),
        "bq1": qkv_b[:HS].reshape(HS, 1), "bk1": qkv_b[HS:2 * HS].reshape(HS, 1),
        "bv1": np.broadcast_to(qkv_b[2 * HS:].reshape(1, HS), (S, HS)),
        "pj": i["L1_attn_proj_w"].reshape(D, NREP, HS).transpose(2, 0, 1),
        "pjb": cols(i["L1_attn_proj_b"]),
        "wr": feat(i["L1_ffn_Wr"]).reshape(P, C * E),
        "br": every(i["L1_ffn_br"]),
        "moe_w": np.concatenate([w1e, w2e], axis=2),
        "b1": i["L1_ffn_b1"].reshape(E, FJ, P).transpose(2, 0, 1).reshape(P, E * FJ),
        "b2": every(i["L1_ffn_b2"]),
    }


def kernel(**inputs):
    import numpy as _np
    import concourse.bacc as _bacc
    from concourse.bass_utils import run_bass_kernel_spmd as _run

    nc = _bacc.Bacc("TRN2", target_bir_lowering=False, num_devices=1)
    arrays, args = {}, {}
    for name, v in lay_out({k: _np.asarray(v) for k, v in inputs.items()}).items():
        v = _np.ascontiguousarray(v)
        arrays[f"in_{name}"] = v
        args[name] = nc.dram_tensor(f"in_{name}", v.shape, mybir.dt.from_np(v.dtype), kind="ExternalInput").ap()
    out = nc.dram_tensor("out_rows", (NTOK, D), F32, kind="ExternalOutput").ap()
    program(nc, args, out)
    r = _run(nc, [arrays], core_ids=[0])
    return r.results[0]["out_rows"].reshape(B, S, D)
```

```python
import numpy as np
import concourse.bass as bass
from concourse import mybir
from contextlib import ExitStack

F32 = mybir.dt.float32
BF16 = mybir.dt.bfloat16
I32 = mybir.dt.int32
U32 = mybir.dt.uint32
ALU = mybir.AluOpType
ACT = mybir.ActivationFunctionType
AX = mybir.AxisListType
RED = bass.bass_isa.ReduceOp

P = 128
B, S_IMG, S_TXT = 32, 36, 32
S = S_IMG + S_TXT
NTOK = B * S
D = 256
C = D // P
TILES = NTOK // P
PAIRS = TILES // 2
LN_STEPS = PAIRS + 1
PATCH = 768
KP = PATCH // P
EG = 4
EGN = B // EG * S_IMG
NTXT = B * S_TXT
TAB = S_TXT + 2
H, DH = 8, 32
HC = H // C
DEEP = 4
LAG = 5
SP1 = S + 1
FF = 1024
FJ = FF // P
GB = 4
GN = GB * S
GROUPS = B // GB
HS = 16
NREP = 16
E = 8
MAX_TILES = (NTOK + E * (P - 1)) // P
EPS = 1e-5
MAGIC = 1.5 * 2.0 ** 23
PSUM_W = 512
WE = C * FF + FJ * D
W_EARLY = 4
DIAG_SLOT, RAW_SLOT = 4, 5
INVERT_AT = 4
ROUND_AT = 2
LARGEST_AT = 0
OUT_AT = 7
DOWN_AT = 4
PE_CHUNKS = (0, 2, 3, 5, 6)
PE_BANKS = (2, 3, 2, 3, 2)
UP_BANKS = (0, 1, 6, 7)
AHEAD = 3
TAPS_LAG = 2
SILU_LAG = 2



def wait(e, sem, v):
    if isinstance(v, int) and v <= 0:
        return
    e.wait_ge(sem, v)


def program(nc, a, out):
    ctx = ExitStack()
    with ctx:
        def sb(name, shape, dt=F32):
            return ctx.enter_context(nc.sbuf_tensor(name, shape, dt))

        def sem(name):
            return ctx.enter_context(nc.semaphore(name))

        moe_w = sb("moe_w", [P, E * WE])
        hT_t = sb("hT", [P, C * NTOK])
        yT_t = sb("yT", [P, C * NTOK])
        tm_t = sb("tm", [P, TILES * D])
        hT = hT_t[:, :].rearrange("p (c n) -> p c n", c=C)
        yT = yT_t[:, :].rearrange("p (c n) -> p c n", c=C)
        tm = tm_t[:, :].rearrange("p (t d) -> p t d", t=TILES)

        class Region:

            def __init__(self, tensor, at, end):
                self.tensor, self.at, self.end = tensor, at, end

            def take(self, shape, dt=F32, parts=P):
                n = int(np.prod(shape))
                words = n // 2 if dt == BF16 else n
                v = self.tensor[0:parts, self.at:self.at + words]
                self.at += words
                assert self.at <= self.end, (self.at, self.end)
                if dt != F32:
                    v = v.bitcast(dt)
                if len(shape) == 2:
                    v = v.rearrange("p (a b) -> p a b", a=shape[0])
                if len(shape) == 3:
                    v = v.rearrange("p (a b c) -> p a b c", a=shape[0], b=shape[1])
                return v

        def last_experts():
            return Region(moe_w, (E - 2) * WE, E * WE)

        ident = sb("ident", [P, P])
        identb = sb("identb", [P, P], BF16)
        onesf = sb("onesf", [P, P])
        neg_half = sb("neg_half", [P, TILES])
        pid = sb("pid", [P, 1])
        gamma = sb("gamma", [P, C])
        beta = sb("beta", [P, C])
        bqu = sb("bqu", [P, C])
        bqv = sb("bqv", [P, C])
        bk0 = sb("bk0", [P, 1])
        bv0 = sb("bv0", [P, 1])
        bo0 = sb("bo0", [P, C])
        hmask = sb("hmask", [P, HC])
        bproj = sb("bproj", [P, C])
        wq_bd = sb("wq_bd", [P, P])
        wk_bd = sb("wk_bd", [P, P])
        wv_bd = sb("wv_bd", [P, P])
        wo = sb("wo", [P, C * D])
        wi = sb("wi", [P, (C * FF + FJ * D) // 2])
        w1i = wi[:, 0:C * FF // 2].bitcast(BF16)
        w2i = wi[:, C * FF // 2:].bitcast(BF16)
        convw = sb("convw", [P, FJ * 3])
        convb = sb("convb", [P, FJ])
        w1m = sb("w1m", [P, 2])
        wsum = sb("wsum", [P, 4])

        r = last_experts()
        patches = r.take([EG, KP, EGN])
        r = Region(tm_t, 0, TILES * D)
        wproj = r.take([KP, D])
        tab = r.take([D], parts=TAB)
        posb = r.take([C, S_IMG])
        sepv = r.take([NTXT], parts=TAB)
        padv = r.take([NTXT], parts=TAB)
        r = Region(yT_t, 0, C * NTOK)
        tok_i = r.take([NTXT], I32, TAB)
        tokf = r.take([NTXT], parts=TAB)
        gidx = r.take([NTXT], parts=TAB)
        base = r.take([NTXT], parts=TAB)
        r = Region(moe_w, RAW_SLOT * WE, (RAW_SLOT + 1) * WE)
        w1raw = r.take([C * FF])
        w2raw = r.take([FJ * D])
        runs = moe_w[0:TAB, (E - 2) * WE + EG * KP * EGN:E * WE][:, 0:NTXT]
        runp = wi[0:TAB, 0:NTXT]

        stage = [sb(f"stage{i}", [P, 2 * D]) for i in range(2)]
        z = [sb(f"z{i}", [P, 2 * D]) for i in range(2)]
        zb = [z[i][:, 0:D].bitcast(BF16) for i in range(2)]
        bn = sb("bn", [P, TILES * 6])
        bnv = bn[:, :].rearrange("p (t k) -> p t k", k=6)
        bsum_t = sb("bsum", [P, 4 * TILES])
        bsum = bsum_t[:, :].rearrange("p (k t) -> p k t", k=4)
        mean = sb("mean", [P, TILES])
        var = sb("var", [P, TILES])
        ve = sb("ve", [P, TILES])
        rstd = sb("rstd", [P, TILES])
        amax = sb("amax", [P, TILES])
        qstep = sb("qstep", [P, TILES])
        qinv = sb("qinv", [P, TILES])

        r = Region(tm_t, 0, TILES * D)
        kbd = [r.take([C, HC * S]) for _ in range(DEEP)]
        qu = [r.take([C, S]) for _ in range(DEEP)]
        yst = [r.take([C, S]) for _ in range(DEEP)]
        qv = r.take([C, S])
        ctxn = r.take([H, DH], parts=S)
        ctxT = r.take([C, S])
        r = last_experts()
        pbd = r.take([C, HC * SP1])
        posp = [r.take([C, HC * SP1], parts=S) for _ in range(2)]
        poss = [r.take([C, HC * S], parts=S) for _ in range(2)]
        sx = [r.take([H, S], parts=S) for _ in range(2)]
        pr = [r.take([H, S], parts=S) for _ in range(2)]
        prT = r.take([H, S], parts=S)
        vaug = [r.take([H, DH + 1], parts=S) for _ in range(2)]
        rz = r.take([H], parts=S)
        mx = [r.take([H], parts=S) for _ in range(2)]
        pe_bd = Region(yT_t, 0, C * NTOK).take([C, HC * SP1])
        wp_bd = z[0][:, 0:P]

        r = last_experts()
        sv = [r.take([FJ, GN]) for _ in range(2)]
        si = r.take([FJ, GN], BF16)
        uu = [r.take([GB, S + 2]) for _ in range(len(UP_BANKS))]
        tt = {j: r.take([GB, S]) for j in range(FJ) if j not in PE_CHUNKS}
        am = [r.take([GN]) for _ in range(2)]
        diag = Region(moe_w, DIAG_SLOT * WE, (DIAG_SLOT + 1) * WE).take([len(PE_CHUNKS), 3, P])
        r = Region(tm_t, 0, TILES * D)
        mr = [r.take([GN]) for _ in range(2)]
        mi = [r.take([GN]) for _ in range(2)]
        fo = [r.take([C, GN]) for _ in range(2)]
        ziT = yT_t[:, 0:NTOK].bitcast(BF16).rearrange("p (c n) -> p c n", c=C)
        rsb = yT_t[:, NTOK:2 * NTOK]

        wqkv = sb("wqkv", [P, C * 3 * HS])
        wqkv_v = wqkv[:, :].rearrange("p (c n) -> p c n", c=C)
        bq1 = sb("bq1", [HS, 1])
        bk1 = sb("bk1", [HS, 1])
        bv1 = sb("bv1", [S, HS])
        pj = sb("pj", [HS, D])
        pjb = sb("pjb", [P, C])
        cmask = sb("cmask", [S, S])
        pj_raw = carve_pj = Region(moe_w, RAW_SLOT * WE, (RAW_SLOT + 1) * WE).take([D, NREP], parts=HS)
        r = Region(tm_t, 0, TILES * D)
        y7 = [r.take([C, GN]) for _ in range(2)]
        q7 = [r.take([GN], parts=HS) for _ in range(2)]
        k7 = [r.take([GN], parts=HS) for _ in range(2)]
        v7 = [r.take([GB, HS], parts=S) for _ in range(2)]
        w7 = [r.take([GB, S], parts=S) for _ in range(2)]
        o7 = [r.take([GN], parts=HS) for _ in range(2)]

        wr = sb("wr", [P, C * E])
        br = sb("br", [P, E])
        lg = sb("lg", [P, TILES * E])
        lgv = lg[:, :].rearrange("p (t e) -> p t e", e=E)
        z3 = hT_t[:, :].rearrange("p (t d) -> p t d", t=TILES)
        r = Region(yT_t, 0, C * NTOK)
        zTs = [r.take([C, 2 * P]) for _ in range(2)]
        oh = r.take([TILES, E])
        ohb = r.take([TILES, E], BF16)
        rt = r.take([TILES, E])
        rcol = r.take([TILES])
        rev = r.take([E])
        thr = r.take([E, TILES])
        cmp_ = r.take([E, TILES])
        cntp = r.take([E])
        cntb = r.take([E], BF16)
        nt = r.take([E])
        tend = r.take([E])
        tst = r.take([E])
        it24 = r.take([MAX_TILES, E])
        te = r.take([MAX_TILES])
        triu = r.take([P], BF16)
        onesb = r.take([P], BF16)
        posu = sb("posu", [P, TILES], U32)
        tei = sb("tei", [1, MAX_TILES], I32)
        zeros = Region(yT_t, 0, C * NTOK)
        b2 = wi
        b1 = sb("b1", [P, E * FJ])
        r = Region(yT_t, 0, C * NTOK)
        xt = [r.take([D]) for _ in range(2)]
        xT = [r.take([D]) for _ in range(2)]
        h1 = r.take([FF])
        hTm = r.take([FJ, P])
        ysb = [r.take([D]) for _ in range(2)]
        b1s = [r.take([FJ]) for _ in range(2)]
        GATH = 6
        fg = z3

        ps = ctx.enter_context(nc.psum_tensor("ps", [P, 8, PSUM_W], F32))

        scr = [nc.dram_tensor(f"shift{i}", [H, S * SP1], F32, kind="Internal").ap() for i in range(2)]
        xs = nc.dram_tensor("sorted_rows", [MAX_TILES * P, D], F32, kind="Internal").ap()
        ys = nc.dram_tensor("sorted_out", [MAX_TILES * P, D], F32, kind="Internal").ap()

        (pool_past, sync_past, ld_emb, ld_txt, ld_ln, ld_at, ld_w12, ld_ff, ld_a1, ld_pj, ld_rt, ld_b2, ld_pe, ld_moe, ld_moe5, ld_moe467,
         consts, iotas, txt_step, posb_ok, emb_mm, emb_out, txt_mm, txt_out,
         ln_staged, ln_tokps, ln_tok, ln_bn, ln_ba, ln_mv, ln_ve, ln_rstd, ln_z, ln_zT, ln_out,
         q_z, q_amax, q_step, q_inv, q_mul, q_diag, q_bps,
         wq_abs, wq_sum, wq_mean, wq_inv, wq_a, wq_b, wq_done, pj_done) = [sem(n) for n in (
             "pool_past sync_past ld_emb ld_txt ld_ln ld_at ld_w12 ld_ff ld_a1 ld_pj ld_rt ld_b2 ld_pe ld_moe ld_moe5 ld_moe467 "
             "consts iotas txt_step posb_ok emb_mm emb_out txt_mm txt_out "
             "ln_staged ln_tokps ln_tok ln_bn ln_ba ln_mv ln_ve ln_rstd ln_z ln_zT ln_out "
             "q_z q_amax q_step q_inv q_mul q_diag q_bps "
             "wq_abs wq_sum wq_mean wq_inv wq_a wq_b wq_done pj_done").split()]
        (at_bias, at_pbps, at_pbd, at_y, at_qkps, at_qkv, at_vps, at_v, at_posps, at_posp, at_cps, at_s, at_mx,
         at_sub, at_p, at_pTps, at_pT, at_ctxps, at_rz, at_ctx, at_ctxTps, at_ctxT, at_wops, at_res, at_ones) = [
             sem(n) for n in (
                 "at_bias at_pbps at_pbd at_y at_qkps at_qkv at_vps at_v at_posps at_posp at_cps at_s at_mx "
                 "at_sub at_p at_pTps at_pT at_ctxps at_rz at_ctx at_ctxTps at_ctxT at_wops at_res at_ones").split()]
        (ff_pad, ff_diag, ff_cv, ff_mm, ff_u, ff_t1, ff_t2, ff_t3, ff_s, ff_am, ff_red, ff_mr, ff_mi, ff_mul, ff_si, ff_ops,
         ff_fo, ff_fo_free, ff_res) = [sem(n) for n in (
             "ff_pad ff_diag ff_cv ff_mm ff_u ff_t1 ff_t2 ff_t3 ff_s ff_am ff_red ff_mr ff_mi ff_mul ff_si ff_ops "
             "ff_fo ff_fo_free ff_res").split()]
        (a1_y, a1_qps, a1_kps, a1_q, a1_k, a1_vps, a1_v, a1_wps, a1_w, a1_ops, a1_o, a1_pps, a1_res) = [
            sem(n) for n in (
                "a1_y a1_qps a1_kps a1_q a1_k a1_vps a1_v a1_wps a1_w a1_ops a1_o a1_pps a1_res").split()]
        (z_kept, rt_c, rt_lgps, rt_lg, rt_step, rt_cntps, rt_pos, rt_te, rt_pps, rt_cb, sc_zero, sc_rows,
         mo_b1, mo_xTps, mo_xT, mo_h1ps, mo_h1a, mo_h1b, mo_hTps, mo_hTa, mo_hTb, mo_yps, mo_y,
         fin_add, fin_out, st_zero) = [
            sem(n) for n in (
                "z_kept rt_c rt_lgps rt_lg rt_step rt_cntps rt_pos rt_te rt_pps rt_cb sc_zero sc_rows "
                "mo_b1 mo_xTps mo_xT mo_h1ps mo_h1a mo_h1b mo_hTps mo_hTa mo_hTb mo_yps mo_y "
                "fin_add fin_out st_zero").split()]
        ld_patch = [sem(f"ld_patch{i}") for i in range(EG)]
        at_out = [sem(f"at_out{i}") for i in range(2)]
        at_in = [sem(f"at_in{i}") for i in range(2)]
        mo_xin = [sem(f"mo_xin{i}") for i in range(2)]
        mo_yout = [sem(f"mo_yout{i}") for i in range(2)]
        fin_in = [sem(f"fin_in{i}") for i in range(GATH)]

        block = ctx.enter_context(nc.Block())

        def tokps(par):
            return ps[:, par, :]

        def zTps(par):
            return ps[:, 2 + par, :]

        def pairs_then_last(e, step, last):
            step(0, 0, 2)
            step(1, 1, 2)
            with e.Fori(1, PAIRS // 2) as i:
                step(2 * i, 0, 2)
                step(2 * i + 1, 1, 2)
            last(PAIRS, 0, 1)

        def pairs_then_last_staged(e, first, second):
            first(0, 0, 2)
            first(1, 1, 2)
            second(0, 0, 2)
            first(2, 0, 2)
            second(1, 1, 2)
            first(3, 1, 2)
            second(2, 0, 2)
            with e.Fori(2, PAIRS // 2) as i:
                first(2 * i, 0, 2)
                second(2 * i - 1, 1, 2)
                first(2 * i + 1, 1, 2)
                second(2 * i, 0, 2)
            first(PAIRS, 0, 1)
            second(PAIRS - 1, 1, 2)
            second(PAIRS, 0, 1)

        def on_pe(g, j):
            return g * len(PE_CHUNKS) + sum(c <= j for c in PE_CHUNKS)

        def on_dve(g, j):
            return g * (FJ - len(PE_CHUNKS)) + sum(c <= j for c in range(FJ) if c not in PE_CHUNKS)

        def batches(e, part, order):
            def step(i, q):
                for name, lag in order:
                    b, turn = DEEP * i + q - lag, (DEEP // 2) * i + (q - lag) // 2
                    if not isinstance(b, int) or 0 <= b < B:
                        part[name](b, (q - lag) % DEEP, turn)
            for s in range(2 * DEEP):
                step(s // DEEP, s % DEEP)
            with e.Fori(2, B // DEEP) as i:
                for q in range(DEEP):
                    step(i, q)
            for s in range(B, B + LAG):
                step(s // DEEP, s % DEEP)

        @block.sync
        def _(sp):
            sp.dma_start(wproj, a["w_proj"]).then_inc(ld_emb, 16)
            for g in range(EG):
                sp.dma_start(patches[:, g], a["patches"][:, g]).then_inc(ld_patch[g], 16)
                if g == 0:
                    sp.dma_start(posb, a["pos"]).then_inc(ld_emb, 16)
                    sp.dma_start(bproj[:, :], a["b_proj"]).then_inc(ld_emb, 16)
            sp.dma_start(w1raw, a["w1"]).then_inc(ld_w12, 16)
            sp.dma_start(w2raw, a["w2"]).then_inc(ld_w12, 16)
            for t, n in ((gamma, "gamma"), (beta, "beta")):
                sp.dma_start(t[:, :], a[n]).then_inc(ld_ln, 16)
            for t, n in ((bqu, "u_bias"), (bqv, "v_bias"), (wsum[:, 0:1], "bq"), (bk0, "bk"), (bv0, "bv"),
                         (bo0, "bo"), (wq_bd, "wq"), (wk_bd, "wk"), (wv_bd, "wv"), (wo, "wo")):
                sp.dma_start(t[:, :], a[n]).then_inc(ld_at, 16)
            for t, n in ((convw, "conv_w"), (convb, "conv_b")):
                sp.dma_start(t[:, :], a[n]).then_inc(ld_ff, 16)
            for t, n in ((wqkv, "wqkv"), (bq1, "bq1"), (bk1, "bk1"), (bv1, "bv1"), (pjb, "pjb")):
                sp.dma_start(t[:, :], a[n]).then_inc(ld_a1, 16)
            for t, n in ((wr, "wr"), (br, "br"), (b1, "b1")):
                sp.dma_start(t[:, :], a[n]).then_inc(ld_rt, 16)
            for e in range(W_EARLY):
                sp.dma_start(moe_w[:, e * WE:(e + 1) * WE], a["moe_w"][:, e]).then_inc(ld_moe, 16)
            sp.wait_ge(wq_done, 2)
            sp.dma_start(pj_raw, a["pj"]).then_inc(ld_pj, 16)

            def scores_back(b, q, turn):
                par = q % 2
                wait(sp, at_s, b - 1)
                sp.sem_inc(sync_past, 1)
                sp.wait_ge(at_out[par], 16 * turn + 16)
                sp.dma_start(poss[par].rearrange("p a (h c) -> p (a h) c", c=S),
                             scr[par][:, S:S + S * S].rearrange("h (i c) -> i h c", c=S)).then_inc(at_in[par], 16)

            def scores_out(b, q, turn):
                par = q % 2
                wait(sp, at_in[par], 16 * turn)
                sp.sem_inc(sync_past, 1)
                sp.wait_ge(at_posp, b + 1)
                sp.dma_start(scr[par].rearrange("h (i c) -> i h c", c=SP1),
                             posp[par].rearrange("p a (h c) -> p (a h) c", c=SP1)).then_inc(at_out[par], 16)

            batches(sp, {"back": scores_back, "out": scores_out}, [("back", 2), ("out", 1)])
            sp.wait_ge(pj_done, 1)
            sp.dma_start(moe_w[:, RAW_SLOT * WE:(RAW_SLOT + 1) * WE], a["moe_w"][:, RAW_SLOT]).then_inc(ld_moe5, 16)
            sp.wait_ge(ff_res, GROUPS)
            for e in (DIAG_SLOT, *range(RAW_SLOT + 1, E)):
                sp.dma_start(moe_w[:, e * WE:(e + 1) * WE], a["moe_w"][:, e]).then_inc(ld_moe467, 16)

            sp.dma_start(b2[:, :], a["b2"]).then_inc(ld_b2, 16)
            sp.wait_ge(st_zero, 1)
            for n in range(3):
                k = MAX_TILES // 3 * P
                sp.dma_start(xs[n * k:(n + 1) * k, :].rearrange("(p t) d -> p (t d)", p=P),
                             tm_t[:, 0:k // P * D]).then_inc(sc_zero, 16)

            def rows_in(i, par):
                wait(sp, mo_xTps, i - 1)
                sp.dma_start(xt[par], xs[bass.ds(i * P, P), :]).then_inc(mo_xin[par], 16)

            def rows_out(i, par):
                sp.wait_ge(mo_y, i + 1)
                sp.dma_start(ys[bass.ds(i * P, P), :], ysb[par]).then_inc(mo_yout[par], 16)

            sp.wait_ge(sc_rows, 16 * TILES)
            rows_in(0, 0)
            rows_in(1, 1)
            with sp.Fori(0, MAX_TILES // 2 - 1) as i:
                for par in range(2):
                    rows_in(2 * i + 2 + par, par)
                    rows_out(2 * i + par, par)
            rows_out(MAX_TILES - 2, 0)
            rows_out(MAX_TILES - 1, 1)

            for t in range(TILES):
                sp.wait_ge(fin_add, t + 1)
                sp.dma_start(out[t * P:(t + 1) * P, :], tm[:, t]).then_inc(fin_out, 16)
            sp.wait_ge(fin_out, 16 * TILES)

        @block.gpsimd
        def _(gp):
            gp.iota(gidx, [[1, NTXT]], base=0, channel_multiplier=0,
                    allow_small_or_imprecise_dtypes=True).then_inc(iotas, 1)
            gp.iota(base.rearrange("p (b s) -> p b s", b=B), [[S_TXT, B], [0, S_TXT]], base=0,
                    channel_multiplier=0, allow_small_or_imprecise_dtypes=True).then_inc(iotas, 1)
            gp.iota(pid[:, :], [[0, 1]], base=0, channel_multiplier=1,
                    allow_small_or_imprecise_dtypes=True).then_inc(iotas, 1)
            gp.memset(ident[:, :], 0.0).then_inc(consts, 1)
            gp.memset(onesf[:, :], 1.0).then_inc(consts, 1)
            gp.memset(neg_half[:, :], -0.5).then_inc(consts, 1)
            gp.memset(hmask[:, :], 1.0).then_inc(consts, 1)
            gp.memset(cmask[:, :], 1.0).then_inc(consts, 1)
            gp.wait_ge(consts, 5)
            gp.affine_select(out=ident[:, :], in_=ident[:, :], compare_op=ALU.not_equal, fill=1.0,
                             base=0, pattern=[[-1, P]], channel_multiplier=1).then_inc(consts, 1)
            gp.affine_select(out=cmask[:, :], in_=cmask[:, :], compare_op=ALU.is_ge, fill=0.0,
                             base=0, pattern=[[1, S]], channel_multiplier=-1).then_inc(consts, 1)
            gp.affine_select(out=hmask[:, :], in_=hmask[:, :], compare_op=ALU.is_ge, fill=0.0,
                             base=0, pattern=[[-DH, HC]], channel_multiplier=1).then_inc(consts, 1)
            gp.wait_ge(consts, 8)
            gp.affine_select(out=hmask[:, :], in_=hmask[:, :], compare_op=ALU.is_ge, fill=0.0,
                             base=DH - 1, pattern=[[DH, HC]], channel_multiplier=-1).then_inc(consts, 1)
            gp.tensor_copy(identb[:, :], ident[:, :]).then_inc(consts, 1)

            for n in range(2):
                gp.wait_ge(wq_abs, n + 1)
                gp.partition_all_reduce(wsum[:, 2 + n:3 + n], w1m[:, n:n + 1], P, RED.add).then_inc(wq_sum, 1)

            def past(gp):
                gp.sem_inc(pool_past, 1)

            def ln_rstd_all(k):
                gp.wait_ge(ln_mv, k + 1)
                if k == 0:
                    gp.tensor_scalar(ve[:, :], var[:, :], 1.0 + EPS, EPS * EPS,
                                     ALU.mult, ALU.add).then_inc(ln_ve, 1)
                else:
                    gp.tensor_scalar(ve[:, :], var[:, :], EPS, None, ALU.add).then_inc(ln_ve, 1)
                gp.wait_ge(ln_ve, k + 1)
                gp.tensor_tensor(rstd[:, :], ve[:, :], neg_half[:, :], ALU.pow).then_inc(ln_rstd, 1)

            ln_rstd_all(0)

            for par in range(2):
                gp.memset(vaug[par][:, :, DH:DH + 1], 1.0).then_inc(at_ones, 1)

            def y_slice(b, q, turn):
                wait(gp, at_vps, b - 3)
                gp.tensor_copy(yst[q], yT[:, :, bass.ds(b * S, S)]).then_inc(at_y, 1)

            def subtract_max(b, q, turn):
                gp.wait_ge(at_mx, b + 1)
                gp.tensor_tensor(sx[q % 2], sx[q % 2], mx[q % 2].unsqueeze(2).to_broadcast([S, H, S]),
                                 ALU.subtract).then_inc(at_sub, 1)

            gp.wait_ge(ln_out, LN_STEPS)
            batches(gp, {"y": y_slice, "sub": subtract_max}, [("y", 0), ("sub", 3)])

            gp.wait_ge(ld_ff, 32)
            for n, j in enumerate(PE_CHUNKS):
                for k in range(3):
                    ins = gp.tensor_scalar(diag[:, n, k], ident[:, :], convw[:, 3 * j + k:3 * j + k + 1], None,
                                           ALU.mult)
            ins.then_inc(ff_diag, 1)

            ln_rstd_all(1)

            for u in uu:
                gp.memset(u[:, :, 0:1], 0.0)
                gp.memset(u[:, :, S + 1:S + 2], 0.0).then_inc(ff_pad, 1)

            def quantise(g, par):
                gp.wait_ge(ff_am, g + 1)
                wait(gp, ff_fo, g - 1)
                past(gp)
                gp.partition_all_reduce(mr[par], am[par], P, RED.absmax).then_inc(ff_red, 1)
                gp.wait_ge(ff_red, g + 1)
                past(gp)
                gp.tensor_scalar(mr[par], mr[par], EPS, 1.0 / 127.0, ALU.max, ALU.mult).then_inc(ff_mr, 1)
                gp.wait_ge(ff_mi, g + 1)
                gp.tensor_tensor(sv[par], sv[par], mi[par].unsqueeze(1).to_broadcast([P, FJ, GN]),
                                 ALU.mult).then_inc(ff_mul, 1)

            def ff_add(g, par):
                gp.wait_ge(ff_fo, g + 1)
                gp.tensor_tensor(hT[:, :, bass.ds(g * GN, GN)], hT[:, :, bass.ds(g * GN, GN)], fo[par],
                                 ALU.add).then_inc(ff_res, 1)
                gp.wait_ge(ff_res, g + 1)
                gp.sem_inc(ff_fo_free, 1)

            gp.sem_inc(ff_fo_free, 2)
            quantise(0, 0)

            def two_groups(i):
                quantise(2 * i + 1, 1)
                ff_add(2 * i, 0)
                quantise(2 * i + 2, 0)
                ff_add(2 * i + 1, 1)

            two_groups(0)
            with gp.Fori(1, GROUPS // 2 - 1) as i:
                two_groups(i)
            quantise(GROUPS - 1, 1)
            ff_add(GROUPS - 2, 0)
            ff_add(GROUPS - 1, 1)

            ln_rstd_all(2)

            def y_group(g, par):
                wait(gp, a1_vps, g - 1)
                gp.tensor_copy(y7[par], yT[:, :, bass.ds(g * GN, GN)]).then_inc(a1_y, 1)

            gp.wait_ge(ln_out, 3 * LN_STEPS)
            y_group(0, 0)
            y_group(1, 1)
            with gp.Fori(1, GROUPS // 2) as i:
                y_group(2 * i, 0)
                y_group(2 * i + 1, 1)
            gp.wait_ge(a1_vps, GROUPS)
            gp.wait_ge(a1_res, GROUPS)
            gp.memset(tm_t[:, 0:MAX_TILES // 3 * D], 0.0).then_inc(st_zero, 1)

            ln_rstd_all(3)

            def keep_z(u, par, n):
                gp.wait_ge(ln_z, 3 * LN_STEPS + u + 1)
                past(gp)
                gp.tensor_copy(hT_t[:, bass.ds(u * 2 * D, n * D)], z[par][:, 0:n * D]).then_inc(z_kept, 1)

            pairs_then_last(gp, keep_z, keep_z)
            gp.wait_ge(rt_lg, LN_STEPS)
            gp.iota(rev, [[-1, E]], base=E, channel_multiplier=0,
                    allow_small_or_imprecise_dtypes=True).then_inc(rt_c, 1)
            gp.iota(thr, [[0, E], [P, TILES]], base=0, channel_multiplier=0,
                    allow_small_or_imprecise_dtypes=True).then_inc(rt_c, 1)
            gp.iota(it24, [[1, MAX_TILES], [0, E]], base=0, channel_multiplier=0,
                    allow_small_or_imprecise_dtypes=True).then_inc(rt_c, 1)
            gp.memset(onesb, 1.0).then_inc(rt_c, 1)
            gp.wait_ge(rt_c, 4)
            gp.affine_select(out=triu, in_=onesb, compare_op=ALU.is_gt, fill=0.0, base=0,
                             pattern=[[1, P]], channel_multiplier=-1).then_inc(rt_c, 1)

            gp.wait_ge(rt_pos, 1)
            gp.wait_ge(z_kept, LN_STEPS)
            gp.wait_ge(sc_zero, 48)
            for t in range(TILES):
                gp.indirect_dma_start(xs, bass.IndirectOffsetOnAxis(ap=posu[:, t:t + 1], axis=0),
                                      z3[:, t], None).then_inc(sc_rows, 16)

            def bias_slice(i, par):
                e = gp.value_load(tei[0:1, bass.ds(i, 1)], min_val=0, max_val=E - 1)
                wait(gp, mo_hTa, i - 1)
                wait(gp, mo_hTb, i - 1)
                past(gp)
                gp.tensor_copy(b1s[par], b1[:, bass.ds(e * FJ, FJ)]).then_inc(mo_b1, 1)

            gp.wait_ge(rt_te, 1)
            bias_slice(0, 0)
            bias_slice(1, 1)
            with gp.Fori(1, MAX_TILES // 2) as i:
                bias_slice(2 * i, 0)
                bias_slice(2 * i + 1, 1)

            gp.wait_ge(sc_rows, 16 * TILES)
            gp.wait_ge(mo_yout[0], 16 * MAX_TILES // 2)
            gp.wait_ge(mo_yout[1], 16 * MAX_TILES // 2)
            for t in range(TILES):
                wait(gp, fin_add, t - GATH + 1)
                gp.indirect_dma_start(fg[:, t], None, ys,
                                      bass.IndirectOffsetOnAxis(ap=posu[:, t:t + 1], axis=0)
                                      ).then_inc(fin_in[t % GATH], 16)

        @block.scalar
        def _(act):
            act.dma_start(tok_i, a["x_txt"]).then_inc(ld_txt, 16)
            act.dma_start(tab, a["table"]).then_inc(ld_emb, 16)
            act.dma_start(wp_bd, a["wp"]).then_inc(ld_pe, 16)
            for m in range(4):
                c, half = m // 2, m % 2
                act.wait_ge(txt_mm, m + 1)
                dst = hT[:, c].rearrange("p (b s) -> p b s", s=S)[:, half * B // 2:(half + 1) * B // 2, S_IMG:S]
                act.activation(dst, ps[:, 4 + m, 0:PSUM_W].rearrange("p (b s) -> p b s", s=S_TXT),
                               ACT.Copy).then_inc(txt_out, 1)
            act.dma_start(pe_bd, a["pe_bd"]).then_inc(ld_pe, 16)
            for c in range(C):
                act.wait_ge(at_pbps, c + 1)
                act.activation(pbd[:, c], ps[:, 4 + c, 0:HC * SP1], ACT.Copy).then_inc(at_pbd, 1)

            def evac_tok(k):
                def step(u, par, n):
                    g = k * LN_STEPS + u
                    act.wait_ge(ln_tokps, g + 1)
                    act.activation(tm_t[:, bass.ds(u * 2 * D, n * D)], tokps(par)[:, 0:n * D],
                                   ACT.Copy).then_inc(ln_tok, 1)
                pairs_then_last(act, step, step)

            def evac_zT(k):
                def step(u, par, n):
                    g = k * LN_STEPS + u
                    act.wait_ge(ln_zT, g + 1)
                    w = n * P
                    if k == 0:
                        for c in range(C):
                            ins = act.activation(yT[:, c, bass.ds(u * 2 * P, w)], zTps(par)[:, c * w:(c + 1) * w],
                                                 ACT.Identity, bias=beta[:, c:c + 1], scale=gamma[:, c:c + 1])
                    elif k == 1:
                        src = zTps(par).bitcast(BF16)[:, 0:C * w].rearrange("p (c n) -> p c n", c=C)
                        act.activation(ziT[:, :, bass.ds(u * 2 * P, w)], src, ACT.Copy)
                        act.wait_ge(q_bps, u + 1)
                        ins = act.activation(rsb[:, bass.ds(u * 2 * P, w)], ps[:, 4 + par, 0:w], ACT.Copy,
                                             scale=w1m[:, 0:1])
                    elif k == 2:
                        src = zTps(par)[:, 0:C * w].rearrange("p (c n) -> p c n", c=C)
                        ins = act.activation(yT[:, :, bass.ds(u * 2 * P, w)], src, ACT.Copy)
                    else:
                        wait(act, rt_lgps, u - 1)
                        src = zTps(par)[:, 0:C * w].rearrange("p (c n) -> p c n", c=C)
                        ins = act.activation(zTs[par][:, :, 0:w], src, ACT.Copy)
                    ins.then_inc(ln_out, 1)
                pairs_then_last(act, step, step)

            act.wait_ge(ld_ln, 32)
            act.wait_ge(emb_out, EG * C)
            evac_tok(0)
            evac_zT(0)

            def exps(b, q, turn):
                act.wait_ge(at_sub, b + 1)
                wait(act, at_pTps, b - 1)
                act.activation(pr[q % 2], sx[q % 2], ACT.Exp, scale=1.0 / D ** 0.5).then_inc(at_p, 1)

            def evac_v(b, q, turn):
                act.wait_ge(at_vps, b + 1)
                wait(act, at_ctxps, b - 1)
                act.activation(vaug[q % 2][:, :, 0:DH], ps[0:S, 1, 0:D].rearrange("p (h d) -> p h d", h=H),
                               ACT.Copy).then_inc(at_v, 1)

            def evac_ctxT(b, q, turn):
                act.wait_ge(at_ctxTps, b + 1)
                wait(act, at_wops, b)
                act.activation(ctxT, ps[:, 0, 0:C * S].rearrange("p (c n) -> p c n", c=C), ACT.Identity,
                               bias=bv0[:, 0:1]).then_inc(at_ctxT, 1)

            def evac_pT(b, q, turn):
                act.wait_ge(at_pTps, b + 1)
                wait(act, at_ctxps, b)
                act.activation(prT.rearrange("p (a h) c -> p a (h c)", a=C), ps[0:S, 6:8, 0:HC * S],
                               ACT.Copy).then_inc(at_pT, 1)

            def evac_pos(b, q, turn):
                act.wait_ge(at_posps, b + 1)
                wait(act, at_out[q % 2], 16 * turn)
                act.activation(posp[q % 2], ps[0:S, 2:4, 0:HC * SP1], ACT.Copy).then_inc(at_posp, 1)

            act.wait_ge(ld_at, 160)
            batches(act, {"exp": exps, "v": evac_v, "ctxT": evac_ctxT, "pT": evac_pT, "pos": evac_pos},
                    [("exp", 4), ("pT", 4), ("v", 4), ("ctxT", LAG), ("pos", 1)])

            evac_tok(1)
            evac_zT(1)

            def tap_mid(g, j):
                act.wait_ge(ff_u, g * FJ + j + 1)
                wait(act, ff_s, (g - 1) * FJ + j + 1)
                act.activation(tt[j], uu[j % 4][:, :, 1:S + 1], ACT.Identity, bias=convb[:, j:j + 1],
                               scale=convw[:, 3 * j + 1:3 * j + 2]).then_inc(ff_t1, 1)

            def silu(g, gpar, j):
                if j == 0:
                    wait(act, ff_si, g - 1)
                dst = sv[gpar]
                if j in PE_CHUNKS:
                    act.wait_ge(ff_cv, on_pe(g, j))
                    src = ps[:, PE_BANKS[PE_CHUNKS.index(j)], 0:GN]
                    act.activation(dst[:, j], src, ACT.Silu, bias=convb[:, j:j + 1]).then_inc(ff_s, 1)
                else:
                    act.wait_ge(ff_t3, on_dve(g, j))
                    act.activation(dst[:, j].rearrange("p (b s) -> p b s", b=GB), tt[j],
                                   ACT.Silu).then_inc(ff_s, 1)

            def ff_group(g, gpar):
                for j in range(FJ + SILU_LAG):
                    if j < FJ and j not in PE_CHUNKS:
                        tap_mid(g, j)
                    if j >= SILU_LAG:
                        silu(g, gpar, j - SILU_LAG)

            act.wait_ge(ld_ff, 32)
            ff_group(0, 0)
            ff_group(1, 1)
            with act.Fori(1, GROUPS // 2) as i:
                ff_group(2 * i, 0)
                ff_group(2 * i + 1, 1)

            evac_tok(2)
            evac_zT(2)

            def evac_qk7(g, par):
                act.wait_ge(a1_qps, g + 1)
                wait(act, a1_wps, g - 1)
                act.activation(q7[par], ps[0:HS, 0, 0:GN], ACT.Identity, bias=bq1[:, 0:1]).then_inc(a1_q, 1)
                act.wait_ge(a1_kps, g + 1)
                act.activation(k7[par], ps[0:HS, 1, 0:GN], ACT.Identity, bias=bk1[:, 0:1]).then_inc(a1_k, 1)

            def evac_o7(g, par):
                act.wait_ge(a1_ops, g + 1)
                act.activation(o7[par], ps[0:HS, 4, 0:GN], ACT.Copy).then_inc(a1_o, 1)

            act.wait_ge(ld_a1, 80)
            evac_qk7(0, 0)
            evac_qk7(1, 1)
            evac_o7(0, 0)
            with act.Fori(1, GROUPS // 2) as i:
                for par in range(2):
                    evac_qk7(2 * i + par, par)
                    evac_o7(2 * i + par - 1, 1 - par)
            evac_o7(GROUPS - 1, 1)

            act.wait_ge(sc_zero, 48)
            evac_tok(3)
            evac_zT(3)

            def evac_x(i, par):
                act.wait_ge(mo_xTps, i + 1)
                wait(act, mo_h1ps, i - 1)
                act.activation(xT[par], ps[:, 6 + par, 0:D], ACT.Copy).then_inc(mo_xT, 1)

            def evac_h(i, par):
                act.wait_ge(mo_h1ps, i + 1)
                wait(act, mo_hTps, i)
                act.activation(h1[:, 0:PSUM_W], ps[:, 0, :], ACT.Copy).then_inc(mo_h1a, 1)

            def relu_a(i, par):
                act.wait_ge(mo_hTps, i + 1)
                act.wait_ge(mo_b1, i + 1)
                for j in range(FJ // 2):
                    ins = act.activation(hTm[:, j], ps[:, 2, j * P:(j + 1) * P], ACT.Relu,
                                         bias=b1s[par][:, j:j + 1])
                ins.then_inc(mo_hTa, 1)

            def expert_step(i, par, more=True):
                if more:
                    evac_x(i + 1, 1 - par)
                evac_h(i, par)
                relu_a(i, par)

            evac_x(0, 0)
            expert_step(0, 0)
            expert_step(1, 1)
            with act.Fori(1, MAX_TILES // 2 - 1) as i:
                expert_step(2 * i, 0)
                expert_step(2 * i + 1, 1)
            expert_step(MAX_TILES - 2, 0)
            expert_step(MAX_TILES - 1, 1, more=False)

        @block.vector
        def _(dve):
            n = [0]

            def step(ins):
                n[0] += 1
                ins.then_inc(txt_step, 1)

            def after_step():
                dve.wait_ge(txt_step, n[0])

            dve.wait_ge(ld_txt, 16)
            dve.wait_ge(iotas, 3)
            step(dve.tensor_copy(tokf, tok_i))
            after_step()
            step(dve.scalar_tensor_tensor(sepv, tokf, 4.0, gidx, ALU.is_equal, ALU.mult))
            step(dve.tensor_scalar(padv, gidx, 1.0, None, ALU.add))
            after_step()
            step(dve.tensor_tensor(sepv, sepv, base, ALU.max))
            step(dve.scalar_tensor_tensor(padv, tokf, 1.0, padv, ALU.is_equal, ALU.mult))
            after_step()
            step(dve.tensor_tensor_scan(runs, sepv, sepv, 0.0, ALU.max, ALU.max))
            step(dve.tensor_tensor_scan(runp, padv, padv, 0.0, ALU.max, ALU.max))
            after_step()
            step(dve.tensor_tensor(runs, gidx, runs, ALU.subtract))
            step(dve.tensor_tensor(runp, runp, base, ALU.is_le))
            after_step()
            step(dve.scalar_tensor_tensor(runs, runs, 1.0, runp, ALU.add, ALU.mult))
            after_step()
            step(dve.tensor_scalar(sepv, runs, 1.0, pid[0:TAB, 0:1], ALU.add, ALU.is_equal))

            dve.wait_ge(ld_emb, 64)
            for c in range(C):
                ins = dve.tensor_scalar(posb[:, c], posb[:, c], bproj[:, c:c + 1], None, ALU.add)
            ins.then_inc(posb_ok, 1)
            dve.wait_ge(posb_ok, 1)
            for g in range(EG):
                for c in range(C):
                    m = g * C + c
                    dve.wait_ge(emb_mm, m + 1)
                    nb = B // EG
                    dst = hT[:, c].rearrange("p (b s) -> p b s", s=S)[:, g * nb:(g + 1) * nb, 0:S_IMG]
                    dve.tensor_tensor(dst, ps[:, m % 4, 0:EGN].rearrange("p (b s) -> p b s", s=S_IMG),
                                      posb[:, c:c + 1, :].to_broadcast([P, nb, S_IMG]),
                                      ALU.add).then_inc(emb_out, 1)

            dve.wait_ge(ld_w12, 32)
            for n_, raw in enumerate((w1raw, w2raw)):
                dve.tensor_reduce(w1m[:, n_:n_ + 1], raw, AX.X, ALU.add,
                                  apply_absolute_value=True).then_inc(wq_abs, 1)
            dve.wait_ge(ld_at, 160)
            dve.tensor_scalar(bqu[:, :], bqu[:, :], wsum[:, 0:1], None, ALU.add)
            dve.tensor_scalar(bqv[:, :], bqv[:, :], wsum[:, 0:1], None, ALU.add).then_inc(at_bias, 1)
            dve.wait_ge(wq_sum, 2)
            dve.tensor_scalar(w1m[:, :], wsum[:, 2:4], 1.0 / (D * FF), EPS, ALU.mult, ALU.max).then_inc(wq_mean, 1)
            dve.wait_ge(wq_mean, 1)
            dve.wait_ge(at_bias, 1)
            dve.reciprocal(wsum[:, 0:2], w1m[:, :]).then_inc(wq_inv, 1)
            dve.wait_ge(wq_inv, 1)
            for n_, raw in enumerate((w1raw, w2raw)):
                dve.tensor_scalar(raw, raw, wsum[:, n_:n_ + 1], MAGIC, ALU.mult, ALU.add).then_inc(wq_a, 1)
            for n_, raw in enumerate((w1raw, w2raw)):
                dve.wait_ge(wq_a, n_ + 1)
                dve.tensor_scalar(raw, raw, -MAGIC, -1.0, ALU.add, ALU.max).then_inc(wq_b, 1)
            for n_, (raw, wi_n) in enumerate(((w1raw, w1i), (w2raw, w2i))):
                dve.wait_ge(wq_b, n_ + 1)
                dve.tensor_scalar(wi_n, raw, 1.0, None, ALU.min).then_inc(wq_done, 1)

            def gather_stats(k):
                def stage_in(u, par, n):
                    g = k * LN_STEPS + u
                    wait(dve, ln_tokps, g - 1)
                    dve.tensor_copy(stage[par][:, 0:n * D].rearrange("p (c n) -> p c n", c=C),
                                    hT[:, :, bass.ds(u * 2 * P, n * P)]).then_inc(ln_staged, 1)

                def stats(u, par, n):
                    g = k * LN_STEPS + u
                    dve.wait_ge(ln_tok, g + 1)
                    for m in range(n):
                        ins = dve.bn_stats(bn[:, bass.ds((2 * u + m) * 6, 6)],
                                           tm_t[:, bass.ds((2 * u + m) * D, D)])
                    ins.then_inc(ln_bn, 1)

                pairs_then_last_staged(dve, stage_in, stats)
                dve.wait_ge(ln_bn, (k + 1) * LN_STEPS)
                dve.tensor_tensor(bsum[:, 0], bnv[:, :, 2], bnv[:, :, 5], ALU.add)
                dve.tensor_tensor(bsum[:, 1], bnv[:, :, 1], bnv[:, :, 4], ALU.subtract)
                dve.tensor_tensor(bsum[:, 2], bnv[:, :, 1], bnv[:, :, 4], ALU.add).then_inc(ln_ba, 1)
                dve.wait_ge(ln_ba, 2 * k + 1)
                dve.scalar_tensor_tensor(bsum[:, 3], bsum[:, 1], 0.25, bsum[:, 1], ALU.mult, ALU.mult)
                dve.tensor_scalar(mean[:, :], bsum[:, 2], 0.5, None, ALU.mult).then_inc(ln_ba, 1)
                dve.wait_ge(ln_ba, 2 * k + 2)
                dve.scalar_tensor_tensor(var[:, :], bsum[:, 0], 1.0 / D, bsum[:, 3], ALU.mult,
                                         ALU.add).then_inc(ln_mv, 1)

            def normalise(k):
                def step(u, par, n):
                    g = k * LN_STEPS + u
                    wait(dve, ln_zT, g - 1)
                    if k == 3:
                        wait(dve, z_kept, u - 1)
                    for m in range(n):
                        t = 2 * u + m
                        dst = z[par][:, m * D:(m + 1) * D]
                        ins = dve.tensor_scalar(dst, tm_t[:, bass.ds(t * D, D)], mean[:, bass.ds(t, 1)],
                                                rstd[:, bass.ds(t, 1)], ALU.subtract, ALU.mult)
                    ins.then_inc(ln_z, 1)
                dve.wait_ge(ln_rstd, k + 1)
                pairs_then_last(dve, step, step)

            dve.wait_ge(txt_out, 4)
            dve.wait_ge(emb_out, EG * C)
            gather_stats(0)
            normalise(0)

            def norm_ctx(b, q, turn):
                dve.wait_ge(at_ctxps, b + 1)
                wait(dve, at_ctxTps, b)
                c_ps = ps[0:S, 1, 0:H * (DH + 1)].rearrange("p (h d) -> p h d", h=H)
                dve.reciprocal(rz, c_ps[:, :, DH]).then_inc(at_rz, 1)
                dve.wait_ge(at_rz, b + 1)
                dve.tensor_tensor(ctxn, c_ps[:, :, 0:DH], rz.unsqueeze(2).to_broadcast([S, H, DH]),
                                  ALU.mult).then_inc(at_ctx, 1)

            def evac_qk(b, q, turn):
                dve.wait_ge(at_qkps, b + 1)
                wait(dve, at_cps, b - 3)
                wait(dve, at_posps, b)
                q_ps = ps[:, 0, 0:C * S].rearrange("p (c n) -> p c n", c=C)
                dve.tensor_tensor(qv, q_ps, bqv[:, :].unsqueeze(2).to_broadcast([P, C, S]), ALU.add)
                dve.tensor_tensor(qu[q], q_ps, bqu[:, :].unsqueeze(2).to_broadcast([P, C, S]), ALU.add)
                for c in range(C):
                    k_ps = ps[:, 0, (C + c) * S:(C + c + 1) * S]
                    ins = dve.scalar_tensor_tensor(
                        kbd[q][:, c].rearrange("p (h n) -> p h n", h=HC),
                        k_ps.unsqueeze(1).to_broadcast([P, HC, S]), bk0[:, 0:1],
                        hmask[:, :].unsqueeze(2).to_broadcast([P, HC, S]), ALU.add, ALU.mult)
                ins.then_inc(at_qkv, 1)

            def add_scores(b, q, turn):
                par = q % 2
                dve.wait_ge(at_cps, b + 1)
                dve.wait_ge(at_in[par], 16 * turn + 16)
                wait(dve, at_p, b - 1)
                dve.tensor_tensor(sx[par].rearrange("p (a h) c -> p a (h c)", a=C), ps[0:S, 4:6, 0:HC * S],
                                  poss[par], ALU.add).then_inc(at_s, 1)
                dve.wait_ge(at_s, b + 1)
                dve.tensor_reduce(mx[par], sx[par], AX.X, ALU.max).then_inc(at_mx, 1)

            def add_res(b, q, turn):
                dve.wait_ge(at_wops, b + 1)
                for c in range(C):
                    dst = hT[:, c, bass.ds(b * S, S)]
                    ins = dve.scalar_tensor_tensor(dst, ps[:, 0, (C + c) * S:(C + c + 1) * S], bo0[:, c:c + 1],
                                                   dst, ALU.add, ALU.add)
                ins.then_inc(at_res, 1)

            dve.wait_ge(consts, 10)
            batches(dve, {"norm": norm_ctx, "qk": evac_qk, "add": add_scores, "res": add_res},
                    [("norm", LAG), ("qk", 1), ("add", 3), ("res", LAG)])

            dve.wait_ge(at_res, B)
            gather_stats(1)
            dve.wait_ge(ln_rstd, 2)
            with dve.Fori(0, TILES) as t:
                x = tm_t[:, bass.ds(t * D, D)]
                dve.tensor_scalar(x, x, mean[:, bass.ds(t, 1)], rstd[:, bass.ds(t, 1)],
                                  ALU.subtract, ALU.mult).then_inc(q_z, 1)
            dve.wait_ge(q_z, TILES)
            dve.tensor_reduce(amax[:, :], tm, AX.X, ALU.max, apply_absolute_value=True).then_inc(q_amax, 1)
            dve.wait_ge(q_amax, 1)
            dve.tensor_scalar(qstep[:, :], amax[:, :], EPS, 1.0 / 127.0, ALU.max, ALU.mult).then_inc(q_step, 1)
            dve.wait_ge(q_step, 1)
            dve.reciprocal(qinv[:, :], qstep[:, :]).then_inc(q_inv, 1)
            dve.wait_ge(q_inv, 1)

            def quant_step(u, par, n):
                g = LN_STEPS + u
                for m in range(n):
                    t = 2 * u + m
                    x = tm_t[:, bass.ds(t * D, D)]
                    ins = dve.tensor_scalar(x, x, qinv[:, bass.ds(t, 1)], MAGIC, ALU.mult, ALU.add)
                ins.then_inc(q_mul, 1)
                wait(dve, ln_zT, g - 1)
                wait(dve, q_bps, u - 1)
                for m in range(n):
                    ins = dve.tensor_scalar(stage[par][:, m * P:(m + 1) * P], ident[:, :],
                                            qstep[:, bass.ds(2 * u + m, 1)], None, ALU.mult)
                ins.then_inc(q_diag, 1)
                dve.wait_ge(q_mul, u + 1)
                dve.tensor_scalar(zb[par][:, 0:n * D], tm_t[:, bass.ds(u * 2 * D, n * D)], -MAGIC, None,
                                  ALU.add).then_inc(ln_z, 1)

            dve.wait_ge(ln_tokps, 2 * LN_STEPS)
            pairs_then_last(dve, quant_step, quant_step)

            def dequant(g, j):
                dve.wait_ge(ff_mm, g * FJ + j + 1)
                bg, bj = (g, j - 4) if j >= 4 else (g - 1, j - 4 + FJ)
                if bj in PE_CHUNKS:
                    wait(dve, ff_cv, on_pe(bg, bj))
                else:
                    wait(dve, ff_t3, on_dve(bg, bj))
                dve.tensor_tensor(uu[j % 4][:, :, 1:S + 1], ps[:, UP_BANKS[j % 4], 0:GN].rearrange("p (b s) -> p b s", b=GB),
                                  rsb[:, bass.ds(g * GN, GN)].rearrange("p (b s) -> p b s", b=GB),
                                  ALU.mult).then_inc(ff_u, 1)

            def taps(g, j):
                n = on_dve(g, j)
                dve.wait_ge(ff_t1, n)
                dve.scalar_tensor_tensor(tt[j], uu[j % 4][:, :, 0:S], convw[:, 3 * j:3 * j + 1], tt[j],
                                         ALU.mult, ALU.add).then_inc(ff_t2, 1)
                dve.wait_ge(ff_t2, n)
                dve.scalar_tensor_tensor(tt[j], uu[j % 4][:, :, 2:S + 2], convw[:, 3 * j + 2:3 * j + 3], tt[j],
                                         ALU.mult, ALU.add).then_inc(ff_t3, 1)

            def largest(g, gpar):
                dve.wait_ge(ff_s, (g + 1) * FJ)
                dve.tensor_reduce(am[gpar], sv[gpar].rearrange("p j n -> p n j"), AX.X, ALU.max,
                                  apply_absolute_value=True).then_inc(ff_am, 1)

            def invert(g, gpar):
                dve.wait_ge(ff_mr, g + 1)
                dve.reciprocal(mi[gpar], mr[gpar]).then_inc(ff_mi, 1)

            def round_si(g, gpar):
                dve.wait_ge(ff_mul, g + 1)
                wait(dve, ff_ops, g)
                dve.tensor_scalar(si, sv[gpar], MAGIC, -MAGIC, ALU.add, ALU.add).then_inc(ff_si, 1)

            def ff_out(g, gpar):
                dve.wait_ge(ff_ops, g + 1)
                wait(dve, ff_fo_free, g + 1)
                for c in range(C):
                    ins = dve.scalar_tensor_tensor(fo[gpar][:, c], ps[:, 4 + c, 0:GN], w1m[:, 1:2], mr[gpar],
                                                   ALU.mult, ALU.mult)
                ins.then_inc(ff_fo, 1)

            def ff_group(g, gpar):
                for j in range(FJ + TAPS_LAG):
                    if j < FJ:
                        dequant(g, j)
                    if TAPS_LAG <= j and j - TAPS_LAG not in PE_CHUNKS:
                        taps(g, j - TAPS_LAG)
                    if j == ROUND_AT and (not isinstance(g, int) or g > 1):
                        round_si(g - 2, gpar)
                    if j == LARGEST_AT and (not isinstance(g, int) or g > 0):
                        largest(g - 1, 1 - gpar)
                    if j == OUT_AT and (not isinstance(g, int) or g > 1):
                        ff_out(g - 2, gpar)
                    if j == INVERT_AT and (not isinstance(g, int) or g > 0):
                        invert(g - 1, 1 - gpar)

            dve.wait_ge(ln_out, 2 * LN_STEPS)
            dve.wait_ge(ff_pad, len(UP_BANKS))
            for g in range(4):
                ff_group(g, g % 2)
            with dve.Fori(2, GROUPS // 2) as i:
                ff_group(2 * i, 0)
                ff_group(2 * i + 1, 1)
            round_si(GROUPS - 2, 0)
            largest(GROUPS - 1, 1)
            invert(GROUPS - 1, 1)
            ff_out(GROUPS - 2, 0)
            round_si(GROUPS - 1, 1)
            ff_out(GROUPS - 1, 1)

            dve.wait_ge(ld_pj, 16)
            dve.tensor_reduce(pj[:, :], pj_raw, AX.X, ALU.add).then_inc(pj_done, 1)

            dve.wait_ge(ff_res, GROUPS)
            gather_stats(2)
            normalise(2)

            def evac_v7(g, par):
                dve.wait_ge(a1_vps, g + 1)
                wait(dve, a1_ops, g - 1)
                dve.tensor_tensor(v7[par], ps[0:S, 2, 0:GB * HS].rearrange("p (b d) -> p b d", b=GB),
                                  bv1[:, :].unsqueeze(1).to_broadcast([S, GB, HS]), ALU.add).then_inc(a1_v, 1)

            def mask7(g, par):
                dve.wait_ge(a1_wps, g + 1)
                dve.tensor_tensor(w7[par], ps[0:S, 3, 0:GN].rearrange("p (b n) -> p b n", b=GB),
                                  cmask[:, :].unsqueeze(1).to_broadcast([S, GB, S]), ALU.mult).then_inc(a1_w, 1)

            def add7(g, par):
                dve.wait_ge(a1_pps, g + 1)
                for c in range(C):
                    dst = hT[:, c, bass.ds(g * GN, GN)]
                    ins = dve.scalar_tensor_tensor(dst, ps[:, 5 + c, 0:GN], pjb[:, c:c + 1], dst,
                                                   ALU.add, ALU.add)
                ins.then_inc(a1_res, 1)

            dve.wait_ge(ld_a1, 80)
            evac_v7(0, 0)
            evac_v7(1, 1)
            mask7(0, 0)
            add7(0, 0)
            with dve.Fori(1, GROUPS // 2) as i:
                for par in range(2):
                    s = 2 * i + par
                    evac_v7(s, par)
                    mask7(s - 1, 1 - par)
                    add7(s - 1, 1 - par)
            mask7(GROUPS - 1, 1)
            add7(GROUPS - 1, 1)

            dve.wait_ge(a1_res, GROUPS)
            gather_stats(3)
            dve.wait_ge(ln_staged, 4 * LN_STEPS)

            normalise(3)

            dve.wait_ge(ld_rt, 48)
            dve.wait_ge(rt_lgps, LN_STEPS)
            dve.tensor_tensor(lgv, ps[:, 4, 0:TILES * E].rearrange("p (t e) -> p t e", e=E),
                              br[:, :].unsqueeze(1).to_broadcast([P, TILES, E]), ALU.add).then_inc(rt_lg, LN_STEPS)

            n[0] = 0

            def rstep(ins):
                n[0] += 1
                ins.then_inc(rt_step, 1)
                dve.wait_ge(rt_step, n[0])

            dve.wait_ge(rt_c, 5)
            dve.wait_ge(rt_lg, LN_STEPS)
            rstep(dve.tensor_reduce(rcol, lgv, AX.X, ALU.max))
            rstep(dve.tensor_tensor(rt, lgv, rcol.unsqueeze(2).to_broadcast([P, TILES, E]), ALU.is_equal))
            rstep(dve.tensor_tensor(rt, rt, rev.unsqueeze(1).to_broadcast([P, TILES, E]), ALU.mult))
            rstep(dve.tensor_reduce(rcol, rt, AX.X, ALU.max))
            rstep(dve.tensor_tensor(oh, rev.unsqueeze(1).to_broadcast([P, TILES, E]),
                                    rcol.unsqueeze(2).to_broadcast([P, TILES, E]), ALU.is_equal))
            dve.tensor_copy(ohb, oh)
            rstep(dve.tensor_reduce(cntp, oh.rearrange("p t e -> p e t"), AX.X, ALU.add))
            dve.tensor_copy(cntb, cntp).then_inc(rt_cb, 1)
            dve.wait_ge(rt_cntps, 1)
            rstep(dve.tensor_copy(nt, ps[:, 5, 0:E]))
            rstep(dve.tensor_tensor(cmp_, nt.unsqueeze(2).to_broadcast([P, E, TILES]), thr, ALU.is_gt))
            rstep(dve.tensor_reduce(nt, cmp_, AX.X, ALU.add))
            rstep(dve.tensor_tensor_scan(tend, onesf[:, 0:E], nt, 0.0, ALU.mult, ALU.add))
            rstep(dve.tensor_tensor(tst, tend, nt, ALU.subtract))
            rstep(dve.tensor_scalar(tst, tst, float(P), None, ALU.mult))
            dve.wait_ge(rt_pps, 1)
            rstep(dve.tensor_tensor(rt, ps[:, 6, 0:TILES * E].rearrange("p (t e) -> p t e", e=E),
                                    tst.unsqueeze(1).to_broadcast([P, TILES, E]), ALU.add))
            rstep(dve.tensor_tensor(rt, rt, oh, ALU.mult))
            rstep(dve.tensor_reduce(rcol, rt, AX.X, ALU.add))
            dve.tensor_copy(posu[:, :], rcol).then_inc(rt_pos, 1)
            rstep(dve.tensor_tensor(it24, it24, tend.unsqueeze(1).to_broadcast([P, MAX_TILES, E]), ALU.is_ge))
            rstep(dve.tensor_reduce(te, it24, AX.X, ALU.add))
            dve.tensor_scalar(tei[:, :], te[0:1, :], float(E - 1), None, ALU.min).then_inc(rt_te, 1)

            def evac_h(i, par):
                dve.wait_ge(mo_h1ps, i + 1)
                wait(dve, mo_hTps, i)
                dve.tensor_copy(h1[:, PSUM_W:FF], ps[:, 1, :]).then_inc(mo_h1b, 1)

            def relu_b(i, par):
                dve.wait_ge(mo_hTps, i + 1)
                dve.wait_ge(mo_b1, i + 1)
                for j in range(FJ // 2, FJ):
                    ins = dve.tensor_scalar(hTm[:, j], ps[:, 3, (j - FJ // 2) * P:(j - FJ // 2 + 1) * P],
                                            b1s[par][:, j:j + 1], 0.0, ALU.add, ALU.max)
                ins.then_inc(mo_hTb, 1)

            def out_y(i, ii, par):
                e = dve.value_load(tei[0:1, bass.ds(i, 1)], min_val=0, max_val=E - 1)
                dve.wait_ge(mo_yps, i + 1)
                wait(dve, mo_yout[par], 16 * ii)
                dve.tensor_tensor(ysb[par], ps[:, 4 + par, 0:D], b2[:, bass.ds(e * D, D)],
                                  ALU.add).then_inc(mo_y, 1)

            dve.wait_ge(rt_te, 1)
            dve.wait_ge(ld_b2, 16)
            evac_h(0, 0)
            relu_b(0, 0)
            evac_h(1, 1)
            out_y(0, 0, 0)
            relu_b(1, 1)

            def two_tiles(i):
                for par in range(2):
                    s = 2 * i + par
                    evac_h(s, par)
                    out_y(s - 1, i + par - 1, 1 - par)
                    relu_b(s, par)

            two_tiles(1)
            with dve.Fori(2, MAX_TILES // 2) as i:
                two_tiles(i)
            out_y(MAX_TILES - 1, MAX_TILES // 2 - 1, 1)

            for t in range(TILES):
                dve.wait_ge(fin_in[t % GATH], 16 * (t // GATH + 1))
                dve.tensor_tensor(tm[:, t], tm[:, t], fg[:, t], ALU.add).then_inc(fin_add, 1)

        @block.tensor
        def _(pe):
            pe.wait_ge(ld_emb, 64)
            for g in range(EG):
                pe.wait_ge(ld_patch[g], 16)
                for c in range(C):
                    m = g * C + c
                    wait(pe, emb_out, m - 3)
                    for k in range(KP):
                        ins = pe.matmul(ps[:, m % 4, 0:EGN], wproj[:, k, c * P:(c + 1) * P],
                                        patches[:, g, k], start=(k == 0), stop=(k == KP - 1))
                    ins.then_inc(emb_mm, 1)
            pe.wait_ge(txt_step, 11)
            for m in range(4):
                c, half = m // 2, m % 2
                pe.matmul(ps[:, 4 + m, 0:PSUM_W], tab[:, c * P:(c + 1) * P],
                          sepv[:, half * PSUM_W:(half + 1) * PSUM_W], start=True, stop=True).then_inc(txt_mm, 1)
            pe.wait_ge(ld_pe, 32)
            pe.wait_ge(txt_out, 4)
            for c in range(C):
                pe.matmul(ps[:, 4 + c, 0:HC * SP1], wp_bd, pe_bd[:, c], start=True, stop=True).then_inc(at_pbps, 1)

            def to_tokens(k):
                def step(u, par, n):
                    g = k * LN_STEPS + u
                    pe.wait_ge(ln_staged, g + 1)
                    wait(pe, ln_tok, g - 1)
                    for m in range(n):
                        for c in range(C):
                            ins = pe.transpose(tokps(par)[:, m * D + c * P:m * D + (c + 1) * P],
                                               stage[par][:, c * n * P + m * P:c * n * P + (m + 1) * P],
                                               ident[:, :])
                    ins.then_inc(ln_tokps, 1)
                pairs_then_last(pe, step, step)

            def to_features(k):
                def step(u, par, n):
                    g = k * LN_STEPS + u
                    pe.wait_ge(ln_z, g + 1)
                    wait(pe, ln_out, g - 1)
                    for c in range(C):
                        for m in range(n):
                            lo = c * n * P + m * P
                            if k == 1:
                                ins = pe.transpose(zTps(par).bitcast(BF16)[:, lo:lo + P],
                                                   zb[par][:, m * D + c * P:m * D + (c + 1) * P], identb[:, :])
                            else:
                                ins = pe.transpose(zTps(par)[:, lo:lo + P],
                                                   z[par][:, m * D + c * P:m * D + (c + 1) * P], ident[:, :])
                    ins.then_inc(ln_zT, 1)
                    if k == 1:
                        pe.wait_ge(q_diag, u + 1)
                        pe.matmul(ps[:, 4 + par, 0:n * P], onesf[:, :], stage[par][:, 0:n * P],
                                  start=True, stop=True).then_inc(q_bps, 1)
                pairs_then_last(pe, step, step)

            pe.wait_ge(consts, 10)
            pe.wait_ge(emb_out, EG * C)
            to_tokens(0)
            to_features(0)

            def project_qk(b, q, turn):
                pe.wait_ge(at_y, b + 1)
                wait(pe, at_res, b - 4)
                for c in range(C):
                    pe.matmul(ps[:, 0, c * S:(c + 1) * S], wq_bd[:, :], yst[q][:, c], start=True, stop=True)
                for c in range(C):
                    ins = pe.matmul(ps[:, 0, (C + c) * S:(C + c + 1) * S], wk_bd[:, :], yst[q][:, c],
                                    start=True, stop=True)
                ins.then_inc(at_qkps, 1)

            def content(b, q, turn):
                pe.wait_ge(at_qkv, b + 1)
                wait(pe, at_s, b)
                for c in range(C):
                    ins = pe.matmul(ps[0:S, 4 + c, 0:HC * S], qu[q][:, c], kbd[q][:, c], start=True, stop=True)
                ins.then_inc(at_cps, 1)

            def project_v(b, q, turn):
                wait(pe, at_ctx, b)
                for c in range(C):
                    ins = pe.matmul(ps[0:S, 1, c * P:(c + 1) * P], yst[q][:, c], wv_bd[:, :],
                                    start=True, stop=True)
                ins.then_inc(at_vps, 1)

            def transpose_ctx(b, q, turn):
                pe.wait_ge(at_ctx, b + 1)
                pe.wait_ge(at_qkv, b + 5 if not isinstance(b, int) else min(b + 5, B))
                flat = ctxn.rearrange("p h d -> p (h d)")
                for c in range(C):
                    ins = pe.transpose(ps[:, 0, c * S:(c + 1) * S], flat[:, c * P:(c + 1) * P], ident[0:S, 0:S])
                ins.then_inc(at_ctxTps, 1)

            def transpose_p(b, q, turn):
                pe.wait_ge(at_p, b + 1)
                wait(pe, at_pT, b)
                for h in range(H):
                    ins = pe.transpose(ps[0:S, 6 + h // HC, h % HC * S:(h % HC + 1) * S], pr[q % 2][:, h],
                                       ident[0:S, 0:S])
                ins.then_inc(at_pTps, 1)

            def out_proj(b, q, turn):
                pe.wait_ge(at_ctxT, b + 1)
                for c in range(C):
                    for k in range(C):
                        ins = pe.matmul(ps[:, 0, (C + c) * S:(C + c + 1) * S],
                                        wo[:, k * D + c * P:k * D + (c + 1) * P], ctxT[:, k],
                                        start=(k == 0), stop=(k == C - 1))
                ins.then_inc(at_wops, 1)

            def position(b, q, turn):
                pe.wait_ge(at_qkv, b + 1)
                wait(pe, at_posp, b)
                for c in range(C):
                    ins = pe.matmul(ps[0:S, 2 + c, 0:HC * SP1], qv[:, c], pbd[:, c], start=True, stop=True)
                ins.then_inc(at_posps, 1)

            def context(b, q, turn):
                pe.wait_ge(at_pT, b + 1)
                pe.wait_ge(at_v, b + 1)
                for h in range(H):
                    ins = pe.matmul(ps[0:S, 1, h * (DH + 1):(h + 1) * (DH + 1)], prT[:, h], vaug[q % 2][:, h],
                                    start=True, stop=True)
                ins.then_inc(at_ctxps, 1)

            pe.wait_ge(ld_at, 160)
            pe.wait_ge(at_pbd, 2)
            pe.wait_ge(at_ones, 2)
            batches(pe, {"qk": project_qk, "content": content, "v": project_v, "ctxT": transpose_ctx,
                         "pT": transpose_p, "out": out_proj, "pos": position, "context": context},
                    [("content", 3), ("pT", 4), ("v", 4), ("ctxT", LAG), ("pos", 1), ("out", LAG),
                     ("context", 4), ("qk", 0)])

            to_tokens(1)
            to_features(1)

            w1v = w1i.rearrange("p (c f) -> p c f", c=C)
            w2v = w2i.rearrange("p (j d) -> p j d", j=FJ)

            def up(g, j):
                wait(pe, ff_u, g * FJ + j - 3)
                for c in range(C):
                    ins = pe.matmul(ps[:, UP_BANKS[j % 4], 0:GN], w1v[:, c, j * P:(j + 1) * P],
                                    ziT[:, c, bass.ds(g * GN, GN)], start=(c == 0), stop=(c == C - 1))
                ins.then_inc(ff_mm, 1)

            def convolve(g, j):
                n = PE_CHUNKS.index(j)
                pe.wait_ge(ff_u, g * FJ + j + 1)
                last = [c for c, b in zip(PE_CHUNKS, PE_BANKS) if b == PE_BANKS[n]]
                m = last.index(j)
                bg, bj = (g, last[m - 1]) if m > 0 else (g - 1, last[-1])
                wait(pe, ff_s, bg * FJ + bj + 1)
                for k in range(3):
                    ins = pe.matmul(ps[:, PE_BANKS[n], 0:GN], diag[:, n, k], uu[j % 4][:, :, k:k + S],
                                    start=(k == 0), stop=(k == 2))
                ins.then_inc(ff_cv, 1)

            def down(g):
                pe.wait_ge(ff_si, g + 1)
                wait(pe, ff_fo, g)
                for c in range(C):
                    for j in range(FJ):
                        ins = pe.matmul(ps[:, 4 + c, 0:GN], w2v[:, j, c * P:(c + 1) * P], si[:, j],
                                        start=(j == 0), stop=(j == FJ - 1))
                ins.then_inc(ff_ops, 1)

            def ff_group(g):
                for j in range(AHEAD):
                    up(g, j)
                for j in range(FJ):
                    if j + AHEAD < FJ:
                        up(g, j + AHEAD)
                    if j in PE_CHUNKS:
                        convolve(g, j)
                    if j == DOWN_AT and (not isinstance(g, int) or g > 1):
                        down(g - 2)

            pe.wait_ge(ln_out, 2 * LN_STEPS)
            pe.wait_ge(wq_done, 2)
            pe.wait_ge(ff_diag, 1)
            for g in range(3):
                ff_group(g)
            with pe.Fori(3, GROUPS) as g:
                ff_group(g)
            down(GROUPS - 2)
            down(GROUPS - 1)

            to_tokens(2)
            to_features(2)

            def project7(g, par):
                pe.wait_ge(a1_y, g + 1)
                wait(pe, a1_q, g)
                for c in range(C):
                    ins = pe.matmul(ps[0:HS, 0, 0:GN], wqkv_v[:, c, 0:HS], y7[par][:, c],
                                    start=(c == 0), stop=(c == C - 1))
                ins.then_inc(a1_qps, 1)
                wait(pe, a1_k, g)
                for c in range(C):
                    ins = pe.matmul(ps[0:HS, 1, 0:GN], wqkv_v[:, c, HS:2 * HS], y7[par][:, c],
                                    start=(c == 0), stop=(c == C - 1))
                ins.then_inc(a1_kps, 1)
                wait(pe, a1_v, g)
                for b in range(GB):
                    for c in range(C):
                        ins = pe.matmul(ps[0:S, 2, b * HS:(b + 1) * HS], y7[par][:, c, b * S:(b + 1) * S],
                                        wqkv_v[:, c, 2 * HS:3 * HS], start=(c == 0), stop=(c == C - 1))
                ins.then_inc(a1_vps, 1)

            def attend7(g, par):
                pe.wait_ge(a1_q, g + 1)
                pe.wait_ge(a1_k, g + 1)
                for b in range(GB):
                    ins = pe.matmul(ps[0:S, 3, b * S:(b + 1) * S], k7[par][:, b * S:(b + 1) * S],
                                    q7[par][:, b * S:(b + 1) * S], start=True, stop=True)
                ins.then_inc(a1_wps, 1)
                pe.wait_ge(a1_w, g + 1)
                pe.wait_ge(a1_v, g + 1)
                for b in range(GB):
                    ins = pe.matmul(ps[0:HS, 4, b * S:(b + 1) * S], v7[par][:, b], w7[par][:, b],
                                    start=True, stop=True)
                ins.then_inc(a1_ops, 1)
                pe.wait_ge(a1_o, g + 1)
                wait(pe, a1_res, g)
                for c in range(C):
                    ins = pe.matmul(ps[:, 5 + c, 0:GN], pj[:, c * P:(c + 1) * P], o7[par], start=True, stop=True)
                ins.then_inc(a1_pps, 1)

            pe.wait_ge(ld_a1, 80)
            pe.wait_ge(pj_done, 1)
            project7(0, 0)
            project7(1, 1)
            attend7(0, 0)
            with pe.Fori(1, GROUPS // 2) as i:
                for par in range(2):
                    project7(2 * i + par, par)
                    attend7(2 * i + par - 1, 1 - par)
            attend7(GROUPS - 1, 1)

            to_tokens(3)

            def z_transposed(u, par, n):
                g = 3 * LN_STEPS + u
                pe.wait_ge(ln_z, g + 1)
                wait(pe, ln_out, g - 1)
                for c in range(C):
                    for m in range(n):
                        lo = c * n * P + m * P
                        ins = pe.transpose(zTps(par)[:, lo:lo + P], z[par][:, m * D + c * P:m * D + (c + 1) * P],
                                           ident[:, :])
                ins.then_inc(ln_zT, 1)

            def router(u, par, n):
                pe.wait_ge(ln_out, 3 * LN_STEPS + u + 1)
                for m in range(n):
                    for c in range(C):
                        ins = pe.matmul(ps[:, 4, bass.ds((2 * u + m) * E, E)], zTs[par][:, c, m * P:(m + 1) * P],
                                        wr[:, c * E:(c + 1) * E], start=(c == 0), stop=(c == C - 1))
                ins.then_inc(rt_lgps, 1)

            pe.wait_ge(ld_rt, 48)
            z_transposed(0, 0, 2)
            z_transposed(1, 1, 2)
            router(0, 0, 2)
            with pe.Fori(1, PAIRS // 2) as i:
                for par in range(2):
                    z_transposed(2 * i + par, par, 2)
                    router(2 * i + par - 1, 1 - par, 2)
            z_transposed(PAIRS, 0, 1)
            router(PAIRS - 1, 1, 2)
            router(PAIRS, 0, 1)

            pe.wait_ge(rt_cb, 1)
            pe.matmul(ps[:, 5, 0:E], onesb, cntb, start=True, stop=True).then_inc(rt_cntps, 1)
            flat = ohb.rearrange("p t e -> p (t e)")
            pe.matmul(ps[:, 6, 0:TILES * E], triu, flat, start=True, stop=False)
            for t in range(TILES - 1):
                m = TILES - 1 - t
                ins = pe.matmul(ps[:, 6, (t + 1) * E:TILES * E].rearrange("p (t e) -> p t e", e=E), onesb,
                                ohb[:, t:t + 1, :].to_broadcast([P, m, E]), start=False, stop=(m == 1))
            ins.then_inc(rt_pps, 1)

            def rows_T(i, ii, par):
                pe.wait_ge(mo_xin[par], 16 * ii + 16)
                wait(pe, mo_xT, i - 1)
                for c in range(C):
                    ins = pe.transpose(ps[:, 6 + par, c * P:(c + 1) * P], xt[par][:, c * P:(c + 1) * P],
                                       ident[:, :])
                ins.then_inc(mo_xTps, 1)

            def up_e(i, par):
                e = pe.value_load(tei[0:1, bass.ds(i, 1)], min_val=0, max_val=E - 1)
                pe.wait_ge(mo_xT, i + 1)
                wait(pe, mo_h1a, i)
                wait(pe, mo_h1b, i)
                for half in range(2):
                    for c in range(C):
                        ins = pe.matmul(ps[:, half, :], xT[par][:, c * P:(c + 1) * P],
                                        moe_w[:, bass.ds(e * WE + c * FF + half * PSUM_W, PSUM_W)],
                                        start=(c == 0), stop=(c == C - 1))
                ins.then_inc(mo_h1ps, 1)

            def hidden_T(i, par):
                pe.wait_ge(mo_h1a, i + 1)
                pe.wait_ge(mo_h1b, i + 1)
                wait(pe, mo_hTa, i)
                wait(pe, mo_hTb, i)
                for j in range(FJ):
                    ins = pe.transpose(ps[:, 2 + j // 4, j % 4 * P:(j % 4 + 1) * P], h1[:, j * P:(j + 1) * P],
                                       ident[:, :])
                ins.then_inc(mo_hTps, 1)

            def down_e(i, par):
                e = pe.value_load(tei[0:1, bass.ds(i, 1)], min_val=0, max_val=E - 1)
                pe.wait_ge(mo_hTa, i + 1)
                pe.wait_ge(mo_hTb, i + 1)
                wait(pe, mo_y, i - 1)
                for j in range(FJ):
                    ins = pe.matmul(ps[:, 4 + par, 0:D], hTm[:, j],
                                    moe_w[:, bass.ds(e * WE + C * FF + j * D, D)],
                                    start=(j == 0), stop=(j == FJ - 1))
                ins.then_inc(mo_yps, 1)

            pe.wait_ge(rt_te, 1)
            pe.wait_ge(ld_moe, 16 * W_EARLY)
            pe.wait_ge(ld_moe5, 16)
            pe.wait_ge(ld_moe467, 48)
            rows_T(0, 0, 0)
            up_e(0, 0)
            rows_T(1, 0, 1)
            hidden_T(0, 0)
            up_e(1, 1)
            down_e(0, 0)
            rows_T(2, 1, 0)
            hidden_T(1, 1)

            def two_tiles(i):
                for par in range(2):
                    s = 2 * i + par
                    up_e(s, par)
                    down_e(s - 1, 1 - par)
                    rows_T(s + 1, i + par, 1 - par)
                    hidden_T(s, par)

            two_tiles(1)
            with pe.Fori(2, MAX_TILES // 2 - 1) as i:
                two_tiles(i)
            s = MAX_TILES - 2
            up_e(s, 0)
            down_e(s - 1, 1)
            rows_T(s + 1, MAX_TILES // 2 - 1, 1)
            hidden_T(s, 0)
            up_e(s + 1, 1)
            down_e(s, 0)
            hidden_T(s + 1, 1)
            down_e(s + 1, 1)


def lay_out(i):
    def cols(v):
        return v.reshape(-1, P).T

    def feat(w):
        return w.T.reshape(-1, P, w.shape[0]).transpose(1, 0, 2)

    def heads(w):
        m = np.zeros((P, P), w.dtype)
        for h in range(HC):
            m[h * DH:(h + 1) * DH, h * DH:(h + 1) * DH] = w
        return m

    def every(v):
        return np.broadcast_to(v.reshape(1, -1), (P, v.size))

    pos = np.arange(S, dtype=np.float32)[:, None]
    div = np.exp(np.arange(0, D, 2, dtype=np.float32) * np.float32(-np.log(10000.0) / D))
    pe = np.zeros((S, D), np.float32)
    pe[:, 0::2] = np.sin(pos * div)
    pe[:, 1::2] = np.cos(pos * div)
    pe_bd = np.zeros((P, C, HC, SP1), np.float32)
    for c in range(C):
        for h in range(HC):
            lo = (c * HC + h) * DH
            pe_bd[h * DH:(h + 1) * DH, c, h, 1:] = pe[:, lo:lo + DH].T

    hp = 6
    patches = (i["x"].reshape(B, hp, 16, hp, 16, 3).transpose(0, 1, 3, 2, 4, 5)
               .reshape(EG, EGN, KP, P).transpose(3, 0, 2, 1))
    w1e = i["L1_ffn_W1"].transpose(2, 0, 1).reshape(C, P, E, FF).transpose(1, 2, 0, 3).reshape(P, E, C * FF)
    w2e = i["L1_ffn_W2"].transpose(2, 0, 1).reshape(FJ, P, E, D).transpose(1, 2, 0, 3).reshape(P, E, FJ * D)
    qkv_b = i["L1_attn_qkv_b"]
    return {
        "patches": patches,
        "w_proj": feat(i["L0_tok_W_proj"]),
        "pos": feat(i["L0_tok_pos_emb"]),
        "b_proj": cols(i["L0_tok_b_proj"]),
        "x_txt": np.broadcast_to(i["x_txt"].reshape(1, -1), (TAB, NTXT)),
        "table": i["L0_txt_weights"][:TAB],
        "gamma": cols(i["L0_attn_ln_gamma"]),
        "beta": cols(i["L0_attn_ln_beta"]),
        "wq": heads(i["L0_attn_Wq"]), "wk": heads(i["L0_attn_Wk"]),
        "wv": heads(i["L0_attn_Wv"]), "wp": heads(i["L0_attn_Wp"]),
        "bq": np.tile(i["L0_attn_bq"], HC).reshape(P, 1),
        "bk": np.tile(i["L0_attn_bk"], HC).reshape(P, 1),
        "bv": np.tile(i["L0_attn_bv"], HC).reshape(P, 1),
        "u_bias": cols(i["L0_attn_u_bias"]), "v_bias": cols(i["L0_attn_v_bias"]),
        "wo": i["L0_attn_Wo"].reshape(C, P, D).transpose(1, 0, 2).reshape(P, C * D),
        "bo": cols(i["L0_attn_bo"]),
        "pe_bd": pe_bd.reshape(P, C, HC * SP1),
        "w1": feat(i["L0_ffn_w1"]).reshape(P, C * FF),
        "w2": feat(i["L0_ffn_w2"]).reshape(P, FJ * D),
        "conv_w": i["L0_ffn_conv_w"].reshape(FJ, P, 3).transpose(1, 0, 2).reshape(P, FJ * 3),
        "conv_b": cols(i["L0_ffn_conv_b"]),
        "wqkv": feat(i["L1_attn_qkv_w"]).reshape(P, C * 3 * HS),
        "bq1": qkv_b[:HS].reshape(HS, 1), "bk1": qkv_b[HS:2 * HS].reshape(HS, 1),
        "bv1": np.broadcast_to(qkv_b[2 * HS:].reshape(1, HS), (S, HS)),
        "pj": i["L1_attn_proj_w"].reshape(D, NREP, HS).transpose(2, 0, 1),
        "pjb": cols(i["L1_attn_proj_b"]),
        "wr": feat(i["L1_ffn_Wr"]).reshape(P, C * E),
        "br": every(i["L1_ffn_br"]),
        "moe_w": np.concatenate([w1e, w2e], axis=2),
        "b1": i["L1_ffn_b1"].reshape(E, FJ, P).transpose(2, 0, 1).reshape(P, E * FJ),
        "b2": every(i["L1_ffn_b2"]),
    }


def kernel(**inputs):
    import numpy as _np
    import concourse.bacc as _bacc
    from concourse.bass_utils import run_bass_kernel_spmd as _run

    nc = _bacc.Bacc("TRN2", target_bir_lowering=False, num_devices=1)
    arrays, args = {}, {}
    for name, v in lay_out({k: _np.asarray(v) for k, v in inputs.items()}).items():
        v = _np.ascontiguousarray(v)
        arrays[f"in_{name}"] = v
        args[name] = nc.dram_tensor(f"in_{name}", v.shape, mybir.dt.from_np(v.dtype), kind="ExternalInput").ap()
    out = nc.dram_tensor("out_rows", (NTOK, D), F32, kind="ExternalOutput").ap()
    program(nc, args, out)
    r = _run(nc, [arrays], core_ids=[0])
    return r.results[0]["out_rows"].reshape(B, S, D)
```

```python
import numpy as np
import concourse.bass as bass
from concourse import mybir
from contextlib import ExitStack

F32 = mybir.dt.float32
BF16 = mybir.dt.bfloat16
I32 = mybir.dt.int32
U32 = mybir.dt.uint32
ALU = mybir.AluOpType
ACT = mybir.ActivationFunctionType
AX = mybir.AxisListType
RED = bass.bass_isa.ReduceOp

P = 128
B, S_IMG, S_TXT = 32, 36, 32
S = S_IMG + S_TXT
NTOK = B * S
D = 256
C = D // P
TILES = NTOK // P
PAIRS = TILES // 2
LN_STEPS = PAIRS + 1
HALF = 6
PARTS = ((0, 2 * HALF), (2 * HALF, TILES))
PATCH = 768
KP = PATCH // P
EG = 4
EGN = B // EG * S_IMG
NTXT = B * S_TXT
TAB = S_TXT + 2
H, DH = 8, 32
HC = H // C
DEEP = 4
LAG = 5
SP1 = S + 1
FF = 1024
FJ = FF // P
GB = 4
GN = GB * S
GROUPS = B // GB
HS = 16
NREP = 16
E = 8
MAX_TILES = (NTOK + E * (P - 1)) // P
ON_POOL = 8
DOWN_AFTER = 4
EPS = 1e-5
MAGIC = 1.5 * 2.0 ** 23
PSUM_W = 512
WE = C * FF + FJ * D
W_EARLY = 4
DIAG_SLOT, RAW_SLOT = 4, 5
LARGEST_AT = 0
INVERT_AT = 5
ROUND_AT = 2
OUT_AT = 7
DOWN_AT = 4
PE_CHUNKS = (0, 2, 3, 4, 6)
PE_BANKS = (2, 3, 2, 3, 2)
UP_BANKS = (0, 1, 6, 7)
AHEAD = 3
TAPS_LAG = 2
SILU_LAG = 2



def wait(e, sem, v):
    if isinstance(v, int) and v <= 0:
        return
    e.wait_ge(sem, v)


def program(nc, a, out):
    ctx = ExitStack()
    with ctx:
        def sb(name, shape, dt=F32):
            return ctx.enter_context(nc.sbuf_tensor(name, shape, dt))

        def sem(name):
            return ctx.enter_context(nc.semaphore(name))

        moe_w = sb("moe_w", [P, E * WE])
        hT_t = sb("hT", [P, C * NTOK])
        yT_t = sb("yT", [P, C * NTOK])
        tm_t = sb("tm", [P, TILES * D])
        hT = hT_t[:, :].rearrange("p (c n) -> p c n", c=C)
        yT = yT_t[:, :].rearrange("p (c n) -> p c n", c=C)
        tm = tm_t[:, :].rearrange("p (t d) -> p t d", t=TILES)

        class Region:

            def __init__(self, tensor, at, end):
                self.tensor, self.at, self.end = tensor, at, end

            def take(self, shape, dt=F32, parts=P):
                n = int(np.prod(shape))
                words = n // 2 if dt == BF16 else n
                v = self.tensor[0:parts, self.at:self.at + words]
                self.at += words
                assert self.at <= self.end, (self.at, self.end)
                if dt != F32:
                    v = v.bitcast(dt)
                if len(shape) == 2:
                    v = v.rearrange("p (a b) -> p a b", a=shape[0])
                if len(shape) == 3:
                    v = v.rearrange("p (a b c) -> p a b c", a=shape[0], b=shape[1])
                return v

        def last_experts():
            return Region(moe_w, (E - 2) * WE, E * WE)

        ident = sb("ident", [P, P])
        identb = sb("identb", [P, P], BF16)
        onesf = sb("onesf", [P, P])
        neg_half = sb("neg_half", [P, TILES])
        pid = sb("pid", [P, 1])
        gamma = sb("gamma", [P, C])
        beta = sb("beta", [P, C])
        bqu = sb("bqu", [P, C])
        bqv = sb("bqv", [P, C])
        bk0 = sb("bk0", [P, 1])
        bv0 = sb("bv0", [P, 1])
        bo0 = sb("bo0", [P, C])
        hmask = sb("hmask", [P, HC])
        bproj = sb("bproj", [P, C])
        wq_bd = sb("wq_bd", [P, P])
        wk_bd = sb("wk_bd", [P, P])
        wv_bd = sb("wv_bd", [P, P])
        wo = sb("wo", [P, C * D])
        wi = sb("wi", [P, (C * FF + FJ * D) // 2])
        w1i = wi[:, 0:C * FF // 2].bitcast(BF16)
        w2i = wi[:, C * FF // 2:].bitcast(BF16)
        convw = sb("convw", [P, FJ * 3])
        convb = sb("convb", [P, FJ])
        w1m = sb("w1m", [P, 2])
        wsum = sb("wsum", [P, 4])

        r = last_experts()
        patches = r.take([EG, KP, EGN])
        r = Region(tm_t, 0, TILES * D)
        wproj = r.take([KP, D])
        tab = r.take([D], parts=TAB)
        posb = r.take([C, S_IMG])
        sepv = r.take([NTXT], parts=TAB)
        padv = r.take([NTXT], parts=TAB)
        r = Region(yT_t, 0, C * NTOK)
        tok_i = r.take([NTXT], I32, TAB)
        tokf = r.take([NTXT], parts=TAB)
        gidx = r.take([NTXT], parts=TAB)
        base = r.take([NTXT], parts=TAB)
        r = Region(moe_w, RAW_SLOT * WE, (RAW_SLOT + 1) * WE)
        w1raw = r.take([C * FF])
        w2raw = r.take([FJ * D])
        runs = moe_w[0:TAB, (E - 2) * WE + EG * KP * EGN:E * WE][:, 0:NTXT]
        runp = wi[0:TAB, 0:NTXT]

        stage = [sb(f"stage{i}", [P, 2 * D]) for i in range(2)]
        z = [sb(f"z{i}", [P, 2 * D]) for i in range(2)]
        zb = [z[i][:, 0:D].bitcast(BF16) for i in range(2)]
        bn = sb("bn", [P, TILES * 6])
        bnv = bn[:, :].rearrange("p (t k) -> p t k", k=6)
        bsum_t = sb("bsum", [P, 4 * TILES])
        bsum = bsum_t[:, :].rearrange("p (k t) -> p k t", k=4)
        mean = sb("mean", [P, TILES])
        var = sb("var", [P, TILES])
        ve = sb("ve", [P, TILES])
        rstd = sb("rstd", [P, TILES])
        amax = sb("amax", [P, TILES])
        qstep = sb("qstep", [P, TILES])
        qinv = sb("qinv", [P, TILES])

        r = Region(tm_t, 0, TILES * D)
        kbd = [r.take([C, HC * S]) for _ in range(DEEP)]
        qu = [r.take([C, S]) for _ in range(DEEP)]
        yst = [r.take([C, S]) for _ in range(DEEP)]
        qv = r.take([C, S])
        ctxn = r.take([H, DH], parts=S)
        ctxT = r.take([C, S])
        r = last_experts()
        pbd = r.take([C, HC * SP1])
        posp = [r.take([C, HC * SP1], parts=S) for _ in range(2)]
        poss = [r.take([C, HC * S], parts=S) for _ in range(2)]
        sx = [r.take([H, S], parts=S) for _ in range(2)]
        pr = [r.take([H, S], parts=S) for _ in range(2)]
        prT = r.take([H, S], parts=S)
        vaug = [r.take([H, DH + 1], parts=S) for _ in range(2)]
        rz = r.take([H], parts=S)
        mx = [r.take([H], parts=S) for _ in range(2)]
        r = Region(moe_w, DIAG_SLOT * WE, (DIAG_SLOT + 1) * WE)
        pe_bd = r.take([C, HC * SP1])
        wp_bd = r.take([P])

        r = last_experts()
        sv = [r.take([FJ, GN]) for _ in range(2)]
        si = r.take([FJ, GN], BF16)
        uu = [r.take([GB, S + 2]) for _ in range(len(UP_BANKS))]
        tt = {j: r.take([GB, S]) for j in range(FJ) if j not in PE_CHUNKS}
        am = [r.take([GN]) for _ in range(2)]
        r = Region(moe_w, DIAG_SLOT * WE, (DIAG_SLOT + 1) * WE)
        diag = r.take([len(PE_CHUNKS), 3, P])
        mr = [r.take([GN]) for _ in range(2)]
        mi = [r.take([GN]) for _ in range(2)]
        fo = [r.take([C, GN]) for _ in range(2)]
        ziT = yT_t[:, 0:NTOK].bitcast(BF16).rearrange("p (c n) -> p c n", c=C)
        rsb = yT_t[:, NTOK:2 * NTOK]

        wqkv = sb("wqkv", [P, C * 3 * HS])
        wqkv_v = wqkv[:, :].rearrange("p (c n) -> p c n", c=C)
        bq1 = sb("bq1", [HS, 1])
        bk1 = sb("bk1", [HS, 1])
        bv1 = sb("bv1", [S, HS])
        pj = sb("pj", [HS, D])
        pjb = sb("pjb", [P, C])
        cmask = sb("cmask", [S, S])
        pj_raw = Region(moe_w, RAW_SLOT * WE, (RAW_SLOT + 1) * WE).take([D, NREP], parts=HS)
        r = Region(tm_t, 0, TILES * D)
        y7 = [r.take([C, GN]) for _ in range(2)]
        q7 = [r.take([GN], parts=HS) for _ in range(2)]
        k7 = [r.take([GN], parts=HS) for _ in range(2)]
        v7 = [r.take([GB, HS], parts=S) for _ in range(2)]
        w7 = [r.take([GB, S], parts=S) for _ in range(2)]
        o7 = [r.take([GN], parts=HS) for _ in range(2)]

        wr = sb("wr", [P, C * E])
        br = sb("br", [P, E])
        lg = sb("lg", [P, TILES * E])
        lgv = lg[:, :].rearrange("p (t e) -> p t e", e=E)
        z3 = hT_t[:, :].rearrange("p (t d) -> p t d", t=TILES)
        r = Region(yT_t, 0, C * NTOK)
        zTs = [r.take([C, 2 * P]) for _ in range(2)]
        oh = r.take([TILES, E])
        ohb = r.take([TILES, E], BF16)
        rt = r.take([TILES, E])
        rcol = r.take([TILES])
        rev = r.take([E])
        thr = r.take([E, TILES])
        cmp_ = r.take([E, TILES])
        cntp = r.take([E])
        cntb = r.take([E], BF16)
        nt = r.take([E])
        tend = r.take([E])
        tst = r.take([E])
        it24 = r.take([MAX_TILES, E])
        te = r.take([MAX_TILES])
        triu = r.take([P], BF16)
        onesb = r.take([P], BF16)
        posu = sb("posu", [P, TILES], U32)
        tei = sb("tei", [1, MAX_TILES], I32)
        used = sb("used", [1, 2], I32)
        zeros = Region(moe_w, RAW_SLOT * WE, (RAW_SLOT + 1) * WE).take([MAX_TILES // 3 * D])
        b2 = wi
        b1 = sb("b1", [P, E * FJ])
        r = Region(yT_t, 0, C * NTOK)
        xt = [r.take([D]) for _ in range(2)]
        xT = [r.take([D]) for _ in range(2)]
        h1 = r.take([FF])
        hTm = r.take([FJ, P])
        ysb = [r.take([D]) for _ in range(2)]
        b1s = [r.take([FJ]) for _ in range(2)]
        GATH = 6
        fg = z3

        ps = ctx.enter_context(nc.psum_tensor("ps", [P, 8, PSUM_W], F32))

        scr = [nc.dram_tensor(f"shift{i}", [H, S * SP1], F32, kind="Internal").ap() for i in range(2)]
        xs = nc.dram_tensor("sorted_rows", [MAX_TILES * P, D], F32, kind="Internal").ap()
        ys = nc.dram_tensor("sorted_out", [MAX_TILES * P, D], F32, kind="Internal").ap()

        (pool_past, sync_past, ld_emb, ld_txt, ld_ln, ld_at, ld_w12, ld_ff, ld_a1, ld_pj, ld_rt, ld_b2, ld_pe,
         ld_moe, ld_moe5, ld_moe467,
         consts, iotas, txt_step, posb_ok, emb_mm, emb_out, txt_mm, txt_out,
         ln_staged, ln_tokps, ln_tok, ln_bn, ln_ba, ln_mv, ln_ve, ln_rstd, ln_z, ln_zT, ln_out,
         q_z, q_amax, q_step, q_inv, q_mul, q_diag, q_bps,
         wq_abs, wq_sum, wq_mean, wq_inv, wq_a, wq_b, wq_done, pj_done) = [sem(n) for n in (
             "pool_past sync_past ld_emb ld_txt ld_ln ld_at ld_w12 ld_ff ld_a1 ld_pj ld_rt ld_b2 ld_pe "
             "ld_moe ld_moe5 ld_moe467 "
             "consts iotas txt_step posb_ok emb_mm emb_out txt_mm txt_out "
             "ln_staged ln_tokps ln_tok ln_bn ln_ba ln_mv ln_ve ln_rstd ln_z ln_zT ln_out "
             "q_z q_amax q_step q_inv q_mul q_diag q_bps "
             "wq_abs wq_sum wq_mean wq_inv wq_a wq_b wq_done pj_done").split()]
        (at_bias, at_pbps, at_pbd, at_y, at_qkps, at_qkv, at_vps, at_v, at_posps, at_posp, at_cps, at_s, at_mx,
         at_sub, at_p, at_pTps, at_pT, at_ctxps, at_rz, at_ctx, at_ctxTps, at_ctxT, at_wops, at_res, at_ones) = [
             sem(n) for n in (
                 "at_bias at_pbps at_pbd at_y at_qkps at_qkv at_vps at_v at_posps at_posp at_cps at_s at_mx "
                 "at_sub at_p at_pTps at_pT at_ctxps at_rz at_ctx at_ctxTps at_ctxT at_wops at_res at_ones").split()]
        (ff_pad, ff_diag, ff_cv, ff_mm, ff_u, ff_t1, ff_t2, ff_t3, ff_s, ff_am, ff_red, ff_mr, ff_mi, ff_mul, ff_si, ff_ops,
         ff_fo, ff_fo_free, ff_res) = [sem(n) for n in (
             "ff_pad ff_diag ff_cv ff_mm ff_u ff_t1 ff_t2 ff_t3 ff_s ff_am ff_red ff_mr ff_mi ff_mul ff_si ff_ops "
             "ff_fo ff_fo_free ff_res").split()]
        (a1_y, a1_qps, a1_kps, a1_q, a1_k, a1_vps, a1_v, a1_wps, a1_w, a1_ops, a1_o, a1_pps, a1_res) = [
            sem(n) for n in (
                "a1_y a1_qps a1_kps a1_q a1_k a1_vps a1_v a1_wps a1_w a1_ops a1_o a1_pps a1_res").split()]
        (z_kept, rt_c, rt_lgps, rt_lg, rt_step, rt_cntps, rt_pos, rt_te, rt_pps, rt_cb, sc_zero, sc_rows,
         mo_b1, mo_xTps, mo_xT, mo_h1ps, mo_h1a, mo_h1b, mo_hTps, mo_hTa, mo_hTb, mo_yps, mo_y,
         fin_add, fin_pool, fin_pool_out, fin_out, st_zero) = [
            sem(n) for n in (
                "z_kept rt_c rt_lgps rt_lg rt_step rt_cntps rt_pos rt_te rt_pps rt_cb sc_zero sc_rows "
                "mo_b1 mo_xTps mo_xT mo_h1ps mo_h1a mo_h1b mo_hTps mo_hTa mo_hTb mo_yps mo_y "
                "fin_add fin_pool fin_pool_out fin_out st_zero").split()]
        ld_patch = [sem(f"ld_patch{i}") for i in range(EG)]
        at_out = [sem(f"at_out{i}") for i in range(2)]
        at_in = [sem(f"at_in{i}") for i in range(2)]
        mo_xin = [sem(f"mo_xin{i}") for i in range(2)]
        mo_yout = [sem(f"mo_yout{i}") for i in range(2)]
        fin_in = [sem(f"fin_in{i}") for i in range(GATH)]

        block = ctx.enter_context(nc.Block())

        def tokps(par):
            return ps[:, par, :]

        def zTps(par):
            return ps[:, 2 + par, :]

        def pairs_then_last(e, step, last):
            step(0, 0, 2)
            step(1, 1, 2)
            with e.Fori(1, PAIRS // 2) as i:
                step(2 * i, 0, 2)
                step(2 * i + 1, 1, 2)
            last(PAIRS, 0, 1)

        def on_pe(g, j):
            return g * len(PE_CHUNKS) + sum(c <= j for c in PE_CHUNKS)

        def on_dve(g, j):
            return g * (FJ - len(PE_CHUNKS)) + sum(c <= j for c in range(FJ) if c not in PE_CHUNKS)

        def batches(e, part, order):
            def step(i, q):
                for name, lag in order:
                    b, turn = DEEP * i + q - lag, (DEEP // 2) * i + (q - lag) // 2
                    if not isinstance(b, int) or 0 <= b < B:
                        part[name](b, (q - lag) % DEEP, turn)
            for s in range(2 * DEEP):
                step(s // DEEP, s % DEEP)
            with e.Fori(2, B // DEEP) as i:
                for q in range(DEEP):
                    step(i, q)
            for s in range(B, B + LAG):
                step(s // DEEP, s % DEEP)

        @block.sync
        def _(sp):
            sp.dma_start(wproj, a["w_proj"]).then_inc(ld_emb, 16)
            for g in range(EG):
                sp.dma_start(patches[:, g], a["patches"][:, g]).then_inc(ld_patch[g], 16)
                if g == 0:
                    sp.dma_start(posb, a["pos"]).then_inc(ld_emb, 16)
                    sp.dma_start(bproj[:, :], a["b_proj"]).then_inc(ld_emb, 16)
            sp.dma_start(w1raw, a["w1"]).then_inc(ld_w12, 16)
            sp.dma_start(w2raw, a["w2"]).then_inc(ld_w12, 16)
            for t, n in ((gamma, "gamma"), (beta, "beta")):
                sp.dma_start(t[:, :], a[n]).then_inc(ld_ln, 16)
            for t, n in ((bqu, "u_bias"), (bqv, "v_bias"), (wsum[:, 0:1], "bq"), (bk0, "bk"), (bv0, "bv"),
                         (bo0, "bo"), (wq_bd, "wq"), (wk_bd, "wk"), (wv_bd, "wv"), (wo, "wo")):
                sp.dma_start(t[:, :], a[n]).then_inc(ld_at, 16)
            for t, n in ((convw, "conv_w"), (convb, "conv_b")):
                sp.dma_start(t[:, :], a[n]).then_inc(ld_ff, 16)
            for t, n in ((wqkv, "wqkv"), (bq1, "bq1"), (bk1, "bk1"), (bv1, "bv1"), (pjb, "pjb")):
                sp.dma_start(t[:, :], a[n]).then_inc(ld_a1, 16)
            for t, n in ((wr, "wr"), (br, "br"), (b1, "b1")):
                sp.dma_start(t[:, :], a[n]).then_inc(ld_rt, 16)
            for e in range(W_EARLY):
                sp.dma_start(moe_w[:, e * WE:(e + 1) * WE], a["moe_w"][:, e]).then_inc(ld_moe, 16)
            def scores_back(b, q, turn):
                par = q % 2
                wait(sp, at_s, b - 1)
                sp.sem_inc(sync_past, 1)
                sp.wait_ge(at_out[par], 16 * turn + 16)
                sp.dma_start(poss[par].rearrange("p a (h c) -> p (a h) c", c=S),
                             scr[par][:, S:S + S * S].rearrange("h (i c) -> i h c", c=S)).then_inc(at_in[par], 16)

            def scores_out(b, q, turn):
                par = q % 2
                wait(sp, at_in[par], 16 * turn)
                sp.sem_inc(sync_past, 1)
                sp.wait_ge(at_posp, b + 1)
                sp.dma_start(scr[par].rearrange("h (i c) -> i h c", c=SP1),
                             posp[par].rearrange("p a (h c) -> p (a h) c", c=SP1)).then_inc(at_out[par], 16)

            batches(sp, {"back": scores_back, "out": scores_out}, [("back", 2), ("out", 1)])
            sp.wait_ge(st_zero, 1)
            for n in range(3):
                k = MAX_TILES // 3 * P
                for rows in (xs, ys):
                    sp.dma_start(rows[n * k:(n + 1) * k, :].rearrange("(p t) d -> p (t d)", p=P),
                                 zeros).then_inc(sc_zero, 16)
            sp.wait_ge(sc_zero, 96)
            sp.dma_start(pj_raw, a["pj"]).then_inc(ld_pj, 16)
            sp.wait_ge(pj_done, 1)
            sp.dma_start(moe_w[:, RAW_SLOT * WE:(RAW_SLOT + 1) * WE], a["moe_w"][:, RAW_SLOT]).then_inc(ld_moe5, 16)
            sp.wait_ge(ff_res, GROUPS)
            for e in (DIAG_SLOT, *range(RAW_SLOT + 1, E)):
                sp.dma_start(moe_w[:, e * WE:(e + 1) * WE], a["moe_w"][:, e]).then_inc(ld_moe467, 16)

            sp.dma_start(b2[:, :], a["b2"]).then_inc(ld_b2, 16)

            def rows_in(i, par):
                wait(sp, mo_xTps, i - 1)
                sp.dma_start(xt[par], xs[bass.ds(i * P, P), :]).then_inc(mo_xin[par], 16)

            def rows_out(i, par):
                sp.wait_ge(mo_y, i + 1)
                sp.dma_start(ys[bass.ds(i * P, P), :], ysb[par]).then_inc(mo_yout[par], 16)

            sp.wait_ge(sc_rows, 16 * TILES)
            rows_in(0, 0)
            rows_in(1, 1)
            with sp.Fori(0, MAX_TILES // 2 - 1) as i:
                for par in range(2):
                    rows_in(2 * i + 2 + par, par)
                    rows_out(2 * i + par, par)
            rows_out(MAX_TILES - 2, 0)
            rows_out(MAX_TILES - 1, 1)
            for lo in range(ON_POOL, TILES, 3):
                hi = min(lo + 3, TILES)
                sp.wait_ge(fin_add, hi - ON_POOL)
                sp.dma_start(out[lo * P:hi * P, :].rearrange("(t p) d -> p t d", p=P), tm[:, lo:hi]
                             ).then_inc(fin_out, 16)
            sp.wait_ge(fin_out, 16 * len(range(ON_POOL, TILES, 3)))
            sp.wait_ge(mo_yout[0], 16 * MAX_TILES // 2)
            sp.wait_ge(mo_yout[1], 16 * MAX_TILES // 2)

        @block.gpsimd
        def _(gp):
            gp.iota(gidx, [[1, NTXT]], base=0, channel_multiplier=0,
                    allow_small_or_imprecise_dtypes=True).then_inc(iotas, 1)
            gp.iota(base.rearrange("p (b s) -> p b s", b=B), [[S_TXT, B], [0, S_TXT]], base=0,
                    channel_multiplier=0, allow_small_or_imprecise_dtypes=True).then_inc(iotas, 1)
            gp.iota(pid[:, :], [[0, 1]], base=0, channel_multiplier=1,
                    allow_small_or_imprecise_dtypes=True).then_inc(iotas, 1)
            gp.memset(ident[:, :], 0.0).then_inc(consts, 1)
            gp.memset(onesf[:, :], 1.0).then_inc(consts, 1)
            gp.memset(neg_half[:, :], -0.5).then_inc(consts, 1)
            gp.memset(hmask[:, :], 1.0).then_inc(consts, 1)
            gp.memset(cmask[:, :], 1.0).then_inc(consts, 1)
            gp.wait_ge(consts, 5)
            gp.affine_select(out=ident[:, :], in_=ident[:, :], compare_op=ALU.not_equal, fill=1.0,
                             base=0, pattern=[[-1, P]], channel_multiplier=1).then_inc(consts, 1)
            gp.affine_select(out=cmask[:, :], in_=cmask[:, :], compare_op=ALU.is_ge, fill=0.0,
                             base=0, pattern=[[1, S]], channel_multiplier=-1).then_inc(consts, 1)
            gp.affine_select(out=hmask[:, :], in_=hmask[:, :], compare_op=ALU.is_ge, fill=0.0,
                             base=0, pattern=[[-DH, HC]], channel_multiplier=1).then_inc(consts, 1)
            gp.wait_ge(consts, 8)
            gp.affine_select(out=hmask[:, :], in_=hmask[:, :], compare_op=ALU.is_ge, fill=0.0,
                             base=DH - 1, pattern=[[DH, HC]], channel_multiplier=-1).then_inc(consts, 1)
            gp.tensor_copy(identb[:, :], ident[:, :]).then_inc(consts, 1)

            def past(gp):
                gp.sem_inc(pool_past, 1)

            def ln_rstd_all(k):
                for part, (lo, hi) in enumerate(PARTS):
                    n = 2 * k + part + 1
                    gp.wait_ge(ln_mv, n)
                    if k == 0:
                        gp.tensor_scalar(ve[:, lo:hi], var[:, lo:hi], 1.0 + EPS, EPS * EPS,
                                         ALU.mult, ALU.add).then_inc(ln_ve, 1)
                    else:
                        gp.tensor_scalar(ve[:, lo:hi], var[:, lo:hi], EPS, None, ALU.add).then_inc(ln_ve, 1)
                    gp.wait_ge(ln_ve, n)
                    gp.tensor_tensor(rstd[:, lo:hi], ve[:, lo:hi], neg_half[:, lo:hi], ALU.pow).then_inc(ln_rstd, 1)

            ln_rstd_all(0)

            for par in range(2):
                gp.memset(vaug[par][:, :, DH:DH + 1], 1.0).then_inc(at_ones, 1)

            def y_slice(b, q, turn):
                wait(gp, at_vps, b - 3)
                gp.tensor_copy(yst[q], yT[:, :, bass.ds(b * S, S)]).then_inc(at_y, 1)

            def weight_sums(b, q, turn):
                if isinstance(b, int) and b == 2:
                    for n in range(2):
                        gp.wait_ge(wq_abs, n + 1)
                        gp.partition_all_reduce(wsum[:, 2 + n:3 + n], w1m[:, n:n + 1], P,
                                                RED.add).then_inc(wq_sum, 1)

            def subtract_max(b, q, turn):
                gp.wait_ge(at_mx, b + 1)
                gp.tensor_tensor(sx[q % 2], sx[q % 2], mx[q % 2].unsqueeze(2).to_broadcast([S, H, S]),
                                 ALU.subtract).then_inc(at_sub, 1)

            gp.wait_ge(ln_out, LN_STEPS)
            batches(gp, {"y": y_slice, "sub": subtract_max, "weights": weight_sums},
                    [("y", 0), ("sub", 3), ("weights", 0)])

            gp.wait_ge(wq_done, 2)
            gp.memset(zeros, 0.0).then_inc(st_zero, 1)
            gp.wait_ge(ld_ff, 32)
            gp.wait_ge(at_pbd, 2)
            for n, j in enumerate(PE_CHUNKS):
                for k in range(3):
                    ins = gp.tensor_scalar(diag[:, n, k], ident[:, :], convw[:, 3 * j + k:3 * j + k + 1], None,
                                           ALU.mult)
            ins.then_inc(ff_diag, 1)

            ln_rstd_all(1)

            def step_diagonal(u, par, n):
                wait(gp, q_bps, u - 1)
                past(gp)
                for m in range(n):
                    ins = gp.tensor_tensor(stage[par][:, m * P:(m + 1) * P], ident[:, :],
                                           qstep[:, bass.ds(2 * u + m, 1)].to_broadcast([P, P]), ALU.mult)
                ins.then_inc(q_diag, 1)

            gp.wait_ge(q_step, 1)
            gp.wait_ge(ln_tokps, 2 * LN_STEPS)
            pairs_then_last(gp, step_diagonal, step_diagonal)

            for u in uu:
                gp.memset(u[:, :, 0:1], 0.0)
                gp.memset(u[:, :, S + 1:S + 2], 0.0).then_inc(ff_pad, 1)

            def quantise(g, par):
                gp.wait_ge(ff_am, g + 1)
                wait(gp, ff_fo, g - 1)
                past(gp)
                gp.partition_all_reduce(mr[par], am[par], P, RED.absmax).then_inc(ff_red, 1)
                gp.wait_ge(ff_red, g + 1)
                past(gp)
                gp.tensor_scalar(mr[par], mr[par], EPS, 1.0 / 127.0, ALU.max, ALU.mult).then_inc(ff_mr, 1)
                if isinstance(g, int) and g == GROUPS - 1:
                    return
                gp.wait_ge(ff_mi, g + 1)
                gp.tensor_tensor(sv[par], sv[par], mi[par].unsqueeze(1).to_broadcast([P, FJ, GN]),
                                 ALU.mult).then_inc(ff_mul, 1)

            def ff_add(g, par):
                gp.wait_ge(ff_fo, g + 1)
                gp.tensor_tensor(hT[:, :, bass.ds(g * GN, GN)], hT[:, :, bass.ds(g * GN, GN)], fo[par],
                                 ALU.add).then_inc(ff_res, 1)
                gp.wait_ge(ff_res, g + 1)
                gp.sem_inc(ff_fo_free, 1)

            gp.sem_inc(ff_fo_free, 2)
            quantise(0, 0)

            def two_groups(i):
                quantise(2 * i + 1, 1)
                ff_add(2 * i, 0)
                quantise(2 * i + 2, 0)
                ff_add(2 * i + 1, 1)

            two_groups(0)
            with gp.Fori(1, GROUPS // 2 - 1) as i:
                two_groups(i)
            quantise(GROUPS - 1, 1)
            ff_add(GROUPS - 2, 0)
            ff_add(GROUPS - 1, 1)

            ln_rstd_all(2)

            ln_rstd_all(3)

            gp.wait_ge(rt_lg, LN_STEPS)
            gp.iota(rev, [[-1, E]], base=E, channel_multiplier=0,
                    allow_small_or_imprecise_dtypes=True).then_inc(rt_c, 1)
            gp.iota(thr, [[0, E], [P, TILES]], base=0, channel_multiplier=0,
                    allow_small_or_imprecise_dtypes=True).then_inc(rt_c, 1)
            gp.iota(it24, [[1, MAX_TILES], [0, E]], base=0, channel_multiplier=0,
                    allow_small_or_imprecise_dtypes=True).then_inc(rt_c, 1)
            gp.memset(onesb, 1.0).then_inc(rt_c, 1)
            gp.wait_ge(rt_c, 4)
            gp.affine_select(out=triu, in_=onesb, compare_op=ALU.is_gt, fill=0.0, base=0,
                             pattern=[[1, P]], channel_multiplier=-1).then_inc(rt_c, 1)

            gp.wait_ge(rt_pos, 1)
            gp.wait_ge(z_kept, LN_STEPS)
            gp.wait_ge(sc_zero, 96)
            for t in range(TILES):
                gp.indirect_dma_start(xs, bass.IndirectOffsetOnAxis(ap=posu[:, t:t + 1], axis=0),
                                      z3[:, t], None).then_inc(sc_rows, 16)

            gp.wait_ge(rt_te, 1)
            gp.wait_ge(sc_rows, 16 * TILES)
            counts = [gp.value_load(used[0:1, par:par + 1], min_val=16 * (TILES // 2), max_val=8 * MAX_TILES)
                      for par in range(2)]
            for par in range(2):
                gp.wait_ge(mo_yout[par], counts[par])
            past(gp)
            for t in range(TILES):
                wait(gp, fin_in[t % GATH], 16 * (t // GATH))
                gp.indirect_dma_start(fg[:, t], None, ys,
                                      bass.IndirectOffsetOnAxis(ap=posu[:, t:t + 1], axis=0)
                                      ).then_inc(fin_in[t % GATH], 16)
            for t in range(ON_POOL):
                gp.wait_ge(fin_in[t % GATH], 16 * (t // GATH + 1))
                gp.tensor_tensor(tm[:, t], tm[:, t], fg[:, t], ALU.add).then_inc(fin_pool, 1)
                if t % 4 == 3:
                    gp.wait_ge(fin_pool, t + 1)
                    gp.dma_start(out[(t - 3) * P:(t + 1) * P, :].rearrange("(t p) d -> p t d", p=P),
                                 tm[:, t - 3:t + 1]).then_inc(fin_pool_out, 16)
            gp.wait_ge(fin_pool_out, 16 * (ON_POOL // 4))

        @block.scalar
        def _(act):
            act.dma_start(tok_i, a["x_txt"]).then_inc(ld_txt, 16)
            act.dma_start(tab, a["table"]).then_inc(ld_emb, 16)
            act.dma_start(wp_bd, a["wp"]).then_inc(ld_pe, 16)
            act.dma_start(pe_bd, a["pe_bd"]).then_inc(ld_pe, 16)
            for m in range(4):
                c, half = m // 2, m % 2
                act.wait_ge(txt_mm, m + 1)
                dst = hT[:, c].rearrange("p (b s) -> p b s", s=S)[:, half * B // 2:(half + 1) * B // 2, S_IMG:S]
                act.activation(dst, ps[:, 4 + m, 0:PSUM_W].rearrange("p (b s) -> p b s", s=S_TXT),
                               ACT.Copy).then_inc(txt_out, 1)
            for c in range(C):
                act.wait_ge(at_pbps, c + 1)
                act.activation(pbd[:, c], ps[:, 4 + c, 0:HC * SP1], ACT.Copy).then_inc(at_pbd, 1)

            def evac_tok(k):
                def step(u, par, n):
                    g = k * LN_STEPS + u
                    act.wait_ge(ln_tokps, g + 1)
                    act.activation(tm_t[:, bass.ds(u * 2 * D, n * D)], tokps(par)[:, 0:n * D],
                                   ACT.Copy).then_inc(ln_tok, 1)
                pairs_then_last(act, step, step)

            def evac_zT(k):
                def step(u, par, n):
                    g = k * LN_STEPS + u
                    act.wait_ge(ln_zT, g + 1)
                    w = n * P
                    if k == 0:
                        for c in range(C):
                            ins = act.activation(yT[:, c, bass.ds(u * 2 * P, w)], zTps(par)[:, c * w:(c + 1) * w],
                                                 ACT.Identity, bias=beta[:, c:c + 1], scale=gamma[:, c:c + 1])
                    elif k == 1:
                        src = zTps(par).bitcast(BF16)[:, 0:C * w].rearrange("p (c n) -> p c n", c=C)
                        act.activation(ziT[:, :, bass.ds(u * 2 * P, w)], src, ACT.Copy)
                        act.wait_ge(q_bps, u + 1)
                        ins = act.activation(rsb[:, bass.ds(u * 2 * P, w)], ps[:, 4 + par, 0:w], ACT.Copy,
                                             scale=w1m[:, 0:1])
                    elif k == 2:
                        src = zTps(par)[:, 0:C * w].rearrange("p (c n) -> p c n", c=C)
                        ins = act.activation(yT[:, :, bass.ds(u * 2 * P, w)], src, ACT.Copy)
                    else:
                        wait(act, rt_lgps, u - 1)
                        src = zTps(par)[:, 0:C * w].rearrange("p (c n) -> p c n", c=C)
                        ins = act.activation(zTs[par][:, :, 0:w], src, ACT.Copy)
                    ins.then_inc(ln_out, 1)
                    if k == 3:
                        act.activation(hT_t[:, bass.ds(u * 2 * D, n * D)], z[par][:, 0:n * D],
                                       ACT.Copy).then_inc(z_kept, 1)
                pairs_then_last(act, step, step)

            act.wait_ge(ld_ln, 32)
            act.wait_ge(emb_out, EG * C)
            evac_tok(0)
            evac_zT(0)

            def exps(b, q, turn):
                act.wait_ge(at_sub, b + 1)
                wait(act, at_pTps, b - 1)
                act.activation(pr[q % 2], sx[q % 2], ACT.Exp, scale=1.0 / D ** 0.5).then_inc(at_p, 1)

            def evac_v(b, q, turn):
                act.wait_ge(at_vps, b + 1)
                wait(act, at_ctxps, b - 1)
                act.activation(vaug[q % 2][:, :, 0:DH], ps[0:S, 1, 0:D].rearrange("p (h d) -> p h d", h=H),
                               ACT.Copy).then_inc(at_v, 1)

            def evac_ctxT(b, q, turn):
                act.wait_ge(at_ctxTps, b + 1)
                wait(act, at_wops, b)
                act.activation(ctxT, ps[:, 0, 0:C * S].rearrange("p (c n) -> p c n", c=C), ACT.Identity,
                               bias=bv0[:, 0:1]).then_inc(at_ctxT, 1)

            def evac_pT(b, q, turn):
                act.wait_ge(at_pTps, b + 1)
                wait(act, at_ctxps, b)
                act.activation(prT.rearrange("p (a h) c -> p a (h c)", a=C), ps[0:S, 6:8, 0:HC * S],
                               ACT.Copy).then_inc(at_pT, 1)

            def evac_pos(b, q, turn):
                act.wait_ge(at_posps, b + 1)
                wait(act, at_out[q % 2], 16 * turn)
                act.activation(posp[q % 2], ps[0:S, 2:4, 0:HC * SP1], ACT.Copy).then_inc(at_posp, 1)

            act.wait_ge(ld_at, 160)
            batches(act, {"exp": exps, "v": evac_v, "ctxT": evac_ctxT, "pT": evac_pT, "pos": evac_pos},
                    [("exp", 4), ("pT", 4), ("v", 4), ("ctxT", LAG), ("pos", 1)])

            evac_tok(1)
            evac_zT(1)

            def tap_mid(g, j):
                act.wait_ge(ff_u, g * FJ + j + 1)
                wait(act, ff_s, (g - 1) * FJ + j + 1)
                act.activation(tt[j], uu[j % 4][:, :, 1:S + 1], ACT.Identity, bias=convb[:, j:j + 1],
                               scale=convw[:, 3 * j + 1:3 * j + 2]).then_inc(ff_t1, 1)

            def silu(g, gpar, j):
                if j == 0:
                    wait(act, ff_si, g - 1)
                dst = sv[gpar]
                if j in PE_CHUNKS:
                    act.wait_ge(ff_cv, on_pe(g, j))
                    src = ps[:, PE_BANKS[PE_CHUNKS.index(j)], 0:GN]
                    act.activation(dst[:, j], src, ACT.Silu, bias=convb[:, j:j + 1]).then_inc(ff_s, 1)
                else:
                    act.wait_ge(ff_t3, on_dve(g, j))
                    act.activation(dst[:, j].rearrange("p (b s) -> p b s", b=GB), tt[j],
                                   ACT.Silu).then_inc(ff_s, 1)

            def ff_group(g, gpar):
                for j in range(FJ + SILU_LAG):
                    if j < FJ and j not in PE_CHUNKS:
                        tap_mid(g, j)
                    if j >= SILU_LAG:
                        silu(g, gpar, j - SILU_LAG)

            act.wait_ge(ld_ff, 32)
            ff_group(0, 0)
            ff_group(1, 1)
            with act.Fori(1, GROUPS // 2) as i:
                ff_group(2 * i, 0)
                ff_group(2 * i + 1, 1)

            evac_tok(2)
            evac_zT(2)

            def evac_q7(g, par):
                act.wait_ge(a1_qps, g + 1)
                wait(act, a1_wps, g - 1)
                act.activation(q7[par], ps[0:HS, 0, 0:GN], ACT.Identity, bias=bq1[:, 0:1]).then_inc(a1_q, 1)

            def evac_k7(g, par):
                act.wait_ge(a1_kps, g + 1)
                act.activation(k7[par], ps[0:HS, 1, 0:GN], ACT.Identity, bias=bk1[:, 0:1]).then_inc(a1_k, 1)

            def evac_o7(g, par):
                act.wait_ge(a1_ops, g + 1)
                act.activation(o7[par], ps[0:HS, 4, 0:GN], ACT.Copy).then_inc(a1_o, 1)

            act.wait_ge(ld_a1, 80)
            evac_q7(0, 0)
            evac_k7(0, 0)
            evac_q7(1, 1)
            evac_o7(0, 0)
            evac_k7(1, 1)
            with act.Fori(1, GROUPS // 2) as i:
                for par in range(2):
                    evac_q7(2 * i + par, par)
                    evac_o7(2 * i + par - 1, 1 - par)
                    evac_k7(2 * i + par, par)
            evac_o7(GROUPS - 1, 1)

            evac_tok(3)
            evac_zT(3)

            def evac_x(i, par):
                act.wait_ge(mo_xTps, i + 1)
                wait(act, mo_h1ps, i - 1)
                act.activation(xT[par], ps[:, 6 + par, 0:D], ACT.Copy).then_inc(mo_xT, 1)

            def evac_h(i, par):
                act.wait_ge(mo_h1ps, i + 1)
                wait(act, mo_hTps, i)
                act.activation(h1[:, 0:PSUM_W], ps[:, 0, :], ACT.Copy).then_inc(mo_h1a, 1)

            def relu_a(i, par):
                act.wait_ge(mo_hTps, i + 1)
                act.wait_ge(mo_b1, i + 1)
                for j in range(FJ // 2):
                    ins = act.activation(hTm[:, j], ps[:, 2, j * P:(j + 1) * P], ACT.Relu,
                                         bias=b1s[par][:, j:j + 1])
                ins.then_inc(mo_hTa, 1)

            def expert_step(i, par, more=True):
                evac_h(i, par)
                if more:
                    evac_x(i + 1, 1 - par)
                relu_a(i, par)

            evac_x(0, 0)
            expert_step(0, 0)
            expert_step(1, 1)
            with act.Fori(1, MAX_TILES // 2 - 1) as i:
                expert_step(2 * i, 0)
                expert_step(2 * i + 1, 1)
            expert_step(MAX_TILES - 2, 0)
            expert_step(MAX_TILES - 1, 1, more=False)

        @block.vector
        def _(dve):
            n = [0]

            def step(ins):
                n[0] += 1
                ins.then_inc(txt_step, 1)

            def after_step():
                dve.wait_ge(txt_step, n[0])

            dve.wait_ge(ld_txt, 16)
            dve.wait_ge(iotas, 3)
            step(dve.tensor_copy(tokf, tok_i))
            after_step()
            step(dve.scalar_tensor_tensor(sepv, tokf, 4.0, gidx, ALU.is_equal, ALU.mult))
            step(dve.tensor_scalar(padv, gidx, 1.0, None, ALU.add))
            after_step()
            step(dve.tensor_tensor(sepv, sepv, base, ALU.max))
            step(dve.scalar_tensor_tensor(padv, tokf, 1.0, padv, ALU.is_equal, ALU.mult))
            after_step()
            step(dve.tensor_tensor_scan(runs, sepv, sepv, 0.0, ALU.max, ALU.max))
            step(dve.tensor_tensor_scan(runp, padv, padv, 0.0, ALU.max, ALU.max))
            after_step()
            step(dve.tensor_tensor(runs, gidx, runs, ALU.subtract))
            step(dve.tensor_tensor(runp, runp, base, ALU.is_le))
            after_step()
            step(dve.scalar_tensor_tensor(runs, runs, 1.0, runp, ALU.add, ALU.mult))
            after_step()
            step(dve.tensor_scalar(sepv, runs, 1.0, pid[0:TAB, 0:1], ALU.add, ALU.is_equal))

            dve.wait_ge(ld_emb, 64)
            for c in range(C):
                ins = dve.tensor_scalar(posb[:, c], posb[:, c], bproj[:, c:c + 1], None, ALU.add)
            ins.then_inc(posb_ok, 1)
            dve.wait_ge(posb_ok, 1)
            for g in range(EG):
                for c in range(C):
                    m = g * C + c
                    dve.wait_ge(emb_mm, m + 1)
                    nb = B // EG
                    dst = hT[:, c].rearrange("p (b s) -> p b s", s=S)[:, g * nb:(g + 1) * nb, 0:S_IMG]
                    dve.tensor_tensor(dst, ps[:, m % 4, 0:EGN].rearrange("p (b s) -> p b s", s=S_IMG),
                                      posb[:, c:c + 1, :].to_broadcast([P, nb, S_IMG]),
                                      ALU.add).then_inc(emb_out, 1)

            def ternary_part(b, q, turn):
                if not isinstance(b, int):
                    return
                n = b % 2
                raw, wi_n = ((w1raw, w1i), (w2raw, w2i))[n]
                if b == 0:
                    dve.wait_ge(ld_w12, 32)
                if b < 2:
                    dve.tensor_reduce(w1m[:, n:n + 1], raw, AX.X, ALU.add,
                                      apply_absolute_value=True).then_inc(wq_abs, 1)
                elif b == 2:
                    dve.wait_ge(wq_sum, 2)
                    dve.tensor_scalar(w1m[:, :], wsum[:, 2:4], 1.0 / (D * FF), EPS, ALU.mult,
                                      ALU.max).then_inc(wq_mean, 1)
                    dve.wait_ge(wq_mean, 1)
                    dve.reciprocal(wsum[:, 0:2], w1m[:, :]).then_inc(wq_inv, 1)
                elif b == 3:
                    dve.wait_ge(wq_inv, 1)
                    for n, raw in enumerate((w1raw, w2raw)):
                        dve.tensor_scalar(raw, raw, wsum[:, n:n + 1], MAGIC, ALU.mult, ALU.add).then_inc(wq_a, 1)
                elif b in (4, 5):
                    dve.wait_ge(wq_a, n + 1)
                    dve.tensor_scalar(raw, raw, -MAGIC, -1.0, ALU.add, ALU.max).then_inc(wq_b, 1)
                elif b in (6, 7):
                    dve.wait_ge(wq_b, n + 1)
                    dve.tensor_scalar(wi_n, raw, 1.0, None, ALU.min).then_inc(wq_done, 1)

            def stage_in(k, u, par, n):
                g = k * LN_STEPS + u
                wait(dve, ln_tokps, g - 1)
                dve.tensor_copy(stage[par][:, 0:n * D].rearrange("p (c n) -> p c n", c=C),
                                hT[:, :, bass.ds(u * 2 * P, n * P)]).then_inc(ln_staged, 1)

            def stats(k, u, par, n):
                g = k * LN_STEPS + u
                dve.wait_ge(ln_tok, g + 1)
                for m in range(n):
                    ins = dve.bn_stats(bn[:, bass.ds((2 * u + m) * 6, 6)],
                                       tm_t[:, bass.ds((2 * u + m) * D, D)])
                ins.then_inc(ln_bn, 1)

            def moments(k, part):
                lo, hi = PARTS[part]
                b, m = bnv[:, lo:hi], bsum[:, :, lo:hi]
                n = 2 * (2 * k + part)
                dve.wait_ge(ln_bn, k * LN_STEPS + (HALF, LN_STEPS)[part])
                dve.tensor_tensor(m[:, 0], b[:, :, 2], b[:, :, 5], ALU.add)
                dve.tensor_tensor(m[:, 1], b[:, :, 1], b[:, :, 4], ALU.subtract)
                dve.tensor_tensor(m[:, 2], b[:, :, 1], b[:, :, 4], ALU.add).then_inc(ln_ba, 1)
                dve.wait_ge(ln_ba, n + 1)
                dve.scalar_tensor_tensor(m[:, 3], m[:, 1], 0.25, m[:, 1], ALU.mult, ALU.mult)
                dve.tensor_scalar(mean[:, lo:hi], m[:, 2], 0.5, None, ALU.mult).then_inc(ln_ba, 1)
                dve.wait_ge(ln_ba, n + 2)
                dve.scalar_tensor_tensor(var[:, lo:hi], m[:, 0], 1.0 / D, m[:, 3], ALU.mult,
                                         ALU.add).then_inc(ln_mv, 1)

            def gather_stats(k):
                stage_in(k, 0, 0, 2)
                stage_in(k, 1, 1, 2)
                for u in (2, 3):
                    stage_in(k, u, u % 2, 2)
                    stats(k, u - 2, u % 2, 2)
                with dve.Fori(2, PAIRS // 2) as i:
                    for par in range(2):
                        stage_in(k, 2 * i + par, par, 2)
                        stats(k, 2 * i + par - 2, par, 2)
                moments(k, 0)
                stage_in(k, PAIRS, 0, 1)
                stats(k, PAIRS - 2, 0, 2)
                stats(k, PAIRS - 1, 1, 2)
                stats(k, PAIRS, 0, 1)
                moments(k, 1)

            def normalise(k):
                def step(u, par, n):
                    g = k * LN_STEPS + u
                    wait(dve, ln_zT, g - 1)
                    if k == 3:
                        wait(dve, z_kept, u - 1)
                    for m in range(n):
                        t = 2 * u + m
                        dst = z[par][:, m * D:(m + 1) * D]
                        ins = dve.tensor_scalar(dst, tm_t[:, bass.ds(t * D, D)], mean[:, bass.ds(t, 1)],
                                                rstd[:, bass.ds(t, 1)], ALU.subtract, ALU.mult)
                    ins.then_inc(ln_z, 1)
                dve.wait_ge(ln_rstd, 2 * k + 1)
                step(0, 0, 2)
                step(1, 1, 2)
                with dve.Fori(1, HALF // 2) as i:
                    step(2 * i, 0, 2)
                    step(2 * i + 1, 1, 2)
                dve.wait_ge(ln_rstd, 2 * k + 2)
                for u in range(HALF, LN_STEPS):
                    step(u, u % 2, 2 if u < PAIRS else 1)

            dve.wait_ge(txt_out, 4)
            dve.wait_ge(emb_out, EG * C)
            gather_stats(0)
            normalise(0)
            dve.wait_ge(ld_at, 160)
            dve.tensor_scalar(bqu[:, :], bqu[:, :], wsum[:, 0:1], None, ALU.add)
            dve.tensor_scalar(bqv[:, :], bqv[:, :], wsum[:, 0:1], None, ALU.add).then_inc(at_bias, 1)
            dve.wait_ge(at_bias, 1)

            def norm_ctx(b, q, turn):
                dve.wait_ge(at_ctxps, b + 1)
                wait(dve, at_ctxTps, b)
                c_ps = ps[0:S, 1, 0:H * (DH + 1)].rearrange("p (h d) -> p h d", h=H)
                dve.reciprocal(rz, c_ps[:, :, DH]).then_inc(at_rz, 1)
                dve.wait_ge(at_rz, b + 1)
                dve.tensor_tensor(ctxn, c_ps[:, :, 0:DH], rz.unsqueeze(2).to_broadcast([S, H, DH]),
                                  ALU.mult).then_inc(at_ctx, 1)

            def evac_qk(b, q, turn):
                dve.wait_ge(at_qkps, b + 1)
                wait(dve, at_cps, b - 3)
                wait(dve, at_posps, b)
                q_ps = ps[:, 0, 0:C * S].rearrange("p (c n) -> p c n", c=C)
                dve.tensor_tensor(qv, q_ps, bqv[:, :].unsqueeze(2).to_broadcast([P, C, S]), ALU.add)
                dve.tensor_tensor(qu[q], q_ps, bqu[:, :].unsqueeze(2).to_broadcast([P, C, S]), ALU.add)
                for c in range(C):
                    k_ps = ps[:, 0, (C + c) * S:(C + c + 1) * S]
                    ins = dve.scalar_tensor_tensor(
                        kbd[q][:, c].rearrange("p (h n) -> p h n", h=HC),
                        k_ps.unsqueeze(1).to_broadcast([P, HC, S]), bk0[:, 0:1],
                        hmask[:, :].unsqueeze(2).to_broadcast([P, HC, S]), ALU.add, ALU.mult)
                ins.then_inc(at_qkv, 1)

            def add_scores(b, q, turn):
                par = q % 2
                dve.wait_ge(at_cps, b + 1)
                dve.wait_ge(at_in[par], 16 * turn + 16)
                wait(dve, at_p, b - 1)
                dve.tensor_tensor(sx[par].rearrange("p (a h) c -> p a (h c)", a=C), ps[0:S, 4:6, 0:HC * S],
                                  poss[par], ALU.add).then_inc(at_s, 1)
                dve.wait_ge(at_s, b + 1)
                dve.tensor_reduce(mx[par], sx[par], AX.X, ALU.max).then_inc(at_mx, 1)

            def add_res(b, q, turn):
                dve.wait_ge(at_wops, b + 1)
                for c in range(C):
                    dst = hT[:, c, bass.ds(b * S, S)]
                    ins = dve.scalar_tensor_tensor(dst, ps[:, 0, (C + c) * S:(C + c + 1) * S], bo0[:, c:c + 1],
                                                   dst, ALU.add, ALU.add)
                ins.then_inc(at_res, 1)

            dve.wait_ge(consts, 10)
            batches(dve, {"norm": norm_ctx, "qk": evac_qk, "add": add_scores, "res": add_res,
                          "ternary": ternary_part},
                    [("norm", LAG), ("qk", 1), ("add", 3), ("res", LAG), ("ternary", 0)])

            dve.wait_ge(at_res, B)
            gather_stats(1)
            dve.wait_ge(ln_rstd, 3)
            def z_tiles(i, n):
                for m in range(n):
                    t = 4 * i + m
                    x = tm_t[:, bass.ds(t * D, D)]
                    dve.tensor_scalar(x, x, mean[:, bass.ds(t, 1)], rstd[:, bass.ds(t, 1)],
                                      ALU.subtract, ALU.mult).then_inc(q_z, 1)

            with dve.Fori(0, HALF // 2) as i:
                z_tiles(i, 4)
            dve.wait_ge(ln_rstd, 4)
            z_tiles(HALF // 2, 4)
            z_tiles(TILES // 4, TILES % 4)
            dve.wait_ge(q_z, TILES)
            dve.tensor_reduce(amax[:, :], tm, AX.X, ALU.max, apply_absolute_value=True).then_inc(q_amax, 1)
            dve.wait_ge(q_amax, 1)
            dve.tensor_scalar(qstep[:, :], amax[:, :], EPS, 1.0 / 127.0, ALU.max, ALU.mult).then_inc(q_step, 1)
            dve.wait_ge(q_step, 1)
            dve.reciprocal(qinv[:, :], qstep[:, :]).then_inc(q_inv, 1)
            dve.wait_ge(q_inv, 1)

            def quant_step(u, par, n):
                g = LN_STEPS + u
                for m in range(n):
                    t = 2 * u + m
                    x = tm_t[:, bass.ds(t * D, D)]
                    ins = dve.tensor_scalar(x, x, qinv[:, bass.ds(t, 1)], MAGIC, ALU.mult, ALU.add)
                ins.then_inc(q_mul, 1)
                wait(dve, ln_zT, g - 1)
                dve.wait_ge(q_mul, u + 1)
                dve.tensor_scalar(zb[par][:, 0:n * D], tm_t[:, bass.ds(u * 2 * D, n * D)], -MAGIC, None,
                                  ALU.add).then_inc(ln_z, 1)

            dve.wait_ge(ln_tokps, 2 * LN_STEPS)
            pairs_then_last(dve, quant_step, quant_step)

            def dequant(g, j):
                dve.wait_ge(ff_mm, g * FJ + j + 1)
                bg, bj = (g, j - 4) if j >= 4 else (g - 1, j - 4 + FJ)
                if bj in PE_CHUNKS:
                    wait(dve, ff_cv, on_pe(bg, bj))
                else:
                    wait(dve, ff_t3, on_dve(bg, bj))
                dve.tensor_tensor(uu[j % 4][:, :, 1:S + 1], ps[:, UP_BANKS[j % 4], 0:GN].rearrange("p (b s) -> p b s", b=GB),
                                  rsb[:, bass.ds(g * GN, GN)].rearrange("p (b s) -> p b s", b=GB),
                                  ALU.mult).then_inc(ff_u, 1)

            def taps(g, j):
                n = on_dve(g, j)
                dve.wait_ge(ff_t1, n)
                dve.scalar_tensor_tensor(tt[j], uu[j % 4][:, :, 0:S], convw[:, 3 * j:3 * j + 1], tt[j],
                                         ALU.mult, ALU.add).then_inc(ff_t2, 1)
                dve.wait_ge(ff_t2, n)
                dve.scalar_tensor_tensor(tt[j], uu[j % 4][:, :, 2:S + 2], convw[:, 3 * j + 2:3 * j + 3], tt[j],
                                         ALU.mult, ALU.add).then_inc(ff_t3, 1)

            def largest(g, gpar):
                dve.wait_ge(ff_s, (g + 1) * FJ)
                dve.tensor_reduce(am[gpar], sv[gpar].rearrange("p j n -> p n j"), AX.X, ALU.max,
                                  apply_absolute_value=True).then_inc(ff_am, 1)

            def invert(g, gpar):
                dve.wait_ge(ff_mr, g + 1)
                dve.reciprocal(mi[gpar], mr[gpar]).then_inc(ff_mi, 1)

            def round_si(g, gpar):
                dve.wait_ge(ff_mul, g + 1)
                wait(dve, ff_ops, g)
                dve.tensor_scalar(si, sv[gpar], MAGIC, -MAGIC, ALU.add, ALU.add).then_inc(ff_si, 1)

            def ff_out(g, gpar):
                dve.wait_ge(ff_ops, g + 1)
                wait(dve, ff_fo_free, g + 1)
                for c in range(C):
                    ins = dve.scalar_tensor_tensor(fo[gpar][:, c], ps[:, 4 + c, 0:GN], w1m[:, 1:2], mr[gpar],
                                                   ALU.mult, ALU.mult)
                ins.then_inc(ff_fo, 1)

            def ff_group(g, gpar):
                for j in range(FJ + TAPS_LAG):
                    if j < FJ:
                        dequant(g, j)
                    if TAPS_LAG <= j and j - TAPS_LAG not in PE_CHUNKS:
                        taps(g, j - TAPS_LAG)
                    if j == ROUND_AT and (not isinstance(g, int) or g > 1):
                        round_si(g - 2, gpar)
                    if j == LARGEST_AT and (not isinstance(g, int) or g > 0):
                        largest(g - 1, 1 - gpar)
                    if j == OUT_AT and (not isinstance(g, int) or g > 1):
                        ff_out(g - 2, gpar)
                    if j == INVERT_AT and (not isinstance(g, int) or g > 0):
                        invert(g - 1, 1 - gpar)

            dve.wait_ge(ln_out, 2 * LN_STEPS)
            dve.wait_ge(ff_pad, len(UP_BANKS))
            for g in range(4):
                ff_group(g, g % 2)
            with dve.Fori(2, GROUPS // 2) as i:
                ff_group(2 * i, 0)
                ff_group(2 * i + 1, 1)
            def pair_in(*us):
                for u in us:
                    stage_in(2, u, u % 2, 2 if u < PAIRS else 1)

            def pair_stats(*us):
                for u in us:
                    stats(2, u, u % 2, 2 if u < PAIRS else 1)

            round_si(GROUPS - 2, 0)
            largest(GROUPS - 1, 1)
            dve.wait_ge(ff_res, GROUPS - 2)
            pair_in(0, 1)
            ff_out(GROUPS - 2, 0)
            pair_in(2)
            pair_stats(0)
            pair_in(3)
            pair_stats(1)
            invert(GROUPS - 1, 1)
            dve.wait_ge(ff_mi, GROUPS)
            dve.tensor_tensor(sv[1], sv[1], mi[1].unsqueeze(1).to_broadcast([P, FJ, GN]),
                              ALU.mult).then_inc(ff_mul, 1)
            round_si(GROUPS - 1, 1)
            pair_in(4)
            pair_stats(2)
            pair_in(5)
            pair_stats(3)
            dve.wait_ge(ld_pj, 16)
            dve.tensor_reduce(pj[:, :], pj_raw, AX.X, ALU.add).then_inc(pj_done, 1)
            dve.wait_ge(ff_res, GROUPS - 1)
            pair_in(6)
            pair_stats(4)
            ff_out(GROUPS - 1, 1)
            pair_stats(5, 6)
            moments(2, 0)
            dve.wait_ge(ff_res, GROUPS)
            pair_in(7, 8)
            pair_stats(7, 8)
            moments(2, 1)
            normalise(2)

            def y_group(g, par):
                dve.tensor_copy(y7[par], yT[:, :, bass.ds(g * GN, GN)]).then_inc(a1_y, 1)

            def evac_v7(g, par):
                dve.wait_ge(a1_vps, g + 1)
                wait(dve, a1_ops, g - 1)
                dve.tensor_tensor(v7[par], ps[0:S, 2, 0:GB * HS].rearrange("p (b d) -> p b d", b=GB),
                                  bv1[:, :].unsqueeze(1).to_broadcast([S, GB, HS]), ALU.add).then_inc(a1_v, 1)

            def mask7(g, par):
                dve.wait_ge(a1_wps, g + 1)
                dve.tensor_tensor(w7[par], ps[0:S, 3, 0:GN].rearrange("p (b n) -> p b n", b=GB),
                                  cmask[:, :].unsqueeze(1).to_broadcast([S, GB, S]), ALU.mult).then_inc(a1_w, 1)

            def add7(g, par):
                dve.wait_ge(a1_pps, g + 1)
                for c in range(C):
                    dst = hT[:, c, bass.ds(g * GN, GN)]
                    ins = dve.scalar_tensor_tensor(dst, ps[:, 5 + c, 0:GN], pjb[:, c:c + 1], dst,
                                                   ALU.add, ALU.add)
                ins.then_inc(a1_res, 1)

            def step7(s, par, more=True):
                mask7(s - 1, 1 - par)
                evac_v7(s, par)
                if more:
                    y_group(s + 1, 1 - par)
                add7(s - 1, 1 - par)

            dve.wait_ge(ln_out, 3 * LN_STEPS)
            y_group(0, 0)
            y_group(1, 1)
            dve.wait_ge(ld_a1, 80)
            evac_v7(0, 0)
            step7(1, 1)
            with dve.Fori(1, GROUPS // 2 - 1) as i:
                for par in range(2):
                    step7(2 * i + par, par)
            step7(GROUPS - 2, 0)
            step7(GROUPS - 1, 1, more=False)
            mask7(GROUPS - 1, 1)
            add7(GROUPS - 1, 1)

            dve.wait_ge(a1_res, GROUPS)
            gather_stats(3)
            dve.wait_ge(ln_staged, 4 * LN_STEPS)

            normalise(3)

            dve.wait_ge(ld_rt, 48)
            dve.wait_ge(rt_lgps, LN_STEPS)
            dve.tensor_tensor(lgv, ps[:, 4, 0:TILES * E].rearrange("p (t e) -> p t e", e=E),
                              br[:, :].unsqueeze(1).to_broadcast([P, TILES, E]), ALU.add).then_inc(rt_lg, LN_STEPS)

            n[0] = 0

            def rstep(ins):
                n[0] += 1
                ins.then_inc(rt_step, 1)
                dve.wait_ge(rt_step, n[0])

            dve.wait_ge(rt_c, 5)
            dve.wait_ge(rt_lg, LN_STEPS)
            rstep(dve.tensor_reduce(rcol, lgv, AX.X, ALU.max))
            rstep(dve.tensor_tensor(rt, lgv, rcol.unsqueeze(2).to_broadcast([P, TILES, E]), ALU.is_equal))
            rstep(dve.tensor_tensor(rt, rt, rev.unsqueeze(1).to_broadcast([P, TILES, E]), ALU.mult))
            rstep(dve.tensor_reduce(rcol, rt, AX.X, ALU.max))
            rstep(dve.tensor_tensor(oh, rev.unsqueeze(1).to_broadcast([P, TILES, E]),
                                    rcol.unsqueeze(2).to_broadcast([P, TILES, E]), ALU.is_equal))
            dve.tensor_copy(ohb, oh)
            rstep(dve.tensor_reduce(cntp, oh.rearrange("p t e -> p e t"), AX.X, ALU.add))
            dve.tensor_copy(cntb, cntp).then_inc(rt_cb, 1)
            dve.wait_ge(rt_cntps, 1)
            rstep(dve.tensor_copy(nt, ps[:, 5, 0:E]))
            rstep(dve.tensor_tensor(cmp_, nt.unsqueeze(2).to_broadcast([P, E, TILES]), thr, ALU.is_gt))
            rstep(dve.tensor_reduce(nt, cmp_, AX.X, ALU.add))
            rstep(dve.tensor_tensor_scan(tend, onesf[:, 0:E], nt, 0.0, ALU.mult, ALU.add))
            rstep(dve.tensor_tensor(tst, tend, nt, ALU.subtract))
            rstep(dve.tensor_scalar(tst, tst, float(P), None, ALU.mult))
            dve.wait_ge(rt_pps, 1)
            rstep(dve.tensor_tensor(rt, ps[:, 6, 0:TILES * E].rearrange("p (t e) -> p t e", e=E),
                                    tst.unsqueeze(1).to_broadcast([P, TILES, E]), ALU.add))
            rstep(dve.tensor_tensor(rt, rt, oh, ALU.mult))
            rstep(dve.tensor_reduce(rcol, rt, AX.X, ALU.add))
            dve.tensor_copy(posu[:, :], rcol).then_inc(rt_pos, 1)
            rstep(dve.tensor_tensor(it24, it24, tend.unsqueeze(1).to_broadcast([P, MAX_TILES, E]), ALU.is_ge))
            rstep(dve.tensor_reduce(te, it24, AX.X, ALU.add))
            for par in range(2):
                rstep(dve.tensor_scalar(cntp[0:1, par:par + 1], tend[0:1, E - 1:E], 0.5, (0.25, -0.25)[par],
                                        ALU.mult, ALU.add))
            rstep(dve.tensor_scalar(cntp[0:1, 0:2], cntp[0:1, 0:2], MAGIC, -MAGIC, ALU.add, ALU.add))
            dve.tensor_scalar(used[:, :], cntp[0:1, 0:2], 16.0, None, ALU.mult)
            dve.tensor_scalar(tei[:, :], te[0:1, :], float(E - 1), None, ALU.min).then_inc(rt_te, 1)

            def evac_h(i, par):
                dve.wait_ge(mo_h1ps, i + 1)
                wait(dve, mo_hTps, i)
                dve.tensor_copy(h1[:, PSUM_W:FF], ps[:, 1, :]).then_inc(mo_h1b, 1)

            def relu_b(i, par):
                dve.wait_ge(mo_hTps, i + 1)
                dve.wait_ge(mo_b1, i + 1)
                for j in range(FJ // 2, FJ):
                    ins = dve.tensor_scalar(hTm[:, j], ps[:, 3, (j - FJ // 2) * P:(j - FJ // 2 + 1) * P],
                                            b1s[par][:, j:j + 1], 0.0, ALU.add, ALU.max)
                ins.then_inc(mo_hTb, 1)

            def out_y(i, ii, par):
                e = dve.value_load(tei[0:1, bass.ds(i, 1)], min_val=0, max_val=E - 1)
                dve.wait_ge(mo_yps, i + 1)
                wait(dve, mo_yout[par], 16 * ii)
                dve.tensor_tensor(ysb[par], ps[:, 4 + par, 0:D], b2[:, bass.ds(e * D, D)],
                                  ALU.add).then_inc(mo_y, 1)

            def bias_slice(i, par):
                e = dve.value_load(tei[0:1, bass.ds(i, 1)], min_val=0, max_val=E - 1)
                dve.tensor_copy(b1s[par], b1[:, bass.ds(e * FJ, FJ)]).then_inc(mo_b1, 1)

            dve.wait_ge(rt_te, 1)
            bias_slice(0, 0)
            bias_slice(1, 1)
            dve.wait_ge(ld_b2, 16)
            evac_h(0, 0)
            relu_b(0, 0)
            evac_h(1, 1)
            out_y(0, 0, 0)
            relu_b(1, 1)
            bias_slice(2, 0)

            def two_tiles(i):
                for par in range(2):
                    s = 2 * i + par
                    evac_h(s, par)
                    out_y(s - 1, i + par - 1, 1 - par)
                    relu_b(s, par)
                    if not isinstance(s, int) or s + 1 < MAX_TILES:
                        bias_slice(s + 1, 1 - par)

            two_tiles(1)
            with dve.Fori(2, MAX_TILES // 2 - 1) as i:
                two_tiles(i)
            two_tiles(MAX_TILES // 2 - 1)
            out_y(MAX_TILES - 1, MAX_TILES // 2 - 1, 1)

            for t in range(ON_POOL, TILES):
                dve.wait_ge(fin_in[t % GATH], 16 * (t // GATH + 1))
                dve.tensor_tensor(tm[:, t], tm[:, t], fg[:, t], ALU.add).then_inc(fin_add, 1)

        @block.tensor
        def _(pe):
            pe.wait_ge(ld_emb, 64)
            for g in range(EG):
                pe.wait_ge(ld_patch[g], 16)
                for c in range(C):
                    m = g * C + c
                    wait(pe, emb_out, m - 3)
                    for k in range(KP):
                        ins = pe.matmul(ps[:, m % 4, 0:EGN], wproj[:, k, c * P:(c + 1) * P],
                                        patches[:, g, k], start=(k == 0), stop=(k == KP - 1))
                    ins.then_inc(emb_mm, 1)
            pe.wait_ge(txt_step, 11)
            for m in range(4):
                c, half = m // 2, m % 2
                pe.matmul(ps[:, 4 + m, 0:PSUM_W], tab[:, c * P:(c + 1) * P],
                          sepv[:, half * PSUM_W:(half + 1) * PSUM_W], start=True, stop=True).then_inc(txt_mm, 1)
            pe.wait_ge(ld_pe, 32)
            pe.wait_ge(txt_out, 4)
            for c in range(C):
                pe.matmul(ps[:, 4 + c, 0:HC * SP1], wp_bd, pe_bd[:, c], start=True, stop=True).then_inc(at_pbps, 1)

            def to_tokens(k):
                def step(u, par, n):
                    g = k * LN_STEPS + u
                    pe.wait_ge(ln_staged, g + 1)
                    wait(pe, ln_tok, g - 1)
                    for m in range(n):
                        for c in range(C):
                            ins = pe.transpose(tokps(par)[:, m * D + c * P:m * D + (c + 1) * P],
                                               stage[par][:, c * n * P + m * P:c * n * P + (m + 1) * P],
                                               ident[:, :])
                    ins.then_inc(ln_tokps, 1)
                if k != 2:
                    pairs_then_last(pe, step, step)
                else:
                    for u in range(DOWN_AFTER):
                        step(u, u % 2, 2)
                    down(GROUPS - 1)
                    for u in range(DOWN_AFTER, LN_STEPS):
                        step(u, u % 2, 2 if u < PAIRS else 1)

            def to_features(k):
                def step(u, par, n):
                    g = k * LN_STEPS + u
                    pe.wait_ge(ln_z, g + 1)
                    wait(pe, ln_out, g - 1)
                    for c in range(C):
                        for m in range(n):
                            lo = c * n * P + m * P
                            if k == 1:
                                ins = pe.transpose(zTps(par).bitcast(BF16)[:, lo:lo + P],
                                                   zb[par][:, m * D + c * P:m * D + (c + 1) * P], identb[:, :])
                            else:
                                ins = pe.transpose(zTps(par)[:, lo:lo + P],
                                                   z[par][:, m * D + c * P:m * D + (c + 1) * P], ident[:, :])
                    ins.then_inc(ln_zT, 1)
                    if k == 1:
                        pe.wait_ge(q_diag, u + 1)
                        pe.matmul(ps[:, 4 + par, 0:n * P], onesf[:, :], stage[par][:, 0:n * P],
                                  start=True, stop=True).then_inc(q_bps, 1)
                pairs_then_last(pe, step, step)

            pe.wait_ge(consts, 10)
            pe.wait_ge(emb_out, EG * C)
            to_tokens(0)
            to_features(0)

            def project_qk(b, q, turn):
                pe.wait_ge(at_y, b + 1)
                wait(pe, at_res, b - 4)
                for c in range(C):
                    pe.matmul(ps[:, 0, c * S:(c + 1) * S], wq_bd[:, :], yst[q][:, c], start=True, stop=True)
                for c in range(C):
                    ins = pe.matmul(ps[:, 0, (C + c) * S:(C + c + 1) * S], wk_bd[:, :], yst[q][:, c],
                                    start=True, stop=True)
                ins.then_inc(at_qkps, 1)

            def content(b, q, turn):
                pe.wait_ge(at_qkv, b + 1)
                wait(pe, at_s, b)
                for c in range(C):
                    ins = pe.matmul(ps[0:S, 4 + c, 0:HC * S], qu[q][:, c], kbd[q][:, c], start=True, stop=True)
                ins.then_inc(at_cps, 1)

            def project_v(b, q, turn):
                wait(pe, at_ctx, b)
                for c in range(C):
                    ins = pe.matmul(ps[0:S, 1, c * P:(c + 1) * P], yst[q][:, c], wv_bd[:, :],
                                    start=True, stop=True)
                ins.then_inc(at_vps, 1)

            def transpose_ctx(b, q, turn):
                pe.wait_ge(at_ctx, b + 1)
                pe.wait_ge(at_qkv, b + 5 if not isinstance(b, int) else min(b + 5, B))
                flat = ctxn.rearrange("p h d -> p (h d)")
                for c in range(C):
                    ins = pe.transpose(ps[:, 0, c * S:(c + 1) * S], flat[:, c * P:(c + 1) * P], ident[0:S, 0:S])
                ins.then_inc(at_ctxTps, 1)

            def transpose_p(b, q, turn):
                pe.wait_ge(at_p, b + 1)
                wait(pe, at_pT, b)
                for h in range(H):
                    ins = pe.transpose(ps[0:S, 6 + h // HC, h % HC * S:(h % HC + 1) * S], pr[q % 2][:, h],
                                       ident[0:S, 0:S])
                ins.then_inc(at_pTps, 1)

            def out_proj(b, q, turn):
                pe.wait_ge(at_ctxT, b + 1)
                for c in range(C):
                    for k in range(C):
                        ins = pe.matmul(ps[:, 0, (C + c) * S:(C + c + 1) * S],
                                        wo[:, k * D + c * P:k * D + (c + 1) * P], ctxT[:, k],
                                        start=(k == 0), stop=(k == C - 1))
                ins.then_inc(at_wops, 1)

            def position(b, q, turn):
                pe.wait_ge(at_qkv, b + 1)
                wait(pe, at_posp, b)
                for c in range(C):
                    ins = pe.matmul(ps[0:S, 2 + c, 0:HC * SP1], qv[:, c], pbd[:, c], start=True, stop=True)
                ins.then_inc(at_posps, 1)

            def context(b, q, turn):
                pe.wait_ge(at_pT, b + 1)
                pe.wait_ge(at_v, b + 1)
                for h in range(H):
                    ins = pe.matmul(ps[0:S, 1, h * (DH + 1):(h + 1) * (DH + 1)], prT[:, h], vaug[q % 2][:, h],
                                    start=True, stop=True)
                ins.then_inc(at_ctxps, 1)

            pe.wait_ge(ld_at, 160)
            pe.wait_ge(at_pbd, 2)
            pe.wait_ge(at_ones, 2)
            batches(pe, {"qk": project_qk, "content": content, "v": project_v, "ctxT": transpose_ctx,
                         "pT": transpose_p, "out": out_proj, "pos": position, "context": context},
                    [("content", 3), ("pT", 4), ("v", 4), ("ctxT", LAG), ("pos", 1), ("out", LAG),
                     ("context", 4), ("qk", 0)])

            to_tokens(1)
            to_features(1)

            w1v = w1i.rearrange("p (c f) -> p c f", c=C)
            w2v = w2i.rearrange("p (j d) -> p j d", j=FJ)

            def up(g, j):
                wait(pe, ff_u, g * FJ + j - 3)
                for c in range(C):
                    ins = pe.matmul(ps[:, UP_BANKS[j % 4], 0:GN], w1v[:, c, j * P:(j + 1) * P],
                                    ziT[:, c, bass.ds(g * GN, GN)], start=(c == 0), stop=(c == C - 1))
                ins.then_inc(ff_mm, 1)

            def convolve(g, j):
                n = PE_CHUNKS.index(j)
                pe.wait_ge(ff_u, g * FJ + j + 1)
                last = [c for c, b in zip(PE_CHUNKS, PE_BANKS) if b == PE_BANKS[n]]
                m = last.index(j)
                bg, bj = (g, last[m - 1]) if m > 0 else (g - 1, last[-1])
                wait(pe, ff_s, bg * FJ + bj + 1)
                for k in range(3):
                    ins = pe.matmul(ps[:, PE_BANKS[n], 0:GN], diag[:, n, k], uu[j % 4][:, :, k:k + S],
                                    start=(k == 0), stop=(k == 2))
                ins.then_inc(ff_cv, 1)

            def down(g):
                pe.wait_ge(ff_si, g + 1)
                wait(pe, ff_fo, g)
                for c in range(C):
                    for j in range(FJ):
                        ins = pe.matmul(ps[:, 4 + c, 0:GN], w2v[:, j, c * P:(c + 1) * P], si[:, j],
                                        start=(j == 0), stop=(j == FJ - 1))
                ins.then_inc(ff_ops, 1)

            def ff_group(g):
                for j in range(AHEAD):
                    up(g, j)
                for j in range(FJ):
                    if j + AHEAD < FJ:
                        up(g, j + AHEAD)
                    if j in PE_CHUNKS:
                        convolve(g, j)
                    if j == DOWN_AT and (not isinstance(g, int) or g > 1):
                        down(g - 2)

            pe.wait_ge(ln_out, 2 * LN_STEPS)
            pe.wait_ge(wq_done, 2)
            pe.wait_ge(ff_diag, 1)
            for g in range(3):
                ff_group(g)
            with pe.Fori(3, GROUPS) as g:
                ff_group(g)
            down(GROUPS - 2)

            to_tokens(2)
            to_features(2)

            def q_of7(g, par):
                pe.wait_ge(a1_y, g + 1)
                wait(pe, a1_q, g)
                for c in range(C):
                    ins = pe.matmul(ps[0:HS, 0, 0:GN], wqkv_v[:, c, 0:HS], y7[par][:, c],
                                    start=(c == 0), stop=(c == C - 1))
                ins.then_inc(a1_qps, 1)

            def kv_of7(g, par):
                wait(pe, a1_k, g)
                for c in range(C):
                    ins = pe.matmul(ps[0:HS, 1, 0:GN], wqkv_v[:, c, HS:2 * HS], y7[par][:, c],
                                    start=(c == 0), stop=(c == C - 1))
                ins.then_inc(a1_kps, 1)
                wait(pe, a1_v, g)
                for b in range(GB):
                    for c in range(C):
                        ins = pe.matmul(ps[0:S, 2, b * HS:(b + 1) * HS], y7[par][:, c, b * S:(b + 1) * S],
                                        wqkv_v[:, c, 2 * HS:3 * HS], start=(c == 0), stop=(c == C - 1))
                ins.then_inc(a1_vps, 1)

            def weights7(g, par):
                pe.wait_ge(a1_q, g + 1)
                pe.wait_ge(a1_k, g + 1)
                wait(pe, a1_w, g)
                for b in range(GB):
                    ins = pe.matmul(ps[0:S, 3, b * S:(b + 1) * S], k7[par][:, b * S:(b + 1) * S],
                                    q7[par][:, b * S:(b + 1) * S], start=True, stop=True)
                ins.then_inc(a1_wps, 1)

            def attend7(g, par):
                pe.wait_ge(a1_w, g + 1)
                pe.wait_ge(a1_v, g + 1)
                wait(pe, a1_o, g)
                for b in range(GB):
                    ins = pe.matmul(ps[0:HS, 4, b * S:(b + 1) * S], v7[par][:, b], w7[par][:, b],
                                    start=True, stop=True)
                ins.then_inc(a1_ops, 1)

            def project7(g, par):
                pe.wait_ge(a1_o, g + 1)
                wait(pe, a1_res, g)
                for c in range(C):
                    ins = pe.matmul(ps[:, 5 + c, 0:GN], pj[:, c * P:(c + 1) * P], o7[par], start=True, stop=True)
                ins.then_inc(a1_pps, 1)

            def step7(g, par, first=False, last=False):
                if not first:
                    weights7(g - 1, 1 - par)
                if not last:
                    q_of7(g, par)
                if not first:
                    attend7(g - 1, 1 - par)
                if not last:
                    kv_of7(g, par)
                if not first:
                    project7(g - 1, 1 - par)

            pe.wait_ge(ld_a1, 80)
            pe.wait_ge(pj_done, 1)
            step7(0, 0, first=True)
            step7(1, 1)
            with pe.Fori(1, GROUPS // 2) as i:
                for par in range(2):
                    step7(2 * i + par, par)
            step7(GROUPS, 0, last=True)

            to_tokens(3)

            def z_transposed(u, par, n):
                g = 3 * LN_STEPS + u
                pe.wait_ge(ln_z, g + 1)
                wait(pe, ln_out, g - 1)
                for c in range(C):
                    for m in range(n):
                        lo = c * n * P + m * P
                        ins = pe.transpose(zTps(par)[:, lo:lo + P], z[par][:, m * D + c * P:m * D + (c + 1) * P],
                                           ident[:, :])
                ins.then_inc(ln_zT, 1)

            def router(u, par, n):
                pe.wait_ge(ln_out, 3 * LN_STEPS + u + 1)
                for m in range(n):
                    for c in range(C):
                        ins = pe.matmul(ps[:, 4, bass.ds((2 * u + m) * E, E)], zTs[par][:, c, m * P:(m + 1) * P],
                                        wr[:, c * E:(c + 1) * E], start=(c == 0), stop=(c == C - 1))
                ins.then_inc(rt_lgps, 1)

            pe.wait_ge(ld_rt, 48)
            z_transposed(0, 0, 2)
            z_transposed(1, 1, 2)
            router(0, 0, 2)
            with pe.Fori(1, PAIRS // 2) as i:
                for par in range(2):
                    z_transposed(2 * i + par, par, 2)
                    router(2 * i + par - 1, 1 - par, 2)
            z_transposed(PAIRS, 0, 1)
            router(PAIRS - 1, 1, 2)
            router(PAIRS, 0, 1)

            pe.wait_ge(rt_cb, 1)
            pe.matmul(ps[:, 5, 0:E], onesb, cntb, start=True, stop=True).then_inc(rt_cntps, 1)
            flat = ohb.rearrange("p t e -> p (t e)")
            pe.matmul(ps[:, 6, 0:TILES * E], triu, flat, start=True, stop=False)
            for t in range(TILES - 1):
                m = TILES - 1 - t
                ins = pe.matmul(ps[:, 6, (t + 1) * E:TILES * E].rearrange("p (t e) -> p t e", e=E), onesb,
                                ohb[:, t:t + 1, :].to_broadcast([P, m, E]), start=False, stop=(m == 1))
            ins.then_inc(rt_pps, 1)

            def rows_T(i, ii, par):
                pe.wait_ge(mo_xin[par], 16 * ii + 16)
                wait(pe, mo_xT, i - 1)
                for c in range(C):
                    ins = pe.transpose(ps[:, 6 + par, c * P:(c + 1) * P], xt[par][:, c * P:(c + 1) * P],
                                       ident[:, :])
                ins.then_inc(mo_xTps, 1)

            def up_e(i, par):
                e = pe.value_load(tei[0:1, bass.ds(i, 1)], min_val=0, max_val=E - 1)
                pe.wait_ge(mo_xT, i + 1)
                wait(pe, mo_h1a, i)
                wait(pe, mo_h1b, i)
                for half in range(2):
                    for c in range(C):
                        ins = pe.matmul(ps[:, half, :], xT[par][:, c * P:(c + 1) * P],
                                        moe_w[:, bass.ds(e * WE + c * FF + half * PSUM_W, PSUM_W)],
                                        start=(c == 0), stop=(c == C - 1))
                ins.then_inc(mo_h1ps, 1)

            def hidden_T(i, par):
                pe.wait_ge(mo_h1a, i + 1)
                pe.wait_ge(mo_h1b, i + 1)
                wait(pe, mo_hTa, i)
                wait(pe, mo_hTb, i)
                for j in range(FJ):
                    ins = pe.transpose(ps[:, 2 + j // 4, j % 4 * P:(j % 4 + 1) * P], h1[:, j * P:(j + 1) * P],
                                       ident[:, :])
                ins.then_inc(mo_hTps, 1)

            def down_e(i, par):
                e = pe.value_load(tei[0:1, bass.ds(i, 1)], min_val=0, max_val=E - 1)
                pe.wait_ge(mo_hTa, i + 1)
                pe.wait_ge(mo_hTb, i + 1)
                wait(pe, mo_y, i - 1)
                for j in range(FJ):
                    ins = pe.matmul(ps[:, 4 + par, 0:D], hTm[:, j],
                                    moe_w[:, bass.ds(e * WE + C * FF + j * D, D)],
                                    start=(j == 0), stop=(j == FJ - 1))
                ins.then_inc(mo_yps, 1)

            pe.wait_ge(rt_te, 1)
            pe.wait_ge(ld_moe, 16 * W_EARLY)
            pe.wait_ge(ld_moe5, 16)
            pe.wait_ge(ld_moe467, 48)
            rows_T(0, 0, 0)
            up_e(0, 0)
            rows_T(1, 0, 1)
            hidden_T(0, 0)
            up_e(1, 1)
            down_e(0, 0)
            rows_T(2, 1, 0)
            hidden_T(1, 1)

            def two_tiles(i):
                for par in range(2):
                    s = 2 * i + par
                    up_e(s, par)
                    down_e(s - 1, 1 - par)
                    rows_T(s + 1, i + par, 1 - par)
                    hidden_T(s, par)

            two_tiles(1)
            with pe.Fori(2, MAX_TILES // 2 - 1) as i:
                two_tiles(i)
            s = MAX_TILES - 2
            up_e(s, 0)
            down_e(s - 1, 1)
            rows_T(s + 1, MAX_TILES // 2 - 1, 1)
            hidden_T(s, 0)
            up_e(s + 1, 1)
            down_e(s, 0)
            hidden_T(s + 1, 1)
            down_e(s + 1, 1)


def lay_out(i):
    def cols(v):
        return v.reshape(-1, P).T

    def feat(w):
        return w.T.reshape(-1, P, w.shape[0]).transpose(1, 0, 2)

    def heads(w):
        m = np.zeros((P, P), w.dtype)
        for h in range(HC):
            m[h * DH:(h + 1) * DH, h * DH:(h + 1) * DH] = w
        return m

    def every(v):
        return np.broadcast_to(v.reshape(1, -1), (P, v.size))

    pos = np.arange(S, dtype=np.float32)[:, None]
    div = np.exp(np.arange(0, D, 2, dtype=np.float32) * np.float32(-np.log(10000.0) / D))
    pe = np.zeros((S, D), np.float32)
    pe[:, 0::2] = np.sin(pos * div)
    pe[:, 1::2] = np.cos(pos * div)
    pe_bd = np.zeros((P, C, HC, SP1), np.float32)
    for c in range(C):
        for h in range(HC):
            lo = (c * HC + h) * DH
            pe_bd[h * DH:(h + 1) * DH, c, h, 1:] = pe[:, lo:lo + DH].T

    hp = 6
    patches = (i["x"].reshape(B, hp, 16, hp, 16, 3).transpose(0, 1, 3, 2, 4, 5)
               .reshape(EG, EGN, KP, P).transpose(3, 0, 2, 1))
    w1e = i["L1_ffn_W1"].transpose(2, 0, 1).reshape(C, P, E, FF).transpose(1, 2, 0, 3).reshape(P, E, C * FF)
    w2e = i["L1_ffn_W2"].transpose(2, 0, 1).reshape(FJ, P, E, D).transpose(1, 2, 0, 3).reshape(P, E, FJ * D)
    qkv_b = i["L1_attn_qkv_b"]
    return {
        "patches": patches,
        "w_proj": feat(i["L0_tok_W_proj"]),
        "pos": feat(i["L0_tok_pos_emb"]),
        "b_proj": cols(i["L0_tok_b_proj"]),
        "x_txt": np.broadcast_to(i["x_txt"].reshape(1, -1), (TAB, NTXT)),
        "table": i["L0_txt_weights"][:TAB],
        "gamma": cols(i["L0_attn_ln_gamma"]),
        "beta": cols(i["L0_attn_ln_beta"]),
        "wq": heads(i["L0_attn_Wq"]), "wk": heads(i["L0_attn_Wk"]),
        "wv": heads(i["L0_attn_Wv"]), "wp": heads(i["L0_attn_Wp"]),
        "bq": np.tile(i["L0_attn_bq"], HC).reshape(P, 1),
        "bk": np.tile(i["L0_attn_bk"], HC).reshape(P, 1),
        "bv": np.tile(i["L0_attn_bv"], HC).reshape(P, 1),
        "u_bias": cols(i["L0_attn_u_bias"]), "v_bias": cols(i["L0_attn_v_bias"]),
        "wo": i["L0_attn_Wo"].reshape(C, P, D).transpose(1, 0, 2).reshape(P, C * D),
        "bo": cols(i["L0_attn_bo"]),
        "pe_bd": pe_bd.reshape(P, C, HC * SP1),
        "w1": feat(i["L0_ffn_w1"]).reshape(P, C * FF),
        "w2": feat(i["L0_ffn_w2"]).reshape(P, FJ * D),
        "conv_w": i["L0_ffn_conv_w"].reshape(FJ, P, 3).transpose(1, 0, 2).reshape(P, FJ * 3),
        "conv_b": cols(i["L0_ffn_conv_b"]),
        "wqkv": feat(i["L1_attn_qkv_w"]).reshape(P, C * 3 * HS),
        "bq1": qkv_b[:HS].reshape(HS, 1), "bk1": qkv_b[HS:2 * HS].reshape(HS, 1),
        "bv1": np.broadcast_to(qkv_b[2 * HS:].reshape(1, HS), (S, HS)),
        "pj": i["L1_attn_proj_w"].reshape(D, NREP, HS).transpose(2, 0, 1),
        "pjb": cols(i["L1_attn_proj_b"]),
        "wr": feat(i["L1_ffn_Wr"]).reshape(P, C * E),
        "br": every(i["L1_ffn_br"]),
        "moe_w": np.concatenate([w1e, w2e], axis=2),
        "b1": i["L1_ffn_b1"].reshape(E, FJ, P).transpose(2, 0, 1).reshape(P, E * FJ),
        "b2": every(i["L1_ffn_b2"]),
    }


def kernel(**inputs):
    import numpy as _np
    import concourse.bacc as _bacc
    from concourse.bass_utils import run_bass_kernel_spmd as _run

    nc = _bacc.Bacc("TRN2", target_bir_lowering=False, num_devices=1)
    arrays, args = {}, {}
    for name, v in lay_out({k: _np.asarray(v) for k, v in inputs.items()}).items():
        v = _np.ascontiguousarray(v)
        arrays[f"in_{name}"] = v
        args[name] = nc.dram_tensor(f"in_{name}", v.shape, mybir.dt.from_np(v.dtype), kind="ExternalInput").ap()
    out = nc.dram_tensor("out_rows", (NTOK, D), F32, kind="ExternalOutput").ap()
    program(nc, args, out)
    r = _run(nc, [arrays], core_ids=[0])
    return r.results[0]["out_rows"].reshape(B, S, D)
```
